# Optimizing a Trainium2 kernel written in Bass

```python
import numpy as np
import jax
import jax.numpy as jnp

def _softmax(x, axis=-1):
    return jax.nn.softmax(x, axis=axis)

def _gelu(x):
    return jax.nn.gelu(x, approximate=True)

def _silu(x):
    return jax.nn.silu(x)

def _sigmoid(x):
    return jax.nn.sigmoid(x)

def _layernorm(x, axis=-1, eps=1e-05):
    m = jnp.mean(x, axis=axis, keepdims=True)
    v = jnp.var(x, axis=axis, keepdims=True)
    return (x - m) / jnp.sqrt(v + eps)

def _scatter_add(tgt, idx, src, axis=0):
    return tgt.at[idx].add(src)

def _segment_sum(src, seg, n):
    return jax.ops.segment_sum(src, seg, n)
kernel_name = 'mk_seq_postln_d1_jaxref_r8_2d77d4'

def setup_inputs(seed: int=0):
    np.random.seed(seed)
    _w = jnp.asarray

    def _L0_attn_setup():
        import jax, jax.numpy as jnp
        import numpy as np
        import math
        DIM = 128
        NUM_HEADS = 16
        HEAD_DIM = DIM // NUM_HEADS
        B, S = (2, 256)
        key = jax.random.key(seed)
        ks = jax.random.split(key, 9)
        sc = 0.02
        return {'x': jax.random.normal(ks[0], (B, S, DIM), jnp.float32), 'Wq': jax.random.normal(ks[1], (DIM, DIM), jnp.float32) * sc, 'bq': jax.random.normal(ks[2], (DIM,), jnp.float32) * sc, 'Wk': jax.random.normal(ks[3], (DIM, DIM), jnp.float32) * sc, 'bk': jax.random.normal(ks[4], (DIM,), jnp.float32) * sc, 'Wv': jax.random.normal(ks[5], (DIM, DIM), jnp.float32) * sc, 'bv': jax.random.normal(ks[6], (DIM,), jnp.float32) * sc, 'Wo': jax.random.normal(ks[7], (DIM, DIM), jnp.float32) * sc, 'bo': jax.random.normal(ks[8], (DIM,), jnp.float32) * sc}
    _L0_attn_in = _L0_attn_setup()

    def _L0_ffn_setup():
        import jax, jax.numpy as jnp
        import numpy as np
        HIDDEN = 128
        FFN = 512
        NUM_EXPERTS = 8
        TOP_K = 2
        BATCH, SEQ = (2, 256)
        key = jax.random.key(seed)
        ks = jax.random.split(key, 6)
        s_h = 1.0 / np.sqrt(HIDDEN)
        s_f = 1.0 / np.sqrt(FFN)
        return {'hidden_states': jax.random.normal(ks[0], (BATCH, SEQ, HIDDEN), jnp.float32), 'gate_w': jax.random.uniform(ks[1], (HIDDEN, NUM_EXPERTS), jnp.float32, -s_h, s_h), 'gate_b': jax.random.uniform(ks[2], (NUM_EXPERTS,), jnp.float32, -s_h, s_h), 'w1': jax.random.uniform(ks[3], (NUM_EXPERTS, HIDDEN, FFN), jnp.float32, -s_h, s_h), 'w3': jax.random.uniform(ks[4], (NUM_EXPERTS, HIDDEN, FFN), jnp.float32, -s_h, s_h), 'w2': jax.random.uniform(ks[5], (NUM_EXPERTS, FFN, HIDDEN), jnp.float32, -s_f, s_f)}
    _L0_ffn_in = _L0_ffn_setup()
    _d = {'L0_attn_x': _L0_attn_in['x'], 'L0_attn_Wq': _L0_attn_in['Wq'], 'L0_attn_bq': _L0_attn_in['bq'], 'L0_attn_Wk': _L0_attn_in['Wk'], 'L0_attn_bk': _L0_attn_in['bk'], 'L0_attn_Wv': _L0_attn_in['Wv'], 'L0_attn_bv': _L0_attn_in['bv'], 'L0_attn_Wo': _L0_attn_in['Wo'], 'L0_attn_bo': _L0_attn_in['bo'], 'L0_ffn_gate_w': _L0_ffn_in['gate_w'], 'L0_ffn_gate_b': _L0_ffn_in['gate_b'], 'L0_ffn_w1': _L0_ffn_in['w1'], 'L0_ffn_w3': _L0_ffn_in['w3'], 'L0_ffn_w2': _L0_ffn_in['w2']}
    _x0 = _d['L0_attn_x']
    _d['L0_attn_x'] = jax.random.normal(jax.random.fold_in(jax.random.key(seed), 1), (16, 512, 128), dtype=_x0.dtype)
    del _x0
    return _d

def reference(L0_attn_x, L0_attn_Wq, L0_attn_bq, L0_attn_Wk, L0_attn_bk, L0_attn_Wv, L0_attn_bv, L0_attn_Wo, L0_attn_bo, L0_ffn_gate_w, L0_ffn_gate_b, L0_ffn_w1, L0_ffn_w3, L0_ffn_w2):

    def _L0_attn_ref(x, Wq, bq, Wk, bk, Wv, bv, Wo, bo):
        import jax, jax.numpy as jnp
        import numpy as np
        import math
        DIM = 128
        NUM_HEADS = 16
        HEAD_DIM = DIM // NUM_HEADS
        B, S = (2, 256)
        b, s, d = x.shape
        h, hd = (NUM_HEADS, HEAD_DIM)

        def split_heads(t):
            return t.reshape(b, s, h, hd).transpose(0, 2, 1, 3)
        q = split_heads(x @ Wq + bq)
        k = split_heads(x @ Wk + bk)
        v = split_heads(x @ Wv + bv)
        scores = jnp.einsum('bhqd,bhkd->bhqk', q, k) / math.sqrt(hd)
        causal = jnp.tril(jnp.ones((s, s), dtype=bool))
        scores = jnp.where(causal[None, None], scores, jnp.asarray(-10000.0, scores.dtype))
        probs = jax.nn.softmax(scores, axis=-1)
        ctx = jnp.einsum('bhqk,bhkd->bhqd', probs, v)
        ctx = ctx.transpose(0, 2, 1, 3).reshape(b, s, d)
        return ctx @ Wo + bo

    def _L0_ffn_ref(hidden_states, gate_w, gate_b, w1, w3, w2):
        import jax, jax.numpy as jnp
        import numpy as np
        HIDDEN = 128
        FFN = 512
        NUM_EXPERTS = 8
        TOP_K = 2
        BATCH, SEQ = (2, 256)
        B, S, D = hidden_states.shape
        T = B * S
        x = hidden_states.reshape(T, D)
        logits = x @ gate_w + gate_b
        probs = jax.nn.softmax(logits.astype(jnp.float32), axis=-1)
        top_w, top_idx = jax.lax.top_k(probs, TOP_K)
        top_w = top_w / jnp.sum(top_w, axis=-1, keepdims=True)
        combine = jnp.zeros((T, NUM_EXPERTS), jnp.float32)
        combine = combine.at[jnp.arange(T)[:, None], top_idx].set(top_w)
        combine = combine.astype(x.dtype)
        h = jax.nn.silu(jnp.einsum('td,edf->tef', x, w1)) * jnp.einsum('td,edf->tef', x, w3)
        out_e = jnp.einsum('tef,efd->ted', h, w2)
        out = jnp.einsum('ted,te->td', out_e, combine)
        return out.reshape(B, S, D)
    x = L0_attn_x
    x = _layernorm(x + _L0_attn_ref(x, L0_attn_Wq, L0_attn_bq, L0_attn_Wk, L0_attn_bk, L0_attn_Wv, L0_attn_bv, L0_attn_Wo, L0_attn_bo), axis=-1)
    x = _layernorm(x + _L0_ffn_ref(x, L0_ffn_gate_w, L0_ffn_gate_b, L0_ffn_w1, L0_ffn_w3, L0_ffn_w2), axis=-1)
    return x

_drawn_inputs = setup_inputs


def setup_inputs(seed=0):
    import zlib

    import numpy as np

    out = dict(_drawn_inputs(seed))
    spreads = {}
    factors = {'L0_attn_Wq': 8.0,
     'L0_attn_bq': 8.0,
     'L0_attn_Wk': 8.0,
     'L0_attn_bk': 64.0,
     'L0_attn_Wv': 7.865,
     'L0_attn_bv': 8.0,
     'L0_attn_Wo': 6.326,
     'L0_ffn_gate_b': 3.279,
     'L0_attn_bo': 4.217}
    for name, (base, spread) in spreads.items():
        noise = np.random.default_rng([zlib.crc32(name.encode()), seed]).standard_normal(out[name].shape)
        drawn = base * np.exp(spread * noise) if base else spread * noise
        out[name] = jnp.asarray(drawn.astype(out[name].dtype))
    for name, factor in factors.items():
        out[name] = (out[name] * factor).astype(out[name].dtype)
    return out
```

```python
from contextlib import ExitStack

import concourse.bass as bass
from concourse import mybir

F32 = mybir.dt.float32
BF16 = mybir.dt.bfloat16
I32 = mybir.dt.int32
ALU = mybir.AluOpType
ACT = mybir.ActivationFunctionType
AX = mybir.AxisListType

P = 128
D = 128
H = 16
HD = D // H
S = 512
NT = S // P
EPS = 1e-5
SCALE = float(HD) ** -0.5
MASKED = -1.0e30
PARTS = 3
SPLIT_ROWS = PARTS * PARTS * HD
STACK = SPLIT_ROWS + PARTS
PAIR = 2
LAG = 12
HALF = H // 2
GROUP = 4
NG = H // GROUP
DIAG, LONG, SHORT = S, S, S // 2
HEAD_P = DIAG + LONG + SHORT
E = 8
TOP_K = 2
FF = 512
FC = FF // P
CG = 4
SUM_COL = HD

MISC = [
    (0, "q", 1), (1, "max1", -1), (2, "ctx0", -2), (3, "ctx1", -2), (4, "k", 1), (5, "ctx2", -2),
    (6, "ctx3", -2), (7, "turn", -2), (8, "out", -2), (9, "max0", 0), (11, "xturn", -2),
    (12, "v", 0), (13, "gate", -2),
]


class Turn:

    def __init__(self, j, c, B, steady=False):
        self.j, self.c, self.B, self.steady = j, c, B, steady

    def has(self, k):
        return self.steady or 0 <= self.c + k < self.B

    def batch(self, k):
        return self.j * 2 + (self.c + k)

    def parity(self, k):
        return (self.c + k) % 2

    def half(self, k):
        return self.j + (self.c + k) // 2

    def before(self):
        return Turn(self.j, self.c - 1, self.B, self.steady)

    def misc_count(self, name):
        n = 0
        for i in range(-1, self.c + 1):
            for _, other, k in MISC:
                if 0 <= i + k < self.B:
                    n += 1
                if i == self.c and other == name:
                    return self.j * (2 * len(MISC)) + n


def turns(eng, B, body):
    first = 3
    pairs = (B - 1 - first) // 2
    for c in range(-1, first):
        body(Turn(0, c, B))
    with eng.Fori(0, pairs) as j:
        for c in (first, first + 1):
            body(Turn(j, c, B, steady=True))
    for c in range(first + 2 * pairs, B + 2):
        body(Turn(0, c, B))


def attention(nc, ctx, a, x1, logits, arena, B):

    def sb(name, shape, dt=F32):
        return ctx.enter_context(nc.sbuf_tensor(name, shape, dt))

    def sem(name):
        return ctx.enter_context(nc.semaphore(name))

    stack_cols = H * S
    def stack(parity, which):
        n = stack_cols // 2
        at = (2 * parity + which) * n
        return arena[:, at:at + n].bitcast(BF16).rearrange("p (h t) -> p h t", h=H)
    q_stack = [stack(p, 0) for p in range(2)]
    k_stack = [stack(p, 1) for p in range(2)]

    wq, wk, wv, wo = (sb(n, [P, D]) for n in ("wq", "wk", "wv", "wo"))
    qk_bias = sb("qk_bias", [P, 2])
    v_bias = sb("v_bias", [P, D])
    o_bias = sb("o_bias", [P, D])
    gate_w = sb("gate_w", [P, 8])
    gate_bias = sb("gate_bias", [P, NT, 8])
    ident = sb("ident", [P, P])
    ident16 = sb("ident16", [P, P], BF16)
    above = sb("above", [P, NT, P], BF16)
    x_t = [sb(f"x_t{p}", [P, S]) for p in range(2)]
    qk = sb("qk", [P, 2, S])
    rest = sb("rest", [P, 2, S])
    part = [sb(f"part{n}", [P, 2, S], BF16) for n in range(PARTS)]
    v_aug = [sb(f"v_aug{p}", [P, NT, H, 32]) for p in range(2)]
    row_max = sb("row_max", [P, 2, NT, HALF])
    off_max = sb("off_max", [P, 2, NT - 1, HALF])
    max_rest = sb("max_rest", [P, NT, HALF])
    max_part = sb("max_part", [P, 2, NT, PARTS, HALF], BF16)
    max_rows = [sb(f"max_rows{h}", [PARTS * HALF, S], BF16) for h in range(2)]
    probs = [sb(f"probs{p}", [P, GROUP * HEAD_P]) for p in range(2)]

    def probs_of(g, first, count):
        strip = lambda at, width: probs[g % 2][:, GROUP * at + first * width:GROUP * at + (first + count) * width]
        return strip(0, DIAG), strip(DIAG, LONG), strip(DIAG + LONG, SHORT)

    ctx_t = [sb(f"ctx_t{p}", [P, NG, S]) for p in range(2)]
    inv_sum = sb("inv_sum", [P, H])
    ctx_n = sb("ctx_n", [P, NT, D])
    ctx_back = sb("ctx_back", [P, S])
    res = sb("res", [P, NT, D])
    stats = sb("stats", [P, NT, 6])
    mean_var = sb("mean_var", [P, NT, 2])
    var_eps = sb("var_eps", [P, NT])
    eps_col = sb("eps_col", [P, NT])
    minus_half = sb("minus_half", [P, NT])
    rstd = sb("rstd", [P, NT])
    x1_now = sb("x1_now", [P, NT, D])
    x1_t = sb("x1_t", [P, S])

    def bank(name):
        return ctx.enter_context(nc.psum_tensor(name, [P, S], F32))
    s_bank = [bank(f"s_bank{n}") for n in range(3)]
    t_bank = [bank(f"t_bank{n}") for n in range(3)]
    c_bank = bank("c_bank")
    m_bank = bank("m_bank")

    consts_loaded = sem("consts_loaded")
    made = sem("made")
    ones_made = sem("ones_made")
    x_t_loaded = [sem(f"x_t_loaded{p}") for p in range(2)]
    x_rows_loaded = sem("x_rows_loaded")
    stacked = [[sem(f"stacked{p}{h}") for h in range(2)] for p in range(2)]
    max_stacked = [sem(f"max_stacked{h}") for h in range(2)]
    s_ready = [sem(f"s_ready{n}") for n in range(3)]
    s_taken = [sem(f"s_taken{n}") for n in range(3)]
    t_ready = [sem(f"t_ready{n}") for n in range(3)]
    t_taken = [sem(f"t_taken{n}") for n in range(3)]
    c_ready = sem("c_ready")
    c_taken = sem("c_taken")
    m_ready = sem("m_ready")
    m_taken = sem("m_taken")
    masked = sem("masked")
    parts_written = [sem(f"parts_written{p}") for p in range(2)]
    part1_made = sem("part1_made")
    rest_made = sem("rest_made")
    part2_made = sem("part2_made")
    part3_made = sem("part3_made")
    max_split = sem("max_split")
    max_step = sem("max_step")
    max_reduced = sem("max_reduced")
    max_copied = sem("max_copied")
    x_plus_made = sem("x_plus_made")
    sums_inverted = sem("sums_inverted")
    x1_kept = sem("x1_kept")
    stats_made = sem("stats_made")
    mean_made = sem("mean_made")
    rstd_made = sem("rstd_made")
    var_eps_made = sem("var_eps_made")
    normed = sem("normed")

    CONSTS = ((wq, a["wq"]), (wk, a["wk"]), (wv, a["wv"]), (wo, a["wo"]), (qk_bias, a["qk_bias"]),
              (v_bias, a["v_bias"]), (o_bias, a["o_bias"]), (gate_w, a["gate_w"]), (gate_bias, a["gate_bias"]))
    scratch = nc.dram_tensor("parts", [2, 2, PARTS, HD, H, S], BF16, kind="Internal").ap()
    STACK_COPIES = [(q_stack, 0, PARTS * c, 0, PARTS) for c in range(PARTS)]
    for c in range(PARTS):
        STACK_COPIES.append((k_stack, 1, PARTS * c, c, PARTS - c))
        if c:
            STACK_COPIES.append((k_stack, 1, PARTS * (c + 1) - c, 0, c))
    M16 = m_bank[:, 0:S // 2].bitcast(BF16)

    def wait_stacks(eng, t, k, half):
        eng.wait_ge(stacked[t.parity(k)][half], 16 * len(STACK_COPIES) * (t.half(k) + 1))

    with nc.Block() as block:

        @block.sync
        def _(sp):
            for n, (tile, src) in enumerate(CONSTS):
                sp.dma_start(tile[:], src).then_inc(consts_loaded, 16)
            sp.wait_ge(ones_made, 4)

            def body(t):
                if t.has(1):
                    if t.has(-1):
                        sp.wait_ge(m_ready, t.before().misc_count("v"))
                    sp.dma_start(x_t[t.parity(1)][:], a["x_t"][t.batch(1)]).then_inc(x_t_loaded[t.parity(1)], 16)
                if t.has(1):
                    par = t.parity(1)
                    if t.has(-1):
                        for half in range(2):
                            wait_stacks(sp, t, -1, half)
                            sp.nop(nofuse=True)
                    for n, part_made in enumerate((part1_made, part2_made, part3_made)):
                        sp.wait_ge(part_made, t.batch(1) + 1)
                        for which in range(2):
                            sp.dma_start(scratch[par, which, n].rearrange("d h t -> h d t"),
                                         part[n][:, which, :]).then_inc(parts_written[par], 16)
                    sp.wait_ge(parts_written[par], 16 * 2 * PARTS * (t.half(1) + 1))
                    for half in range(2):
                        if t.has(-1):
                            sp.wait_ge(t_ready[2], (H // PAIR) * t.batch(-1) + (half + 1) * (HALF // PAIR))
                        for stacks, which, row, first, parts in STACK_COPIES:
                            heads = slice(half * HALF, (half + 1) * HALF)
                            sp.dma_start(
                                stacks[par][HD * row:HD * (row + parts), heads, :],
                                scratch[par, which, first:first + parts, :, heads, :].rearrange("n d h t -> (n d) h t"),
                            ).then_inc(stacked[par][half], 16)
                if t.has(-2):
                    sp.wait_ge(normed, NT * (t.batch(-2) + 1))
                    sp.dma_start(x1[:, bass.ds(NT * t.batch(-2), NT), :], x1_now[:]).then_inc(x1_kept, 16)
                if t.has(-1):
                    sp.dma_start(res[:], a["x_rows"][t.batch(-1)]).then_inc(x_rows_loaded, 16)

            turns(sp, B, body)
            sp.wait_ge(x1_kept, 16 * B)

        @block.gpsimd
        def _(pool):
            pool.memset(ident[:], 0.0).then_inc(made, 1)
            pool.memset(ident16[:], 0.0).then_inc(made, 1)
            pool.memset(above[:], 0.0).then_inc(made, 1)
            pool.memset(eps_col[:], EPS).then_inc(made, 1)
            pool.memset(minus_half[:], -0.5).then_inc(made, 1)
            pool.wait_ge(made, 5)
            for tile in (ident, ident16):
                pool.affine_select(out=tile[:], in_=tile[:], compare_op=ALU.not_equal, fill=1.0, base=0,
                                   pattern=[[-1, P]], channel_multiplier=1).then_inc(made, 1)
            pool.affine_select(out=above[:], in_=above[:], compare_op=ALU.is_ge, fill=MASKED, base=0,
                               pattern=[[0, NT], [-1, P]], channel_multiplier=1).then_inc(made, 1)

            def mask(t, k, h):
                pool.wait_ge(t_taken[0], H * t.batch(k) + h + 1)
                diagonal, _, _ = probs_of(h // GROUP, h % GROUP - 1, PAIR)
                blocks = diagonal.rearrange("p (b c) -> p b c", c=P)
                pool.nop(nofuse=True)
                pool.affine_select(out=blocks, in_=blocks, compare_op=ALU.is_ge, fill=0.0, base=0,
                                   pattern=[[0, PAIR * NT], [1, P]], channel_multiplier=-1).then_inc(masked, 1)

            def body(t):
                for s in range(H):
                    h, k = ((s - LAG) % H, 0 if s >= LAG else -1)
                    if s == 1 and t.has(-2):
                        pool.wait_ge(x_rows_loaded, 16 * (t.batch(-2) + 1))
                        pool.tensor_tensor(res[:], res[:], o_bias[:].rearrange("p (o d) -> p o d", o=1).to_broadcast([P, NT, D]),
                                           ALU.add).then_inc(x_plus_made, 1)
                    if s == 6 and t.has(1):
                        pool.wait_ge(part1_made, t.batch(1) + 1)
                        pool.tensor_tensor(rest[:], qk[:], part[0][:], ALU.subtract).then_inc(rest_made, 1)
                    if s == 8 and t.has(1):
                        pool.wait_ge(part2_made, t.batch(1) + 1)
                        pool.tensor_tensor(part[2][:], rest[:], part[1][:], ALU.subtract).then_inc(part3_made, 1)
                    if s == 9 and t.has(-2):
                        pool.wait_ge(mean_made, NT * (t.batch(-2) + 1))
                        if t.has(-3):
                            pool.wait_ge(normed, NT * (t.batch(-3) + 1))
                        pool.tensor_tensor(var_eps[:], mean_var[:, :, 1], eps_col[:], ALU.add).then_inc(var_eps_made, 1)
                        pool.wait_ge(var_eps_made, t.batch(-2) + 1)
                        pool.tensor_tensor(rstd[:], var_eps[:], minus_half[:], ALU.pow).then_inc(rstd_made, 1)
                    if h % PAIR == 1 and t.has(k):
                        mask(t, k, h)

            pool.wait_ge(consts_loaded, 16 * len(CONSTS))
            pool.wait_ge(made, 8)
            turns(pool, B, body)

        @block.tensor
        def _(pe):
            pe.wait_ge(made, 8)
            pe.wait_ge(consts_loaded, 16 * len(CONSTS))

            def scores(t, h):
                par, b = t.parity(0), t.batch(0)
                first = not t.steady and t.c == 0 and h == 0
                if h % HALF == 0:
                    wait_stacks(pe, t, 0, h // HALF)
                q, k = q_stack[par][0:SPLIT_ROWS, h, :], k_stack[par][0:SPLIT_ROWS, h, :]

                def product(bank, at, n, first, blocks):
                    return pe.matmul(bank[:, at:at + blocks * P], q[:, n * P:(n + 1) * P], k[:, first * P:(first + blocks) * P],
                                     start=True, stop=True)

                if not first:
                    pe.wait_ge(s_taken[0], H * b + h)
                for n in range(NT):
                    pe.matmul(s_bank[0][:, n * P:(n + 1) * P], q[:, n * P:(n + 1) * P], k[:, n * P:(n + 1) * P],
                              start=(n == 0), stop=False, skip_group_check=True)
                pe.matmul(s_bank[0][:], ident16[:], above[:].rearrange("p n c -> p (n c)"), start=False, stop=True,
                          skip_group_check=True).then_inc(s_ready[0], 1)
                if not first:
                    pe.wait_ge(s_taken[1], H * b + h)
                product(s_bank[1], 0, 3, 0, 3)
                product(s_bank[1], 3 * P, 1, 0, 1).then_inc(s_ready[1], 1)
                if h % PAIR == 0:
                    if not first:
                        pe.wait_ge(s_taken[2], HALF * b + h // PAIR)
                    product(s_bank[2], 0, 2, 0, 2)
                else:
                    product(s_bank[2], SHORT, 2, 0, 2).then_inc(s_ready[2], 1)

            def scores_t(t, kk, h):
                par, b = t.parity(kk), t.batch(kk)
                first = not t.steady and t.c + kk == 0 and h == 0
                if h % HALF == 0:
                    pe.wait_ge(max_stacked[h // HALF], 16 * (b + 1))
                q, k = q_stack[par][0:STACK, h, :], k_stack[par][0:STACK, h, :]

                def product(bank, at, n, first, blocks):
                    return pe.matmul(bank[:, at:at + blocks * P], k[:, n * P:(n + 1) * P], q[:, first * P:(first + blocks) * P],
                                     start=True, stop=True)

                if not first:
                    pe.wait_ge(t_taken[0], H * b + h)
                for n in range(NT):
                    mm = product(t_bank[0], n * P, n, n, 1)
                mm.then_inc(t_ready[0], 1)
                if not first:
                    pe.wait_ge(t_taken[1], H * b + h)
                product(t_bank[1], 0, 0, 1, 3)
                product(t_bank[1], 3 * P, 2, 3, 1).then_inc(t_ready[1], 1)
                if h % PAIR == 0:
                    if not first:
                        pe.wait_ge(t_taken[2], HALF * b + h // PAIR)
                    product(t_bank[2], 0, 1, 2, 2)
                else:
                    product(t_bank[2], SHORT, 1, 2, 2).then_inc(t_ready[2], 1)

            def context(t, g, piece):
                b = t.batch(-1)
                if piece == 0:
                    pe.wait_ge(masked, (H // PAIR) * b + (GROUP // PAIR) * (g + 1))
                    pe.wait_ge(t_taken[2], (H // PAIR) * b + (GROUP // PAIR) * (g + 1))
                    if g > 0 or t.has(-2):
                        pe.wait_ge(c_taken, NG * b + g)
                    if g == 0:
                        pe.wait_ge(m_taken, t.before().misc_count("v"))
                diagonal, long, short = probs_of(g, 0, GROUP)
                runs = [[(long, LONG, 0, 0, 1, 3)],
                        [(short, SHORT, 0, 1, 2, 2), (long, LONG, 3 * P, 2, 3, 1)],
                        [(diagonal, DIAG, n * P, n, n, 1) for n in range(NT)]][piece]
                for strip, width, at, n, first, count in runs:
                    for j in range(GROUP):
                        mm = pe.matmul(c_bank[32 * j:32 * j + 32, first * P:(first + count) * P],
                                       v_aug[t.parity(-1)][:, n, GROUP * g + j, :],
                                       strip[:, j * width + at:j * width + at + count * P],
                                       start=(piece == 0), stop=(n == NT - 1), skip_group_check=True)
                if piece == 2:
                    mm.then_inc(c_ready, 1)

            def misc(t, name, k):
                count = t.misc_count(name)
                b = t.batch(k)
                if t.steady or count > 1:
                    pe.wait_ge(m_taken, count - 1)
                if name in ("q", "k"):
                    if name == "q":
                        pe.wait_ge(x_t_loaded[t.parity(k)], 16 * (t.half(k) + 1))
                    mm = pe.matmul(m_bank[:], (wq if name == "q" else wk)[:], x_t[t.parity(k)][:], start=True, stop=True)
                elif name == "v":
                    for n in range(NT):
                        mm = pe.matmul(m_bank[:, n * D:(n + 1) * D], x_t[t.parity(k)][:, n * P:(n + 1) * P], wv[:],
                                       start=True, stop=True)
                elif name in ("max0", "max1"):
                    half = int(name[-1])
                    pe.wait_ge(max_split, 2 * b + half + 1)
                    for n in range(NT):
                        mm = pe.transpose(M16[0:PARTS * HALF, n * P:(n + 1) * P],
                                          max_part[:, half, n, :, :].rearrange("p a h -> p (a h)"), ident16[:])
                elif name[:3] == "ctx":
                    n = int(name[-1])
                    if n == 0:
                        pe.wait_ge(c_taken, NG * (b + 1))
                    for g in range(NG):
                        mm = pe.transpose(m_bank[:, g * P:(g + 1) * P], ctx_t[t.parity(k)][:, g, n * P:(n + 1) * P], ident[:])
                elif name == "turn":
                    for n in range(NT):
                        mm = pe.transpose(m_bank[:, n * P:(n + 1) * P], ctx_n[:, n, :], ident[:])
                elif name == "out":
                    for n in range(NT):
                        mm = pe.matmul(m_bank[:, n * D:(n + 1) * D], ctx_back[:, n * P:(n + 1) * P], wo[:],
                                       start=True, stop=True)
                elif name == "xturn":
                    pe.wait_ge(normed, NT * (b + 1))
                    for n in range(NT):
                        mm = pe.transpose(m_bank[:, n * P:(n + 1) * P], x1_now[:, n, :], ident[:])
                elif name == "gate":
                    for n in range(NT):
                        mm = pe.matmul(m_bank[:, n * 8:(n + 1) * 8], x1_t[:, n * P:(n + 1) * P], gate_w[:],
                                       start=True, stop=True)
                mm.then_inc(m_ready, 1)

            def body(t):
                for s in range(H):
                    if t.has(0):
                        scores(t, s)
                    kk = 0 if s >= LAG else -1
                    if t.has(kk):
                        scores_t(t, kk, (s - LAG) % H)
                    if s % GROUP > 0 and t.has(-1):
                        context(t, s // GROUP, s % GROUP - 1)
                    for slot, name, k in MISC:
                        if slot == s and t.has(k):
                            misc(t, name, k)

            turns(pe, B, body)

        @block.scalar
        def _(act):
            def exps(t, kk, h):
                b = t.batch(kk)
                diagonal, long, _ = probs_of(h // GROUP, h % GROUP, 1)
                if h % GROUP == 0 and (t.steady or NG * (t.c + kk) + h // GROUP >= 2):
                    act.wait_ge(c_ready, NG * b + h // GROUP - 1)
                act.wait_ge(t_ready[0], H * b + h + 1)
                act.activation(diagonal, t_bank[0][:], ACT.Exp, scale=SCALE).then_inc(t_taken[0], 1)

                act.wait_ge(t_ready[1], H * b + h + 1)
                act.activation(long, t_bank[1][:], ACT.Exp, scale=SCALE).then_inc(t_taken[1], 1)
                if h % PAIR == 1:
                    _, _, short = probs_of(h // GROUP, h % GROUP - 1, PAIR)
                    act.wait_ge(t_ready[2], HALF * b + h // PAIR + 1)
                    act.activation(short, t_bank[2][:], ACT.Exp, scale=SCALE).then_inc(t_taken[2], 1)

            def misc(t, name, k):
                count = t.misc_count(name)
                b = t.batch(k)
                if name in ("q", "k"):
                    which = int(name == "k")
                    act.wait_ge(m_ready, count)
                    if which == 0 and (t.steady or t.c + k > 0):
                        act.wait_ge(part3_made, b)
                    act.activation(qk[:, which, :], m_bank[:], ACT.Identity, bias=qk_bias[:, which:which + 1]).then_inc(m_taken, 1)
                elif name in ("max0", "max1"):
                    half = int(name[-1])
                    act.wait_ge(m_ready, count)
                    if t.steady or t.c + k > 0:
                        act.wait_ge(max_stacked[half], 16 * b)
                    act.activation(max_rows[half][:], M16[0:PARTS * HALF, 0:S], ACT.Copy).then_inc(m_taken, 1)
                    act.wait_ge(m_taken, count)
                    act.dma_start(
                        q_stack[t.parity(k)][SPLIT_ROWS:STACK, half * HALF:(half + 1) * HALF, :],
                        max_rows[half][:],
                    ).then_inc(max_stacked[half], 16)
                elif name == "turn":
                    act.wait_ge(m_ready, count)
                    act.activation(ctx_back[:], m_bank[:], ACT.Copy).then_inc(m_taken, 1)
                elif name == "xturn":
                    act.wait_ge(m_ready, count)
                    act.activation(x1_t[:], m_bank[:], ACT.Copy).then_inc(m_taken, 1)

            def keep_context(t, k, g):
                act.wait_ge(c_ready, NG * t.batch(k) + g + 1)
                if g == 0 and t.has(-3):
                    act.wait_ge(m_taken, t.before().misc_count("ctx3"))
                act.activation(ctx_t[t.parity(k)][:, g, :], c_bank[:], ACT.Copy).then_inc(c_taken, 1)

            def body(t):
                for s in range(H):
                    if s == 0 and t.has(-2):
                        keep_context(t, -2, NG - 1)
                    if s % GROUP == 0 and s > 0 and t.has(-1):
                        keep_context(t, -1, s // GROUP - 1)
                    for slot, name, k in MISC:
                        if slot == s - 1 and t.has(k):
                            misc(t, name, k)
                    kk = 0 if s >= LAG else -1
                    if t.has(kk):
                        exps(t, kk, (s - LAG) % H)

            act.wait_ge(consts_loaded, 16 * len(CONSTS))
            turns(act, B, body)

        @block.vector
        def _(dve):
            for p in range(2):
                nc.vector.memset(v_aug[p][:], 1.0).then_inc(ones_made, 1)
                nc.vector.memset(k_stack[p][64:P, :, :], 1.0).then_inc(ones_made, 1)
            dve.wait_ge(consts_loaded, 16 * len(CONSTS))

            def maxima(t, h):
                b = t.batch(0)
                half, hh = h // HALF, h % HALF
                if hh == 0 and (t.steady or t.c > 0):
                    dve.wait_ge(max_split, 2 * b + half - 1)
                off = lambda n: off_max[:, half, n - 1, hh:hh + 1]
                dve.wait_ge(s_ready[0], H * b + h + 1)
                nc.vector.tensor_reduce(row_max[:, half, :, hh], s_bank[0][:].rearrange("p (n c) -> p n c", n=NT), AX.X,
                                        ALU.max).then_inc(s_taken[0], 1)

                dve.wait_ge(s_ready[1], H * b + h + 1)
                nc.vector.tensor_reduce(off(3), s_bank[1][:, 0:3 * P], AX.X, ALU.max).then_inc(max_reduced, 1)
                nc.vector.tensor_reduce(off(1), s_bank[1][:, 3 * P:S], AX.X, ALU.max).then_inc(s_taken[1], 1)
                if h % PAIR == 1:
                    dve.wait_ge(s_ready[2], HALF * b + h // PAIR + 1)
                    nc.vector.tensor_reduce(off_max[:, half, 1, hh - 1:hh + 1],
                                            s_bank[2][:].rearrange("p (h c) -> p h c", h=PAIR), AX.X,
                                            ALU.max).then_inc(s_taken[2], 1)
                if hh == HALF - 1:
                    split_maxima(t, half)

            def split_maxima(t, half):
                b = t.batch(0)
                m = row_max[:, half, :, :]
                pieces = [max_part[:, half, :, n, :] for n in range(PARTS)]
                if t.steady or t.c > 0:
                    dve.wait_ge(m_ready, t.before().misc_count("max0") if half == 0 else t.misc_count("max1"))
                dve.wait_ge(s_taken[0], H * b + (half + 1) * HALF)
                dve.wait_ge(max_reduced, H * b + (half + 1) * HALF)
                dve.wait_ge(s_taken[1], H * b + (half + 1) * HALF)
                dve.wait_ge(s_taken[2], HALF * b + (half + 1) * (HALF // PAIR))
                step = 4 * (2 * b + half)
                nc.vector.tensor_tensor(m[:, 1:NT], m[:, 1:NT], off_max[:, half], ALU.max).then_inc(max_step, 1)
                dve.wait_ge(max_step, step + 1)
                nc.vector.tensor_scalar(pieces[0], m, -1.0, None, ALU.mult).then_inc(max_step, 1)
                dve.wait_ge(max_step, step + 2)
                nc.vector.scalar_tensor_tensor(out=max_rest[:], in0=m, scalar=-1.0, in1=pieces[0], op0=ALU.mult,
                                               op1=ALU.subtract).then_inc(max_step, 1)
                dve.wait_ge(max_step, step + 3)
                nc.vector.tensor_copy(pieces[1], max_rest[:]).then_inc(max_step, 1)
                dve.wait_ge(max_step, step + 4)
                nc.vector.tensor_tensor(pieces[2], max_rest[:], pieces[1], ALU.subtract).then_inc(max_split, 1)

            def misc(t, name, k):
                count = t.misc_count(name)
                b = t.batch(k)
                if name == "k":
                    dve.wait_ge(m_taken, count)
                    if t.steady or t.c + k > 0:
                        dve.wait_ge(parts_written[t.parity(k - 1)], 16 * 2 * PARTS * (t.half(k - 1) + 1))
                    nc.vector.tensor_copy(part[0][:], qk[:]).then_inc(part1_made, 1)
                elif name == "v":
                    dve.wait_ge(m_ready, count)
                    if t.steady or t.c + k >= 2:
                        dve.wait_ge(c_ready, NG * (b - 1))
                    for n in range(NT):
                        add = nc.vector.tensor_tensor(
                            v_aug[t.parity(k)][:, n, :, 0:HD], m_bank[:, n * D:(n + 1) * D].rearrange("p (h d) -> p h d", d=HD),
                            v_bias[:].rearrange("p (h d) -> p h d", d=HD), ALU.add)
                    add.then_inc(m_taken, 1)
                elif name[:3] == "ctx":
                    n = int(name[-1])
                    dve.wait_ge(m_ready, count)
                    if n == 0 and t.has(-3):
                        dve.wait_ge(m_taken, t.before().misc_count("turn"))
                    strips = m_bank[:].rearrange("p (h c) -> p h c", h=H)
                    nc.vector.reciprocal(inv_sum[:], strips[:, :, SUM_COL]).then_inc(sums_inverted, 1)
                    dve.wait_ge(sums_inverted, NT * b + n + 1)
                    nc.vector.tensor_tensor(ctx_n[:, n, :].rearrange("p (h d) -> p h d", h=H), strips[:, :, 0:HD],
                                            inv_sum[:].rearrange("p (h o) -> p h o", o=1).to_broadcast([P, H, HD]),
                                            ALU.mult).then_inc(m_taken, 1)
                elif name == "out":
                    dve.wait_ge(m_ready, count)
                    dve.wait_ge(x_plus_made, b + 1)
                    nc.vector.tensor_tensor(res[:].rearrange("p n d -> p (n d)"), m_bank[:],
                                            res[:].rearrange("p n d -> p (n d)"), ALU.add).then_inc(m_taken, 1)
                    dve.wait_ge(m_taken, count)
                    nc.vector.bn_stats(stats[:, 0, :], res[:, 0, :]).then_inc(stats_made, 1)
                    for n in range(1, NT):
                        nc.vector.bn_stats(stats[:, n, :], res[:, n, :]).then_inc(stats_made, 1)
                    if t.steady or t.c + k > 0:
                        dve.wait_ge(rstd_made, b)
                    for n in range(NT):
                        dve.wait_ge(stats_made, NT * b + n + 1)
                        dve.nop(nofuse=True)
                        nc.vector.bn_aggr(mean_var[:, n, :], stats[:, n, :]).then_inc(mean_made, 1)
                elif name == "gate":
                    dve.wait_ge(m_ready, count)
                    nc.vector.tensor_tensor(logits[:, bass.ds(b * NT, NT), :],
                                            m_bank[:, 0:NT * 8].rearrange("p (n e) -> p n e", n=NT), gate_bias[:],
                                            ALU.add).then_inc(m_taken, 1)

            def normalise(t):
                b = t.batch(-2)
                dve.wait_ge(rstd_made, b + 1)
                if t.has(-3):
                    dve.wait_ge(x1_kept, 16 * b)
                for n in range(NT):
                    nc.vector.tensor_scalar(x1_now[:, n, :], res[:, n, :], mean_var[:, n, 0:1], rstd[:, n:n + 1],
                                            ALU.subtract, ALU.mult).then_inc(normed, 1)

            def body(t):
                for s in range(H):
                    for slot, name, k in MISC:
                        if slot == s - 1 and t.has(k):
                            misc(t, name, k)
                    if s == 7 and t.has(1):
                        dve.wait_ge(rest_made, t.batch(1) + 1)
                        nc.vector.tensor_copy(part[1][:], rest[:]).then_inc(part2_made, 1)
                    if s == 10 and t.has(-2):
                        normalise(t)
                    if t.has(0):
                        maxima(t, s)

            dve.wait_ge(ones_made, 4)
            turns(dve, B, body)



class Step:

    def __init__(self, j, c, first, count, steady=False):
        self.j, self.c, self.first, self.count, self.steady = j, c, first, count, steady

    def has(self, k):
        return self.steady or self.first <= self.c + k < self.first + self.count

    def block(self, k=0):
        return self.j * 2 + (self.c + k)

    def parity(self, k=0):
        return (self.c + k) % 2

    def half(self, k=0):
        return self.j + (self.c + k) // 2

    def later(self, k, n):
        return self.steady or self.c + k >= n


def steps(eng, first, count, body):
    for c in range(first - 1, first + 2):
        body(Step(0, c, first, count))
    pairs = (count - 4) // 2
    with eng.Fori(0, pairs) as j:
        for c in (first + 2, first + 3):
            body(Step(j, c, first, count, steady=True))
    for c in range(first + 2 + 2 * pairs, first + count + 2):
        body(Step(0, c, first, count))


def most_blocks(tiles):
    n = (TOP_K * tiles * P + E * (P - 1)) // P
    return n + n % 2


def experts(nc, ctx, a, x1, logits, arena, chunks, out):

    def sb(name, shape, dt=F32):
        return ctx.enter_context(nc.sbuf_tensor(name, shape, dt))

    def sem(name):
        return ctx.enter_context(nc.semaphore(name))

    tiles = sum(n for _, n in chunks)
    most = max(n for _, n in chunks)
    blocks = [most_blocks(n) for _, n in chunks]
    first_block = [sum(blocks[:c]) for c in range(len(chunks))]
    n_blocks = sum(blocks)

    w1 = arena[:, 0:E * FF]
    w3 = arena[:, E * FF:2 * E * FF]
    w2 = arena[:, 2 * E * FF:3 * E * FF]

    x_slots = nc.dram_tensor("x_slots", [n_blocks * P, D], F32, kind="Internal").ap()
    y_slots = nc.dram_tensor("y_slots", [n_blocks * P, D], F32, kind="Internal").ap()

    zeros = sb("zeros", [P, 8 * D])
    iota_i = sb("iota_i", [P, E], I32)
    rank = sb("rank", [P, E])
    block_i = sb("block_i", [1, max(blocks)], I32)
    block_no = sb("block_no", [1, max(blocks)])
    earlier = sb("earlier", [P, P], BF16)
    ones16 = sb("ones16", [P, P], BF16)
    ones_row = sb("ones_row", [P, most])
    ones8 = sb("ones8", [P, E])
    wide = {n: sb(n, [P, most, E]) for n in ("prob", "match", "one_hot1", "one_hot2", "slot_e", "picked")}
    chosen = sb("chosen", [P, most, E], BF16)
    tile_sum = sb("tile_sum", [P, E, most])
    tile_end = sb("tile_end", [P, E, most])
    thin = {n: sb(n, [P, most]) for n in ("top", "total", "inverse", "first_rank", "prob1", "prob2")}
    weight = [sb(f"weight{k}", [P, tiles]) for k in range(TOP_K)]
    slot = [sb(f"slot{k}", [P, tiles], I32) for k in range(TOP_K)]
    few = {n: sb(n, [P, E]) for n in ("filled", "ends", "starts")}
    few_i = sb("few_i", [P, E], I32)
    at_or_past = sb("at_or_past", [1, max(blocks), E])
    block_e = sb("block_e", [1, max(blocks)])
    w_offset = sb("w_offset", [1, n_blocks], I32)
    ident = sb("identity", [P, P])

    x_in = [sb(f"x_in{p}", [P, D]) for p in range(2)]
    x_t = [sb(f"x_in_t{p}", [P, P]) for p in range(2)]
    silu = [sb(f"silu{p}", [P, FF]) for p in range(2)]
    gated = [sb(f"gated{p}", [P, FF]) for p in range(2)]
    h_t = [sb(f"h_t{p}", [P, FC, P]) for p in range(2)]
    y_out = [sb(f"y_out{p}", [P, D]) for p in range(2)]

    picks = [sb(f"picks{p}", [P, CG, TOP_K, D]) for p in range(2)]
    part_sum = sb("part_sum", [P, CG, D])
    total_sum = [sb(f"total_sum{p}", [P, CG, D]) for p in range(2)]
    stats = sb("stats2", [P, CG, 6])
    mean_var = [sb(f"mean_var2{p}", [P, CG, 2]) for p in range(2)]
    var_eps = sb("var_eps2", [P, CG])
    eps_col = sb("eps_col2", [P, CG])
    minus_half = sb("minus_half2", [P, CG])
    rstd = [sb(f"rstd2{p}", [P, CG]) for p in range(2)]
    final = [sb(f"final{p}", [P, CG, D]) for p in range(2)]

    def bank(name):
        return ctx.enter_context(nc.psum_tensor(name, [P, S], F32))
    h1_bank = [bank(f"h1_bank{p}") for p in range(2)]
    h3_bank = [bank(f"h3_bank{p}") for p in range(2)]
    ht_bank = [bank(f"ht_bank{p}") for p in range(2)]
    xt_bank = bank("xt_bank")
    y_bank = bank("y_bank")

    weights_loaded = sem("weights_loaded")
    zeroed = sem("zeroed")
    made = sem("made2")
    zeros_made = sem("zeros_made")
    iota_made = sem("iota_made")
    routed = sem("routed")
    exp_done = sem("exp_done")
    shifted = sem("shifted")
    counted = sem("counted")
    slots_made = sem("slots_made")
    scattered = [sem(f"scattered{c}") for c in range(len(chunks))]
    x_loaded = [sem(f"x_loaded{p}") for p in range(2)]
    x_turned = sem("x_turned")
    xt_copied = sem("xt_copied")
    h1_ready = sem("h1_ready")
    h3_ready = sem("h3_ready")
    silu_made = sem("silu_made")
    h_gated = sem("h_gated")
    ht_ready = sem("ht_ready")
    ht_copied = sem("ht_copied")
    y_ready = sem("y_ready")
    y_copied = sem("y_copied")
    y_stored = [sem(f"y_stored{p}") for p in range(2)]
    gathered = [sem(f"gathered{p}") for p in range(2)]
    summed = sem("summed")
    sum_step = sem("sum_step")
    stats_made = sem("stats_made2")
    mean_made = sem("mean_made2")
    var_eps_made = sem("var_eps_made2")
    rstd_made = sem("rstd_made2")
    final_made = sem("final_made")
    stored = [sem(f"stored{p}") for p in range(2)]

    n_groups = tiles // CG
    N_ZERO = n_blocks * P * D // (P * 8 * D)
    N_MADE = 7

    def y_all_stored(eng, block):
        for p in range(2):
            eng.wait_ge(y_stored[p], 16 * ((block - p + 1) // 2))

    with nc.Block() as block:

        @block.sync
        def _(sp):
            for n, (tile, name) in enumerate(((w1, "w1"), (w3, "w3"))):
                sp.dma_start(tile.rearrange("p (e f) -> p e f", e=E), a[name].rearrange("e d f -> d e f")).then_inc(weights_loaded, 16)
            for e in range(E):
                sp.dma_start(w2[:, e * FF:(e + 1) * FF].rearrange("p (c d) -> p c d", c=FC),
                             a["w2"][e].rearrange("(c p) d -> p c d", p=P)).then_inc(weights_loaded, 16)
            sp.wait_ge(zeros_made, 1)
            for n in range(N_ZERO):
                sp.dma_start(x_slots[n * 8 * P:(n + 1) * 8 * P].rearrange("(p r) d -> p (r d)", p=P), zeros[:]).then_inc(zeroed, 16)

            for c, (_, n_tiles) in enumerate(chunks):
                sp.wait_ge(scattered[c], 16 * TOP_K * n_tiles)

                def load(t, k):
                    sp.dma_start(x_in[t.parity(k)][:], x_slots[bass.ds(t.block(k) * P, P), :]).then_inc(x_loaded[t.parity(k)], 16)

                def body(t):
                    if t.c == t.first - 1 and not t.steady:
                        load(t, 1)
                        load(t, 2)
                    elif t.has(0) and (t.steady or t.has(2)):
                        sp.wait_ge(x_turned, t.block() + 1)
                        load(t, 2)
                    if t.has(-2):
                        sp.wait_ge(y_copied, t.block(-1))
                        sp.dma_start(y_slots[bass.ds(t.block(-2) * P, P), :], y_out[t.parity(-2)][:]).then_inc(y_stored[t.parity(-2)], 16)

                steps(sp, first_block[c], blocks[c], body)

            out_g = out.rearrange("(g n p) d -> g p n d", n=CG, p=P)
            with sp.Fori(0, n_groups // 2) as j:
                for p in range(2):
                    sp.wait_ge(final_made, (j * 2 + (p + 1)) * CG)
                    sp.dma_start(out_g[j * 2 + p], final[p][:]).then_inc(stored[p], 16)
            y_all_stored(sp, n_blocks)
            for p in range(2):
                sp.wait_ge(stored[p], 16 * (n_groups // 2))

        @block.gpsimd
        def _(pool):
            pool.iota(iota_i[:], [[-1, E]], base=E, channel_multiplier=0).then_inc(iota_made, 1)
            pool.iota(block_i[:], [[1, max(blocks)]], base=0, channel_multiplier=0).then_inc(iota_made, 1)
            pool.memset(ident[:], 0.0).then_inc(made, 1)
            pool.memset(earlier[:], 1.0).then_inc(made, 1)
            pool.memset(ones16[:], 1.0).then_inc(made, 1)
            pool.memset(eps_col[:], EPS).then_inc(made, 1)
            pool.memset(minus_half[:], -0.5).then_inc(made, 1)
            pool.wait_ge(made, 5)
            pool.affine_select(out=ident[:], in_=ident[:], compare_op=ALU.not_equal, fill=1.0, base=0,
                               pattern=[[-1, P]], channel_multiplier=1).then_inc(made, 1)
            pool.affine_select(out=earlier[:], in_=earlier[:], compare_op=ALU.is_ge, fill=0.0, base=-1,
                               pattern=[[1, P]], channel_multiplier=-1).then_inc(made, 1)
            pool.wait_ge(zeroed, 16 * N_ZERO)
            for c, (t0, n_tiles) in enumerate(chunks):
                pool.wait_ge(slots_made, TOP_K * (c + 1))
                for n in range(t0, t0 + n_tiles):
                    for k in range(TOP_K):
                        pool.indirect_dma_start(
                            out=x_slots, out_offset=bass.IndirectOffsetOnAxis(ap=slot[k][:, n:n + 1], axis=0),
                            in_=x1[:, n, :], in_offset=None).then_inc(scattered[c], 16)

            def scale(g):
                p = g % 2
                pool.wait_ge(mean_made, CG * (g + 1))
                if g >= 1:
                    pool.wait_ge(rstd_made, g)
                pool.tensor_tensor(var_eps[:], mean_var[p][:, :, 1], eps_col[:], ALU.add).then_inc(var_eps_made, 1)
                pool.wait_ge(var_eps_made, g + 1)
                if g >= 2:
                    pool.wait_ge(final_made, CG * (g - 1))
                pool.tensor_tensor(rstd[p][:], var_eps[:], minus_half[:], ALU.pow).then_inc(rstd_made, 1)

            for c, (t0, n_tiles) in enumerate(chunks):
                y_all_stored(pool, first_block[c] + blocks[c])
                for g in range(t0 // CG, (t0 + n_tiles) // CG):
                    if g >= 2:
                        pool.wait_ge(summed, CG * (g - 1))
                    for n in range(CG):
                        for k in range(TOP_K):
                            pool.indirect_dma_start(
                                out=picks[g % 2][:, n, k, :], out_offset=None, in_=y_slots,
                                in_offset=bass.IndirectOffsetOnAxis(ap=slot[k][:, g * CG + n:g * CG + n + 1], axis=0),
                            ).then_inc(gathered[g % 2], 16)
                    if g >= 1:
                        scale(g - 1)
            scale(n_groups - 1)

        @block.vector
        def _(dve):
            chain = [0]

            def link(ins):
                chain[0] += 1
                ins.then_inc(routed, 1)
                dve.wait_ge(routed, chain[0])

            v = nc.vector
            v.memset(zeros[:], 0.0).then_inc(zeros_made, 1)
            link(v.memset(ones_row[:], 1.0))
            link(v.memset(ones8[:], 1.0))
            dve.wait_ge(iota_made, 2)
            link(v.tensor_copy(rank[:], iota_i[:]))
            link(v.tensor_copy(block_no[:], block_i[:]))

            def route(c):
                t0, n = chunks[c]
                nb = blocks[c]
                prob, match, one_hot1, one_hot2, slot_e, picked = (wide[x][:, 0:n, :] for x in (
                    "prob", "match", "one_hot1", "one_hot2", "slot_e", "picked"))
                top, total, inverse, first_rank, prob1, prob2 = (thin[x][:, 0:n] for x in (
                    "top", "total", "inverse", "first_rank", "prob1", "prob2"))
                filled, ends, starts = (few[x][:] for x in ("filled", "ends", "starts"))
                per_tile = lambda x: x.rearrange("p (n o) -> p n o", o=1).to_broadcast([P, n, E])
                ranks = rank[:].rearrange("p (o e) -> p o e", o=1).to_broadcast([P, n, E])
                here = logits[:, t0:t0 + n, :]

                link(v.tensor_reduce(top, here, AX.X, ALU.max))
                v.tensor_tensor(match, here, per_tile(top), ALU.subtract).then_inc(shifted, 1)
                dve.wait_ge(exp_done, c + 1)
                link(v.tensor_reduce(total, prob, AX.X, ALU.add))
                link(v.reciprocal(inverse, total))
                link(v.tensor_tensor(prob, prob, per_tile(inverse), ALU.mult))
                link(v.tensor_reduce(prob1, prob, AX.X, ALU.max))
                link(v.tensor_tensor(match, prob, per_tile(prob1), ALU.is_equal))
                link(v.tensor_tensor(match, match, ranks, ALU.mult))
                link(v.tensor_reduce(first_rank, match, AX.X, ALU.max))
                link(v.tensor_tensor(one_hot1, ranks, per_tile(first_rank), ALU.is_equal))
                link(v.scalar_tensor_tensor(out=prob, in0=one_hot1, scalar=-2.0, in1=prob, op0=ALU.mult, op1=ALU.add))
                link(v.tensor_reduce(prob2, prob, AX.X, ALU.max))
                link(v.tensor_tensor(match, prob, per_tile(prob2), ALU.is_equal))
                link(v.tensor_tensor(match, match, ranks, ALU.mult))
                link(v.tensor_reduce(first_rank, match, AX.X, ALU.max))
                link(v.tensor_tensor(one_hot2, ranks, per_tile(first_rank), ALU.is_equal))
                v.tensor_tensor(chosen[:, 0:n, :], one_hot1, one_hot2, ALU.add).then_inc(shifted, 1)
                link(v.tensor_tensor(total, prob1, prob2, ALU.add))
                link(v.reciprocal(inverse, total))
                link(v.tensor_tensor(weight[0][:, t0:t0 + n], prob1, inverse, ALU.mult))
                link(v.tensor_tensor(weight[1][:, t0:t0 + n], prob2, inverse, ALU.mult))
                sums, ends_t = tile_sum[:, :, 0:n], tile_end[:, :, 0:n]
                dve.wait_ge(counted, 2 * (c + 1))
                link(v.tensor_copy(sums, y_bank[:, 0:n * E].rearrange("p (n e) -> p e n", e=E)))
                for e in range(E):
                    link(v.tensor_tensor_scan(ends_t[:, e, :], ones_row[:, 0:n], sums[:, e, :], 0.0, ALU.mult, ALU.add))
                link(v.tensor_scalar(few_i[:], ends_t[:, :, n - 1], float(P - 1), None, ALU.add))
                link(v.tensor_single_scalar(few_i[:], few_i[:], 7, ALU.logical_shift_right))
                link(v.tensor_copy(filled, few_i[:]))
                link(v.tensor_tensor_scan(ends, ones8[:], filled, 0.0, ALU.mult, ALU.add))
                link(v.tensor_tensor(starts, ends, filled, ALU.subtract))
                link(v.tensor_scalar(starts, starts, float(first_block[c]), float(P), ALU.add, ALU.mult))
                link(v.tensor_tensor(ends_t, ends_t, sums, ALU.subtract))
                link(v.tensor_tensor(ends_t, ends_t, starts.rearrange("p (e o) -> p e o", o=1).to_broadcast([P, E, n]), ALU.add))
                link(v.tensor_tensor(slot_e, xt_bank[:, 0:n * E].rearrange("p (n e) -> p n e", e=E),
                                     ends_t.rearrange("p e n -> p n e"), ALU.add))
                for k, one_hot in enumerate((one_hot1, one_hot2)):
                    link(v.tensor_tensor(picked, slot_e, one_hot, ALU.mult))
                    link(v.tensor_reduce(first_rank, picked, AX.X, ALU.add))
                    v.tensor_copy(slot[k][:, t0:t0 + n], first_rank).then_inc(slots_made, 1)
                    dve.wait_ge(slots_made, TOP_K * c + k + 1)
                link(v.tensor_tensor(at_or_past[:, 0:nb, :],
                                     block_no[:, 0:nb].rearrange("p (b o) -> p b o", o=1).to_broadcast([1, nb, E]),
                                     ends[0:1].rearrange("p (o e) -> p o e", o=1).to_broadcast([1, nb, E]), ALU.is_ge))
                link(v.tensor_reduce(block_e[:, 0:nb], at_or_past[:, 0:nb, :], AX.X, ALU.add))
                v.tensor_scalar(w_offset[:, first_block[c]:first_block[c] + nb], block_e[:, 0:nb], float(E - 1), float(FF),
                                ALU.min, ALU.mult).then_inc(shifted, 1)

            for c in range(len(chunks)):
                route(c)

            def body(t):
                if t.has(1):
                    dve.wait_ge(x_turned, t.block(2))
                    if t.later(1, 2):
                        dve.wait_ge(h3_ready, t.block())
                    v.tensor_copy(x_t[t.parity(1)][:], xt_bank[:, 0:P]).then_inc(xt_copied, 1)
                if t.has(0):
                    dve.wait_ge(silu_made, t.block(1))
                    dve.wait_ge(h3_ready, t.block(1))
                    if t.later(0, 2):
                        dve.wait_ge(ht_ready, t.block(-1))
                    v.tensor_tensor(gated[t.parity()][:], silu[t.parity()][:], h3_bank[t.parity()][:], ALU.mult).then_inc(h_gated, 1)
                if t.has(-2):
                    dve.wait_ge(y_ready, t.block(-1))
                    if t.later(-2, 2):
                        dve.wait_ge(y_stored[t.parity(-2)], 16 * t.half(-2))
                    v.tensor_copy(y_out[t.parity(-2)][:], y_bank[:, 0:D]).then_inc(y_copied, 1)

            for c in range(len(chunks)):
                steps(dve, first_block[c], blocks[c], body)

            def combine(j, p):
                g = j * 2 + p
                dve.wait_ge(gathered[p], 16 * CG * TOP_K * (j + 1))
                for n in range(CG):
                    tile = g * CG + n
                    v.scalar_tensor_tensor(out=part_sum[:, n, :], in0=picks[p][:, n, 0, :], scalar=weight[0][:, bass.ds(tile, 1)],
                                           in1=x1[:, tile, :], op0=ALU.mult, op1=ALU.add).then_inc(sum_step, 1)
                for n in range(CG):
                    tile = g * CG + n
                    dve.wait_ge(sum_step, tile + 1)
                    v.scalar_tensor_tensor(out=total_sum[p][:, n, :], in0=picks[p][:, n, 1, :], scalar=weight[1][:, bass.ds(tile, 1)],
                                           in1=part_sum[:, n, :], op0=ALU.mult, op1=ALU.add).then_inc(summed, 1)
                for n in range(CG):
                    dve.wait_ge(summed, g * CG + n + 1)
                    v.bn_stats(stats[:, n, :], total_sum[p][:, n, :]).then_inc(stats_made, 1)
                for n in range(CG):
                    dve.wait_ge(stats_made, g * CG + n + 1)
                    dve.nop(nofuse=True)
                    v.bn_aggr(mean_var[p][:, n, :], stats[:, n, :]).then_inc(mean_made, 1)

            def normalise(j, p, wait_store):
                g = j * 2 + p
                dve.wait_ge(rstd_made, g + 1)
                if wait_store:
                    dve.wait_ge(stored[p], 16 * j)
                for n in range(CG):
                    v.tensor_scalar(final[p][:, n, :], total_sum[p][:, n, :], mean_var[p][:, n, 0:1], rstd[p][:, n:n + 1],
                                    ALU.subtract, ALU.mult).then_inc(final_made, 1)

            combine(0, 0)
            combine(0, 1)
            normalise(0, 0, False)
            combine(1, 0)
            normalise(0, 1, False)
            combine(1, 1)
            normalise(1, 0, True)
            with dve.Fori(2, n_groups // 2) as j:
                combine(j, 0)
                normalise(j - 1, 1, True)
                combine(j, 1)
                normalise(j, 0, True)
            normalise(n_groups // 2 - 1, 1, True)

        @block.scalar
        def _(act):
            for c, (t0, n) in enumerate(chunks):
                act.wait_ge(shifted, 3 * c + 1)
                act.activation(wide["prob"][:, 0:n, :], wide["match"][:, 0:n, :], ACT.Exp).then_inc(exp_done, 1)

            def body(t):
                if t.has(0):
                    act.wait_ge(h1_ready, t.block(1))
                    if t.later(0, 2):
                        act.wait_ge(h_gated, t.block(-1))
                    act.activation(silu[t.parity()][:], h1_bank[t.parity()][:], ACT.Silu).then_inc(silu_made, 1)
                if t.has(-1):
                    act.wait_ge(ht_ready, t.block())
                    if t.later(-1, 2):
                        act.wait_ge(y_ready, t.block(-2))
                    act.activation(h_t[t.parity(-1)][:].rearrange("p c t -> p (c t)"), ht_bank[t.parity(-1)][:], ACT.Copy).then_inc(ht_copied, 1)

            for c in range(len(chunks)):
                steps(act, first_block[c], blocks[c], body)

        @block.tensor
        def _(pe):
            pe.wait_ge(made, N_MADE)
            for c, (t0, n) in enumerate(chunks):
                pe.wait_ge(shifted, 3 * c + 2)
                pe.matmul(xt_bank[:, 0:n * E], earlier[:], chosen[:, 0:n, :].rearrange("p n e -> p (n e)"), start=True, stop=True).then_inc(counted, 1)
                pe.matmul(y_bank[:, 0:n * E], ones16[:], chosen[:, 0:n, :].rearrange("p n e -> p (n e)"), start=True, stop=True).then_inc(counted, 1)
                pe.wait_ge(shifted, 3 * c + 3)

            pe.wait_ge(weights_loaded, 16 * (2 + E))

            def offset(t, k):
                return pe.value_load(w_offset[0:1, bass.ds(t.block(k), 1)], min_val=0, max_val=(E - 1) * FF)

            def body(t):
                p = t.parity()
                if t.has(0):
                    e = offset(t, 0)
                    pe.wait_ge(xt_copied, t.block(1))
                    if t.later(0, 2):
                        pe.wait_ge(silu_made, t.block(-1))
                    pe.matmul(h1_bank[p][:], x_t[p][:], w1[:, bass.ds(e, FF)], start=True, stop=True).then_inc(h1_ready, 1)
                    if t.later(0, 2):
                        pe.wait_ge(h_gated, t.block(-1))
                    pe.matmul(h3_bank[p][:], x_t[p][:], w3[:, bass.ds(e, FF)], start=True, stop=True).then_inc(h3_ready, 1)
                if t.has(1):
                    pe.wait_ge(x_loaded[t.parity(1)], 16 * (t.half(1) + 1))
                    if t.later(1, 1):
                        pe.wait_ge(xt_copied, t.block(1))
                    pe.transpose(xt_bank[:, 0:P], x_in[t.parity(1)][:], ident[:]).then_inc(x_turned, 1)
                if t.has(-1):
                    pe.wait_ge(h_gated, t.block())
                    if t.later(-1, 2):
                        pe.wait_ge(ht_copied, t.block(-2))
                    for f in range(FC):
                        mm = pe.transpose(ht_bank[t.parity(-1)][:, f * P:(f + 1) * P], gated[t.parity(-1)][:, f * P:(f + 1) * P], ident[:])
                    mm.then_inc(ht_ready, 1)
                if t.has(-2):
                    e = offset(t, -2)
                    pe.wait_ge(ht_copied, t.block(-1))
                    if t.later(-2, 1):
                        pe.wait_ge(y_copied, t.block(-2))
                    for f in range(FC):
                        mm = pe.matmul(y_bank[:, 0:D], h_t[t.parity(-2)][:, f, :], w2[:, bass.ds(e + f * D, D)],
                                       start=(f == 0), stop=(f == FC - 1))
                    mm.then_inc(y_ready, 1)

            for c in range(len(chunks)):
                steps(pe, first_block[c], blocks[c], body)


def build(nc, a, out, B):
    with ExitStack() as ctx:
        x1 = ctx.enter_context(nc.sbuf_tensor("x1", [P, NT * B, D], F32))
        logits = ctx.enter_context(nc.sbuf_tensor("logits", [P, NT * B, E], F32))
        arena = ctx.enter_context(nc.sbuf_tensor("arena", [P, 2 * H * S], F32))
        with ExitStack() as own:
            attention(nc, own, a, x1, logits, arena, B)
        with ExitStack() as own:
            experts(nc, own, a, x1, logits, arena, [(0, NT * B)], out)


def kernel(**inputs):
    import concourse.bacc as bacc
    import numpy as np
    from concourse.bass_utils import run_bass_kernel_spmd

    w = {name.split("_", 2)[2]: np.asarray(value) for name, value in inputs.items()}
    B = w["x"].shape[0]
    across = lambda v, n: np.ascontiguousarray(np.broadcast_to(v, (P, n, v.shape[0])))
    layouts = {
        "x_t": w["x"].transpose(0, 2, 1),
        "x_rows": w["x"].reshape(B, NT, P, D).transpose(0, 2, 1, 3),
        "wq": w["Wq"], "wk": w["Wk"], "wv": w["Wv"], "wo": w["Wo"],
        "qk_bias": np.stack([w["bq"], w["bk"]], 1),
        "v_bias": across(w["bv"], 1)[:, 0], "o_bias": across(w["bo"], 1)[:, 0],
        "gate_w": w["gate_w"], "gate_bias": across(w["gate_b"], NT),
        "w1": w["w1"], "w3": w["w3"], "w2": w["w2"],
    }
    layouts = {f"in_{name}": np.ascontiguousarray(value) for name, value in layouts.items()}
    nc = bacc.Bacc("TRN2", target_bir_lowering=False, num_devices=1)
    a = {name[3:]: nc.dram_tensor(name, v.shape, mybir.dt.from_np(v.dtype), kind="ExternalInput").ap()
         for name, v in layouts.items()}
    out = nc.dram_tensor("out", [B * S, D], F32, kind="ExternalOutput").ap()
    build(nc, a, out, B)
    r = run_bass_kernel_spmd(nc, [layouts], core_ids=[0])
    return r.results[0]["out"].reshape(B, S, D)
```

```python
from contextlib import ExitStack

import concourse.bass as bass
from concourse import mybir

F32 = mybir.dt.float32
F32R = mybir.dt.float32r
BF16 = mybir.dt.bfloat16
I32 = mybir.dt.int32
ALU = mybir.AluOpType
ACT = mybir.ActivationFunctionType
AX = mybir.AxisListType

P = 128
D = 128
H = 16
HD = D // H
S = 512
NT = S // P
EPS = 1e-5
SCALE = float(HD) ** -0.5
MASKED = -1.0e30
ONES_16 = 1.0 + 0x3F80 / 2**23
PARTS = 3
SPLIT_ROWS = PARTS * PARTS * HD
STACK = SPLIT_ROWS + PARTS
PAIR = 2
LAG = 12
HALF = H // 2
GROUP = 4
NG = H // GROUP
DIAG, LONG, SHORT = S, S, S // 2
HEAD_P = DIAG + LONG + SHORT
E = 8
TOP_K = 2
FF = 512
FC = FF // P
PERIOD = 6
FIRST_STEPS = 8
ROUTING_STEPS = {-1: (0,), 0: (1, 2), 1: (3, 4), 2: (5, 6), 3: (7, 8), 4: (9,), 5: (10,), 6: (11, 12), 7: (13, 14)}
TILES_STEP, RANKS_STEP = 4, 6
CG = 4
ZERO_COLS = 8 * D
SCATTER_SLOT = 4
SCATTERS = (2, 2, 1, 1)
SUM_COL = HD

MISC = [
    (0, "q", 1), (1, "max1", -1), (2, "ctx0", -2), (3, "ctx1", -2), (4, "k", 1), (5, "ctx2", -2),
    (6, "ctx3", -2), (7, "turn", -2), (8, "out", -2), (9, "max0", 0), (10, "tiles", None),
    (11, "xturn", -2), (12, "v", 0), (13, "gate", -2), (14, "ranks", None),
]
LATE = 5


class Turn:

    def __init__(self, j, c, B, steady=False):
        self.j, self.c, self.B, self.steady = j, c, B, steady

    def has(self, k):
        return k is not None if self.steady else self.among(self.c, k)

    def among(self, c, k):
        return c == self.B - 3 if k is None else 0 <= c + k < self.B

    def batch(self, k):
        return self.j * 2 + (self.c + (k or 0))

    def parity(self, k):
        return (self.c + k) % 2

    def half(self, k):
        return self.j + (self.c + k) // 2

    def before(self):
        return Turn(self.j, self.c - 1, self.B, self.steady)

    def misc_count(self, name):
        n = 0
        for i in range(-1, self.c + 1):
            for _, other, k in MISC:
                if self.among(i, k):
                    n += 1
                if i == self.c and other == name:
                    return self.j * (2 * sum(k is not None for _, _, k in MISC)) + n


def turns(eng, B, body):
    first = 3
    pairs = (B - 3 - first) // 2
    for c in range(-1, first):
        body(Turn(0, c, B))
    with eng.Fori(0, pairs) as j:
        for c in (first, first + 1):
            body(Turn(j, c, B, steady=True))
    for c in range(first + 2 * pairs, B + 2):
        body(Turn(0, c, B))


def most_blocks(tiles):
    n, unit = (TOP_K * tiles * P + E * (P - 1)) // P, ZERO_COLS // D
    return -(-n // unit) * unit


class Routing:

    def __init__(self, nc, ctx, a, logits, x1, B):
        self.nc, self.a, self.logits, self.x1 = nc, a, logits, x1
        self.chunks = [(0, NT * (B - LATE)), (NT * (B - LATE), NT * LATE)]
        self.tiles = NT * B
        self.blocks = [most_blocks(n) for _, n in self.chunks]
        self.first_block = [0, self.blocks[0]]
        self.n_blocks = sum(self.blocks)
        most, wide_b = max(n for _, n in self.chunks), max(self.blocks)

        def sb(name, shape, dt=F32):
            return ctx.enter_context(nc.sbuf_tensor(name, shape, dt))

        def sem(name):
            return ctx.enter_context(nc.semaphore(name))

        self.x_slots, self.y_slots = (
            [nc.dram_tensor(f"{name}{c}", [n * P, D], F32, kind="Internal").ap() for c, n in enumerate(self.blocks)]
            for name in ("x_slots", "y_slots"))
        self.iota_i = sb("iota_i", [P, E], I32)
        self.rank = sb("rank", [P, E])
        self.block_i = sb("block_i", [1, wide_b], I32)
        self.block_no = sb("block_no", [1, wide_b])
        self.earlier = sb("earlier", [P, P], BF16)
        self.ones16 = sb("ones16", [P, P], BF16)
        self.ones_row = sb("ones_row", [P, most])
        self.wide = {n: sb(n, [P, most, E], dt) for n, dt in (("prob", F32), ("match", F32), ("one_hot1", BF16), ("one_hot2", BF16))}
        self.chosen = sb("chosen", [P, most, E], BF16)
        self.tile_sum = sb("tile_sum", [P, E, most])
        self.tile_end = sb("tile_end", [P, E, most])
        self.thin = {n: sb(n, [P, most]) for n in ("top", "total", "inverse", "first_rank", "prob1", "prob2")}
        self.weight = [sb(f"weight{k}", [P, self.tiles]) for k in range(TOP_K)]
        self.slot = [sb(f"slot{k}", [P, self.tiles], I32) for k in range(TOP_K)]
        self.few = {n: sb(n, [P, E]) for n in ("filled", "ends", "starts")}
        self.few_i = sb("few_i", [P, E], I32)
        self.block_e = sb("block_e", [1, wide_b])
        self.w_offset = sb("w_offset", [1, self.n_blocks], I32)

        self.w13_loaded = sem("w13_loaded")
        self.w2_loaded = sem("w2_loaded")
        self.upper_made = sem("upper_made")
        self.lower_made = sem("lower_made")
        self.zeroed = sem("zeroed")
        self.made = sem("routing_made")
        self.iota_made = sem("iota_made")
        self.linked = sem("linked")
        self.logits_shifted = sem("logits_shifted")
        self.exp_done = sem("exp_done")
        self.chosen_made = sem("chosen_made")
        self.slots_made = sem("slots_made")
        self.offsets_made = sem("offsets_made")
        self.scattered = [sem(f"scattered{c}") for c in range(len(self.chunks))]
        self.links = 0
        self.sent = [0, 0]
        rows = ZERO_COLS // D * P
        assert all(n * P % rows == 0 for n in self.blocks)
        self.N_ZERO = self.n_blocks * P // rows

    def zero_slots(self, sp, zeros):
        rows = ZERO_COLS // D * P
        for slots, blocks in zip(self.x_slots, self.blocks):
            for n in range(blocks * P // rows):
                sp.dma_start(slots[n * rows:(n + 1) * rows].rearrange("(p r) d -> p (r d)", p=P), zeros).then_inc(self.zeroed, 16)

    def load_weights(self, sp, arena, part):
        if part == 0:
            for n, name in enumerate(("w1", "w3")):
                sp.dma_start(arena[:, n * E * FF:(n + 1) * E * FF].rearrange("p (e f) -> p e f", e=E),
                             self.a[name].rearrange("e d f -> d e f")).then_inc(self.w13_loaded, 16)
        else:
            for e in range(E):
                sp.dma_start(arena[:, (2 * E + e) * FF:(2 * E + e + 1) * FF].rearrange("p (c d) -> p c d", c=FC),
                             self.a["w2"][e].rearrange("(c p) d -> p c d", p=P)).then_inc(self.w2_loaded, 16)

    def upper(self, act, arena, probs, n):
        if n == 0:
            act.wait_ge(self.w13_loaded, 16 * 2)
        at = slice(n * FF, (n + 1) * FF)
        act.activation(probs[:, at].bitcast(F32R), arena[:, at], ACT.Copy).then_inc(self.upper_made, 1)

    def lower(self, dve, arena, probs, n):
        dve.wait_ge(self.upper_made, n + 1)
        at = slice(n * FF, (n + 1) * FF)
        self.nc.vector.tensor_tensor(arena[:, at].bitcast(F32R), arena[:, at], probs[:, at], ALU.subtract).then_inc(self.lower_made, 1)

    def constants(self, pool):
        pool.iota(self.iota_i[:], [[-1, E]], base=E, channel_multiplier=0).then_inc(self.iota_made, 1)
        pool.iota(self.block_i[:], [[1, max(self.blocks)]], base=0, channel_multiplier=0).then_inc(self.iota_made, 1)
        pool.memset(self.earlier[:], 1.0).then_inc(self.made, 1)
        pool.memset(self.ones16[:], 1.0).then_inc(self.made, 1)
        pool.memset(self.ones_row[:], 1.0).then_inc(self.made, 1)
        pool.wait_ge(self.made, 3)
        pool.affine_select(out=self.earlier[:], in_=self.earlier[:], compare_op=ALU.is_ge, fill=0.0, base=-1,
                           pattern=[[1, P]], channel_multiplier=-1).then_inc(self.made, 1)

    def scatter(self, pool, c, count=None):
        t0, n = self.chunks[c]
        first = self.sent[c]
        self.sent[c] = TOP_K * n if count is None else min(first + count, TOP_K * n)
        if first == 0:
            pool.wait_ge(self.zeroed, 16 * self.N_ZERO)
            pool.wait_ge(self.slots_made, TOP_K * (c + 1))
        for at in range(first, self.sent[c]):
            tile, k = t0 + at // TOP_K, at % TOP_K
            pool.indirect_dma_start(
                out=self.x_slots[c], out_offset=bass.IndirectOffsetOnAxis(ap=self.slot[k][:, tile:tile + 1], axis=0),
                in_=self.x1[:, tile, :], in_offset=None).then_inc(self.scattered[c], 16)

    def exponentials(self, act, c):
        n = self.chunks[c][1]
        act.wait_ge(self.logits_shifted, c + 1)
        act.activation(self.wide["prob"][:, 0:n, :], self.wide["match"][:, 0:n, :], ACT.Exp).then_inc(self.exp_done, 1)

    def count_tiles(self, pe, c, bank):
        n = self.chunks[c][1]
        pe.wait_ge(self.made, 4)
        pe.wait_ge(self.chosen_made, c + 1)
        return pe.matmul(bank[:, 0:n * E], self.ones16[:], self.chosen[:, 0:n, :].rearrange("p n e -> p (n e)"), start=True, stop=True)

    def count_ranks(self, pe, c, bank):
        n = self.chunks[c][1]
        pe.wait_ge(self.chosen_made, c + 1)
        return pe.matmul(bank[:, 0:n * E], self.earlier[:], self.chosen[:, 0:n, :].rearrange("p n e -> p (n e)"), start=True, stop=True)

    def vector(self, dve, c, stage, bank=None, read=None, value=None):
        v = self.nc.vector

        def link(ins):
            self.links += 1
            ins.then_inc(self.linked, 1)
            dve.wait_ge(self.linked, self.links)

        t0, n = self.chunks[c]
        nb = self.blocks[c]
        prob, match, one_hot1, one_hot2 = (self.wide[x][:, 0:n, :] for x in ("prob", "match", "one_hot1", "one_hot2"))
        top, total, inverse, first_rank, prob1, prob2 = (self.thin[x][:, 0:n] for x in (
            "top", "total", "inverse", "first_rank", "prob1", "prob2"))
        filled, ends, starts = (self.few[x][:] for x in ("filled", "ends", "starts"))
        sums, ends_t = self.tile_sum[:, :, 0:n], self.tile_end[:, :, 0:n]
        per_tile = lambda x: x.rearrange("p (n o) -> p n o", o=1).to_broadcast([P, n, E])
        ranks = self.rank[:].rearrange("p (o e) -> p o e", o=1).to_broadcast([P, n, E])
        here = self.logits[:, t0:t0 + n, :]

        if stage == 0:
            if c == 0:
                dve.wait_ge(self.iota_made, 2)
                link(v.tensor_copy(self.rank[:], self.iota_i[:]))
                link(v.tensor_copy(self.block_no[:], self.block_i[:]))
            link(v.tensor_reduce(top, here, AX.X, ALU.max))
            v.tensor_tensor(match, here, per_tile(top), ALU.subtract).then_inc(self.logits_shifted, 1)
        elif stage == 1:
            dve.wait_ge(self.exp_done, c + 1)
            link(v.tensor_reduce(total, prob, AX.X, ALU.add))
            link(v.reciprocal(inverse, total))
            link(v.tensor_tensor(prob, prob, per_tile(inverse), ALU.mult))
        elif stage == 2:
            link(v.tensor_reduce(prob1, prob, AX.X, ALU.max))
            link(v.tensor_tensor(match, prob, per_tile(prob1), ALU.is_equal))
        elif stage == 3:
            link(v.tensor_tensor(match, match, ranks, ALU.mult))
            link(v.tensor_reduce(first_rank, match, AX.X, ALU.max))
        elif stage == 4:
            link(v.tensor_tensor(one_hot1, ranks, per_tile(first_rank), ALU.is_equal))
            link(v.scalar_tensor_tensor(out=prob, in0=one_hot1, scalar=-2.0, in1=prob, op0=ALU.mult, op1=ALU.add))
        elif stage == 5:
            link(v.tensor_reduce(prob2, prob, AX.X, ALU.max))
            link(v.tensor_tensor(match, prob, per_tile(prob2), ALU.is_equal))
        elif stage == 6:
            link(v.tensor_tensor(match, match, ranks, ALU.mult))
            link(v.tensor_reduce(first_rank, match, AX.X, ALU.max))
        elif stage == 7:
            link(v.tensor_tensor(one_hot2, ranks, per_tile(first_rank), ALU.is_equal))
            v.tensor_tensor(self.chosen[:, 0:n, :], one_hot1, one_hot2, ALU.add).then_inc(self.chosen_made, 1)
        elif stage == 8:
            link(v.tensor_tensor(total, prob1, prob2, ALU.add))
            link(v.reciprocal(inverse, total))
            link(v.tensor_tensor(self.weight[0][:, t0:t0 + n], prob1, inverse, ALU.mult))
            link(v.tensor_tensor(self.weight[1][:, t0:t0 + n], prob2, inverse, ALU.mult))
        elif stage == 9:
            v.tensor_copy(sums, bank[:, 0:n * E].rearrange("p (n e) -> p e n", e=E)).then_inc(read, 1)
            dve.wait_ge(read, value)
            for e in range(E):
                scan = v.tensor_tensor_scan(ends_t[:, e, :], self.ones_row[:, 0:n], sums[:, e, :], 0.0, ALU.mult, ALU.add)
                link(scan)
        elif stage == 10:
            link(v.tensor_scalar(self.few_i[:], ends_t[:, :, n - 1], float(P - 1), None, ALU.add))
            link(v.tensor_single_scalar(self.few_i[:], self.few_i[:], 7, ALU.logical_shift_right))
            link(v.tensor_copy(filled, self.few_i[:]))
            link(v.tensor_tensor_scan(ends, self.ones_row[:, 0:E], filled, 0.0, ALU.mult, ALU.add))
            link(v.tensor_tensor(starts, ends, filled, ALU.subtract))
            link(v.tensor_scalar(starts, starts, float(P), None, ALU.mult))
            link(v.tensor_tensor(ends_t, ends_t, sums, ALU.subtract))
            link(v.tensor_tensor(ends_t, ends_t, starts.rearrange("p (e o) -> p e o", o=1).to_broadcast([P, E, n]), ALU.add))
        elif stage == 11:
            v.tensor_tensor(match, bank[:, 0:n * E].rearrange("p (n e) -> p n e", e=E), ends_t.rearrange("p e n -> p n e"),
                            ALU.add).then_inc(read, 1)
            dve.wait_ge(read, value)
        elif stage in (12, 13):
            k = stage - 12
            link(v.tensor_tensor(prob, match, (one_hot1, one_hot2)[k], ALU.mult))
            link(v.tensor_reduce(first_rank, prob, AX.X, ALU.add))
            v.tensor_copy(self.slot[k][:, t0:t0 + n], first_rank).then_inc(self.slots_made, 1)
            dve.wait_ge(self.slots_made, TOP_K * c + k + 1)
        elif stage == 14:
            e_of, by = self.block_e[:, 0:nb], self.block_no[:, 0:nb]
            link(v.tensor_scalar(e_of, by, ends[0:1, 0:1], None, ALU.is_ge))
            for e in range(1, E - 1):
                link(v.scalar_tensor_tensor(out=e_of, in0=by, scalar=ends[0:1, e:e + 1], in1=e_of, op0=ALU.is_ge, op1=ALU.add))
            v.tensor_scalar(self.w_offset[:, self.first_block[c]:self.first_block[c] + nb], e_of, float(FF), None,
                            ALU.mult).then_inc(self.offsets_made, 1)


def attention(nc, ctx, a, x1, logits, arena, both_probs, routing, B):

    def sb(name, shape, dt=F32):
        return ctx.enter_context(nc.sbuf_tensor(name, shape, dt))

    def sem(name):
        return ctx.enter_context(nc.semaphore(name))

    stack_cols = H * S
    def stack(parity, which):
        n = stack_cols // 2
        at = (2 * parity + which) * n
        return arena[:, at:at + n].bitcast(BF16).rearrange("p (h t) -> p h t", h=H)
    q_stack = [stack(p, 0) for p in range(2)]
    k_stack = [stack(p, 1) for p in range(2)]

    wq, wk, wv, wo = (sb(n, [P, D]) for n in ("wq", "wk", "wv", "wo"))
    qk_bias = sb("qk_bias", [P, 2])
    v_bias = sb("v_bias", [P, D])
    o_bias = sb("o_bias", [P, D])
    gate_w = sb("gate_w", [P, 8])
    gate_bias = sb("gate_bias", [P, NT, 8])
    ident = sb("ident", [P, P])
    ident16 = sb("ident16", [P, P], BF16)
    above = sb("above", [P, NT, P], BF16)
    x_t = [sb(f"x_t{p}", [P, S]) for p in range(2)]
    qk = sb("qk", [P, 2, S])
    rest = sb("rest", [P, 2, S])
    part = [sb(f"part{n}", [P, 2, S], BF16) for n in range(PARTS)]
    v_aug = [sb(f"v_aug{p}", [P, NT, H, 16]) for p in range(2)]
    row_max = sb("row_max", [P, 2, NT, HALF])
    off_max = sb("off_max", [P, 2, NT - 1, HALF])
    max_rest = sb("max_rest", [P, NT, HALF])
    max_part = sb("max_part", [P, 2, NT, PARTS, HALF], BF16)
    max_rows = [sb(f"max_rows{h}", [PARTS * HALF, S], BF16) for h in range(2)]
    probs = [both_probs[:, p * GROUP * HEAD_P:(p + 1) * GROUP * HEAD_P] for p in range(2)]

    def probs_of(g, first, count):
        strip = lambda at, width: probs[g % 2][:, GROUP * at + first * width:GROUP * at + (first + count) * width]
        return strip(0, DIAG), strip(DIAG, LONG), strip(DIAG + LONG, SHORT)

    ctx_t = [sb(f"ctx_t{p}", [P, NG, S]) for p in range(2)]
    inv_sum = sb("inv_sum", [P, H])
    res = sb("res", [P, NT, D])
    stats = sb("stats", [P, NT, 6])
    mean_var = sb("mean_var", [P, NT, 2])
    var_eps = sb("var_eps", [P, NT])
    eps_col = sb("eps_col", [P, NT])
    minus_half = sb("minus_half", [P, NT])
    rstd = sb("rstd", [P, NT])
    ctx_n = sb("ctx_n", [P, NT, D])
    x1_now = ctx_n
    turned = sb("turned", [P, S])

    def bank(name):
        return ctx.enter_context(nc.psum_tensor(name, [P, S], F32))
    s_bank = [bank(f"s_bank{n}") for n in range(3)]
    t_bank = [bank(f"t_bank{n}") for n in range(3)]
    c_bank = bank("c_bank")
    m_bank = bank("m_bank")

    consts_loaded = sem("consts_loaded")
    made = sem("made")
    ones_made = sem("ones_made")
    x_t_loaded = [sem(f"x_t_loaded{p}") for p in range(2)]
    x_rows_loaded = sem("x_rows_loaded")
    stacked = [[sem(f"stacked{p}{h}") for h in range(2)] for p in range(2)]
    max_stacked = [sem(f"max_stacked{h}") for h in range(2)]
    s_ready = [sem(f"s_ready{n}") for n in range(3)]
    s_taken = [sem(f"s_taken{n}") for n in range(3)]
    t_ready = [sem(f"t_ready{n}") for n in range(3)]
    t_taken = [sem(f"t_taken{n}") for n in range(3)]
    c_ready = sem("c_ready")
    c_taken = sem("c_taken")
    m_ready = sem("m_ready")
    m_taken = sem("m_taken")
    masked = sem("masked")
    parts_written = [sem(f"parts_written{p}") for p in range(2)]
    part1_made = sem("part1_made")
    rest_made = sem("rest_made")
    part2_made = sem("part2_made")
    part3_made = sem("part3_made")
    max_split = sem("max_split")
    max_step = sem("max_step")
    max_reduced = sem("max_reduced")
    max_copied = sem("max_copied")
    x_plus_made = sem("x_plus_made")
    sums_inverted = sem("sums_inverted")
    x1_kept = sem("x1_kept")
    stats_made = sem("stats_made")
    mean_made = sem("mean_made")
    rstd_made = sem("rstd_made")
    var_eps_made = sem("var_eps_made")
    normed = sem("normed")

    CONSTS = ((wq, a["wq"]), (qk_bias, a["qk_bias"]), (wk, a["wk"]), (wv, a["wv"]), (wo, a["wo"]),
              (v_bias, a["v_bias"]), (o_bias, a["o_bias"]), (gate_w, a["gate_w"]), (gate_bias, a["gate_bias"]))
    scratch = nc.dram_tensor("parts", [2, 2, PARTS, HD, H, S], BF16, kind="Internal").ap()
    STACK_COPIES = [(q_stack, 0, PARTS * c, 0, PARTS) for c in range(PARTS)]
    for c in range(PARTS):
        STACK_COPIES.append((k_stack, 1, PARTS * c, c, PARTS - c))
        if c:
            STACK_COPIES.append((k_stack, 1, PARTS * (c + 1) - c, 0, c))
    M16 = m_bank[:, 0:S // 2].bitcast(BF16)

    def wait_stacks(eng, t, k, half):
        eng.wait_ge(stacked[t.parity(k)][half], 16 * len(STACK_COPIES) * (t.half(k) + 1))

    zeros = probs[1][:, 0:ZERO_COLS]
    ONES_FIRST, ONES = 1, 6

    with nc.Block() as block:

        @block.sync
        def _(sp):
            def body(t):
                if t.has(1):
                    if t.has(-1):
                        sp.wait_ge(m_ready, t.before().misc_count("v"))
                    sp.dma_start(x_t[t.parity(1)][:], a["x_t"][t.batch(1)]).then_inc(x_t_loaded[t.parity(1)], 16)
                if not t.steady and t.c == -1:
                    for tile, src in CONSTS:
                        sp.dma_start(tile[:], src).then_inc(consts_loaded, 16)
                if not t.steady and t.c in (-1, 0):
                    sp.wait_ge(ones_made, ONES_FIRST if t.c == -1 else ONES)
                if not t.steady and t.c == 0:
                    routing.zero_slots(sp, zeros)
                if t.has(1):
                    par = t.parity(1)
                    if t.has(-1):
                        for half in range(2):
                            wait_stacks(sp, t, -1, half)
                            sp.nop(nofuse=True)
                    for n, part_made in enumerate((part1_made, part2_made, part3_made)):
                        sp.wait_ge(part_made, t.batch(1) + 1)
                        for which in range(2):
                            sp.dma_start(scratch[par, which, n].rearrange("d h t -> h d t"),
                                         part[n][:, which, :]).then_inc(parts_written[par], 16)
                    sp.wait_ge(parts_written[par], 16 * 2 * PARTS * (t.half(1) + 1))
                    for half in range(2):
                        if t.has(-1):
                            sp.wait_ge(t_ready[2], (H // PAIR) * t.batch(-1) + (half + 1) * (HALF // PAIR))
                        for stacks, which, row, first, parts in STACK_COPIES:
                            heads = slice(half * HALF, (half + 1) * HALF)
                            sp.dma_start(
                                stacks[par][HD * row:HD * (row + parts), heads, :],
                                scratch[par, which, first:first + parts, :, heads, :].rearrange("n d h t -> (n d) h t"),
                            ).then_inc(stacked[par][half], 16)
                if t.has(-2):
                    sp.wait_ge(normed, NT * (t.batch(-2) + 1))
                    sp.dma_start(x1[:, bass.ds(NT * t.batch(-2), NT), :], x1_now[:]).then_inc(x1_kept, 16)
                if t.has(-1):
                    sp.dma_start(res[:], a["x_rows"][t.batch(-1)]).then_inc(x_rows_loaded, 16)

                if not t.steady and t.c == B:
                    routing.load_weights(sp, arena, 0)
                if not t.steady and t.c == B + 1:
                    sp.wait_ge(t_ready[2], (H // PAIR) * B)
                    routing.load_weights(sp, arena, 1)

            turns(sp, B, body)
            sp.wait_ge(x1_kept, 16 * B)

        @block.gpsimd
        def _(pool):
            routing.constants(pool)
            pool.memset(ident[:], 0.0).then_inc(made, 1)
            pool.memset(ident16[:], 0.0).then_inc(made, 1)
            pool.memset(above[:], 0.0).then_inc(made, 1)
            pool.memset(eps_col[:], EPS).then_inc(made, 1)
            pool.memset(minus_half[:], -0.5).then_inc(made, 1)
            pool.wait_ge(made, 5)
            for tile in (ident, ident16):
                pool.affine_select(out=tile[:], in_=tile[:], compare_op=ALU.not_equal, fill=1.0, base=0,
                                   pattern=[[-1, P]], channel_multiplier=1).then_inc(made, 1)
            pool.affine_select(out=above[:], in_=above[:], compare_op=ALU.is_ge, fill=MASKED, base=0,
                               pattern=[[0, NT], [-1, P]], channel_multiplier=1).then_inc(made, 1)

            def mask(t, k, h):
                pool.wait_ge(t_taken[0], H * t.batch(k) + h + 1)
                diagonal, _, _ = probs_of(h // GROUP, h % GROUP - 1, PAIR)
                blocks = diagonal.rearrange("p (b c) -> p b c", c=P)
                pool.nop(nofuse=True)
                pool.affine_select(out=blocks, in_=blocks, compare_op=ALU.is_ge, fill=0.0, base=0,
                                   pattern=[[0, PAIR * NT], [1, P]], channel_multiplier=-1).then_inc(masked, 1)

            def body(t):
                for s in range(H):
                    h, k = ((s - LAG) % H, 0 if s >= LAG else -1)
                    if (t.c, s) == (B - 2, SCATTER_SLOT):
                        pool.wait_ge(x1_kept, 16 * (B - LATE))
                    if (t.c, s) >= (B - 2, SCATTER_SLOT):
                        routing.scatter(pool, 0, SCATTERS[t.c - (B - 2)])
                    if s == 1 and t.has(-2):
                        pool.wait_ge(x_rows_loaded, 16 * (t.batch(-2) + 1))
                        pool.tensor_tensor(res[:], res[:], o_bias[:].rearrange("p (o d) -> p o d", o=1).to_broadcast([P, NT, D]),
                                           ALU.add).then_inc(x_plus_made, 1)
                    if s == 6 and t.has(1):
                        pool.wait_ge(part1_made, t.batch(1) + 1)
                        pool.tensor_tensor(rest[:], qk[:], part[0][:], ALU.subtract).then_inc(rest_made, 1)
                    if s == 8 and t.has(1):
                        pool.wait_ge(part2_made, t.batch(1) + 1)
                        pool.tensor_tensor(part[2][:], rest[:], part[1][:], ALU.subtract).then_inc(part3_made, 1)
                    if s == 9 and t.has(-2):
                        pool.wait_ge(mean_made, NT * (t.batch(-2) + 1))
                        if t.has(-3):
                            pool.wait_ge(normed, NT * (t.batch(-3) + 1))
                        pool.tensor_tensor(var_eps[:], mean_var[:, :, 1], eps_col[:], ALU.add).then_inc(var_eps_made, 1)
                        pool.wait_ge(var_eps_made, t.batch(-2) + 1)
                        pool.tensor_tensor(rstd[:], var_eps[:], minus_half[:], ALU.pow).then_inc(rstd_made, 1)
                    if h % PAIR == 1 and t.has(k):
                        mask(t, k, h)

            pool.wait_ge(consts_loaded, 16 * len(CONSTS))
            pool.wait_ge(made, 8)
            turns(pool, B, body)
            routing.scatter(pool, 0)

        @block.tensor
        def _(pe):
            pe.wait_ge(consts_loaded, 16 * len(CONSTS))

            def scores(t, h):
                par, b = t.parity(0), t.batch(0)
                first = not t.steady and t.c == 0 and h == 0
                if h % HALF == 0:
                    wait_stacks(pe, t, 0, h // HALF)
                q, k = q_stack[par][0:SPLIT_ROWS, h, :], k_stack[par][0:SPLIT_ROWS, h, :]

                def product(bank, at, n, first, blocks):
                    return pe.matmul(bank[:, at:at + blocks * P], q[:, n * P:(n + 1) * P], k[:, first * P:(first + blocks) * P],
                                     start=True, stop=True)

                if not first:
                    pe.wait_ge(s_taken[0], H * b + h)
                for n in range(NT):
                    pe.matmul(s_bank[0][:, n * P:(n + 1) * P], q[:, n * P:(n + 1) * P], k[:, n * P:(n + 1) * P],
                              start=(n == 0), stop=False, skip_group_check=True)
                pe.matmul(s_bank[0][:], ident16[:], above[:].rearrange("p n c -> p (n c)"), start=False, stop=True,
                          skip_group_check=True).then_inc(s_ready[0], 1)
                if not first:
                    pe.wait_ge(s_taken[1], H * b + h)
                product(s_bank[1], 0, 3, 0, 3)
                product(s_bank[1], 3 * P, 1, 0, 1).then_inc(s_ready[1], 1)
                if h % PAIR == 0:
                    if not first:
                        pe.wait_ge(s_taken[2], HALF * b + h // PAIR)
                    product(s_bank[2], 0, 2, 0, 2)
                else:
                    product(s_bank[2], SHORT, 2, 0, 2).then_inc(s_ready[2], 1)

            def scores_t(t, kk, h):
                par, b = t.parity(kk), t.batch(kk)
                first = not t.steady and t.c + kk == 0 and h == 0
                if h % HALF == 0:
                    pe.wait_ge(max_stacked[h // HALF], 16 * (b + 1))
                q, k = q_stack[par][0:STACK, h, :], k_stack[par][0:STACK, h, :]

                def product(bank, at, n, first, blocks):
                    return pe.matmul(bank[:, at:at + blocks * P], k[:, n * P:(n + 1) * P], q[:, first * P:(first + blocks) * P],
                                     start=True, stop=True)

                if not first:
                    pe.wait_ge(t_taken[0], H * b + h)
                for n in range(NT):
                    mm = product(t_bank[0], n * P, n, n, 1)
                mm.then_inc(t_ready[0], 1)
                if not first:
                    pe.wait_ge(t_taken[1], H * b + h)
                product(t_bank[1], 0, 0, 1, 3)
                product(t_bank[1], 3 * P, 2, 3, 1).then_inc(t_ready[1], 1)
                if h % PAIR == 0:
                    if not first:
                        pe.wait_ge(t_taken[2], HALF * b + h // PAIR)
                    product(t_bank[2], 0, 1, 2, 2)
                else:
                    product(t_bank[2], SHORT, 1, 2, 2).then_inc(t_ready[2], 1)

            def context(t, g, piece):
                b = t.batch(-1)
                if piece == 0:
                    pe.wait_ge(masked, (H // PAIR) * b + (GROUP // PAIR) * (g + 1))
                    pe.wait_ge(t_taken[2], (H // PAIR) * b + (GROUP // PAIR) * (g + 1))
                    if g > 0 or t.has(-2):
                        pe.wait_ge(c_taken, NG * b + g)
                    if g == 0:
                        pe.wait_ge(m_taken, t.before().misc_count("v"))
                diagonal, long, short = probs_of(g, 0, GROUP)
                runs = [[(long, LONG, 0, 0, 1, 3)],
                        [(short, SHORT, 0, 1, 2, 2), (long, LONG, 3 * P, 2, 3, 1)],
                        [(diagonal, DIAG, n * P, n, n, 1) for n in range(NT)]][piece]
                for strip, width, at, n, first, count in runs:
                    for j in range(GROUP):
                        mm = pe.matmul(c_bank[32 * j:32 * j + 16, first * P:(first + count) * P],
                                       v_aug[t.parity(-1)][:, n, GROUP * g + j, :],
                                       strip[:, j * width + at:j * width + at + count * P],
                                       start=(piece == 0), stop=(n == NT - 1), skip_group_check=True)
                if piece == 2:
                    mm.then_inc(c_ready, 1)

            def misc(t, name, k):
                count = t.misc_count(name)
                b = t.batch(k)
                if t.steady or count > 1:
                    pe.wait_ge(m_taken, count - 1)
                if name == "tiles":
                    mm = routing.count_tiles(pe, 0, m_bank)
                elif name == "ranks":
                    mm = routing.count_ranks(pe, 0, m_bank)
                elif name in ("q", "k"):
                    if name == "q":
                        pe.wait_ge(x_t_loaded[t.parity(k)], 16 * (t.half(k) + 1))
                    mm = pe.matmul(m_bank[:], (wq if name == "q" else wk)[:], x_t[t.parity(k)][:], start=True, stop=True)
                elif name == "v":
                    for n in range(NT):
                        mm = pe.matmul(m_bank[:, n * D:(n + 1) * D], x_t[t.parity(k)][:, n * P:(n + 1) * P], wv[:],
                                       start=True, stop=True)
                elif name in ("max0", "max1"):
                    half = int(name[-1])
                    pe.wait_ge(max_split, 2 * b + half + 1)
                    for n in range(NT):
                        mm = pe.transpose(M16[0:PARTS * HALF, n * P:(n + 1) * P],
                                          max_part[:, half, n, :, :].rearrange("p a h -> p (a h)"), ident16[:])
                elif name[:3] == "ctx":
                    n = int(name[-1])
                    if n == 0:
                        pe.wait_ge(c_taken, NG * (b + 1))
                    for g in range(NG):
                        mm = pe.transpose(m_bank[:, g * P:(g + 1) * P], ctx_t[t.parity(k)][:, g, n * P:(n + 1) * P], ident[:])
                elif name == "turn":
                    for n in range(NT):
                        mm = pe.transpose(m_bank[:, n * P:(n + 1) * P], ctx_n[:, n, :], ident[:])
                elif name == "out":
                    for n in range(NT):
                        mm = pe.matmul(m_bank[:, n * D:(n + 1) * D], turned[:, n * P:(n + 1) * P], wo[:],
                                       start=True, stop=True)
                elif name == "xturn":
                    pe.wait_ge(normed, NT * (b + 1))
                    for n in range(NT):
                        mm = pe.transpose(m_bank[:, n * P:(n + 1) * P], x1_now[:, n, :], ident[:])
                elif name == "gate":
                    for n in range(NT):
                        mm = pe.matmul(m_bank[:, n * 8:(n + 1) * 8], turned[:, n * P:(n + 1) * P], gate_w[:],
                                       start=True, stop=True)
                mm.then_inc(m_ready, 1)

            def body(t):
                if not t.steady and t.c == 0:
                    pe.wait_ge(made, 8)
                    pe.wait_ge(ones_made, ONES)
                for s in range(H):
                    if t.has(0):
                        scores(t, s)
                    kk = 0 if s >= LAG else -1
                    if t.has(kk):
                        scores_t(t, kk, (s - LAG) % H)
                    if s % GROUP > 0 and t.has(-1):
                        context(t, s // GROUP, s % GROUP - 1)
                    for slot, name, k in MISC:
                        if slot == s and t.has(k):
                            misc(t, name, k)

            turns(pe, B, body)

        @block.scalar
        def _(act):
            def exps(t, kk, h):
                b = t.batch(kk)
                diagonal, long, _ = probs_of(h // GROUP, h % GROUP, 1)
                if not t.steady and t.c + kk == 0 and h == GROUP:
                    act.wait_ge(routing.zeroed, 16 * routing.N_ZERO)
                if h % GROUP == 0 and (t.steady or NG * (t.c + kk) + h // GROUP >= 2):
                    act.wait_ge(c_ready, NG * b + h // GROUP - 1)
                act.wait_ge(t_ready[0], H * b + h + 1)
                act.activation(diagonal, t_bank[0][:], ACT.Exp, scale=SCALE).then_inc(t_taken[0], 1)

                act.wait_ge(t_ready[1], H * b + h + 1)
                act.activation(long, t_bank[1][:], ACT.Exp, scale=SCALE).then_inc(t_taken[1], 1)
                if h % PAIR == 1:
                    _, _, short = probs_of(h // GROUP, h % GROUP - 1, PAIR)
                    act.wait_ge(t_ready[2], HALF * b + h // PAIR + 1)
                    act.activation(short, t_bank[2][:], ACT.Exp, scale=SCALE).then_inc(t_taken[2], 1)

            def misc(t, name, k):
                count = t.misc_count(name)
                b = t.batch(k)
                if name in ("q", "k"):
                    which = int(name == "k")
                    act.wait_ge(m_ready, count)
                    if which == 0 and (t.steady or t.c + k > 0):
                        act.wait_ge(part3_made, b)
                    act.activation(qk[:, which, :], m_bank[:], ACT.Identity, bias=qk_bias[:, which:which + 1]).then_inc(m_taken, 1)
                elif name in ("max0", "max1"):
                    half = int(name[-1])
                    act.wait_ge(m_ready, count)
                    if t.steady or t.c + k > 0:
                        act.wait_ge(max_stacked[half], 16 * b)
                    act.activation(max_rows[half][:], M16[0:PARTS * HALF, 0:S], ACT.Copy).then_inc(m_taken, 1)
                    act.wait_ge(m_taken, count)
                    act.dma_start(
                        q_stack[t.parity(k)][SPLIT_ROWS:STACK, half * HALF:(half + 1) * HALF, :],
                        max_rows[half][:],
                    ).then_inc(max_stacked[half], 16)
                elif name == "turn":
                    act.wait_ge(m_ready, count)
                    act.activation(turned[:], m_bank[:], ACT.Copy).then_inc(m_taken, 1)
                elif name == "xturn":
                    act.wait_ge(m_ready, count)
                    act.activation(turned[:], m_bank[:], ACT.Copy).then_inc(m_taken, 1)

            def keep_context(t, k, g):
                act.wait_ge(c_ready, NG * t.batch(k) + g + 1)
                if g == 0 and t.has(-3):
                    act.wait_ge(m_taken, t.before().misc_count("ctx3"))
                act.activation(ctx_t[t.parity(k)][:, g, :], c_bank[:], ACT.Copy).then_inc(c_taken, 1)

            def body(t):
                for s in range(H):
                    if s == 1 and t.has(None):
                        routing.exponentials(act, 0)
                    if not t.steady and t.c == B + 1:
                        if s == 0:
                            act.wait_ge(c_ready, NG * B)
                        routing.upper(act, arena, both_probs, s)
                    if s == 0 and t.has(-2):
                        keep_context(t, -2, NG - 1)
                    if s % GROUP == 0 and s > 0 and t.has(-1):
                        keep_context(t, -1, s // GROUP - 1)
                    for slot, name, k in MISC:
                        if slot == s - 1 and t.has(k):
                            misc(t, name, k)
                    kk = 0 if s >= LAG else -1
                    if t.has(kk):
                        exps(t, kk, (s - LAG) % H)

            act.wait_ge(consts_loaded, 16 * len(CONSTS))
            turns(act, B, body)

        @block.vector
        def _(dve):
            def ones_below(parity):
                pairs = k_stack[parity][64:P, :, :].rearrange("p h t -> p (h t)").bitcast(F32)
                nc.vector.memset(pairs, ONES_16).then_inc(ones_made, 1)

            ones_below(0)
            dve.wait_ge(consts_loaded, 16 * len(CONSTS))

            def maxima(t, h):
                b = t.batch(0)
                half, hh = h // HALF, h % HALF
                if hh == 0 and (t.steady or t.c > 0):
                    dve.wait_ge(max_split, 2 * b + half - 1)
                off = lambda n: off_max[:, half, n - 1, hh:hh + 1]
                dve.wait_ge(s_ready[0], H * b + h + 1)
                nc.vector.tensor_reduce(row_max[:, half, :, hh], s_bank[0][:].rearrange("p (n c) -> p n c", n=NT), AX.X,
                                        ALU.max).then_inc(s_taken[0], 1)

                dve.wait_ge(s_ready[1], H * b + h + 1)
                nc.vector.tensor_reduce(off(3), s_bank[1][:, 0:3 * P], AX.X, ALU.max).then_inc(max_reduced, 1)
                nc.vector.tensor_reduce(off(1), s_bank[1][:, 3 * P:S], AX.X, ALU.max).then_inc(s_taken[1], 1)
                if h % PAIR == 1:
                    dve.wait_ge(s_ready[2], HALF * b + h // PAIR + 1)
                    nc.vector.tensor_reduce(off_max[:, half, 1, hh - 1:hh + 1],
                                            s_bank[2][:].rearrange("p (h c) -> p h c", h=PAIR), AX.X,
                                            ALU.max).then_inc(s_taken[2], 1)
                if hh == HALF - 1:
                    split_maxima(t, half)

            def split_maxima(t, half):
                b = t.batch(0)
                m = row_max[:, half, :, :]
                pieces = [max_part[:, half, :, n, :] for n in range(PARTS)]
                if t.steady or t.c > 0:
                    dve.wait_ge(m_ready, t.before().misc_count("max0") if half == 0 else t.misc_count("max1"))
                dve.wait_ge(s_taken[0], H * b + (half + 1) * HALF)
                dve.wait_ge(max_reduced, H * b + (half + 1) * HALF)
                dve.wait_ge(s_taken[1], H * b + (half + 1) * HALF)
                dve.wait_ge(s_taken[2], HALF * b + (half + 1) * (HALF // PAIR))
                step = 4 * (2 * b + half)
                nc.vector.tensor_tensor(m[:, 1:NT], m[:, 1:NT], off_max[:, half], ALU.max).then_inc(max_step, 1)
                dve.wait_ge(max_step, step + 1)
                nc.vector.tensor_scalar(pieces[0], m, -1.0, None, ALU.mult).then_inc(max_step, 1)
                dve.wait_ge(max_step, step + 2)
                nc.vector.scalar_tensor_tensor(out=max_rest[:], in0=m, scalar=-1.0, in1=pieces[0], op0=ALU.mult,
                                               op1=ALU.subtract).then_inc(max_step, 1)
                dve.wait_ge(max_step, step + 3)
                nc.vector.tensor_copy(pieces[1], max_rest[:]).then_inc(max_step, 1)
                dve.wait_ge(max_step, step + 4)
                nc.vector.tensor_tensor(pieces[2], max_rest[:], pieces[1], ALU.subtract).then_inc(max_split, 1)

            def misc(t, name, k):
                count = t.misc_count(name)
                b = t.batch(k)
                if name == "tiles":
                    dve.wait_ge(m_ready, count)
                    routing.vector(dve, 0, 9, m_bank, m_taken, count)
                elif name == "ranks":
                    dve.wait_ge(m_ready, count)
                    routing.vector(dve, 0, 11, m_bank, m_taken, count)
                elif name == "k":
                    dve.wait_ge(m_taken, count)
                    if t.steady or t.c + k > 0:
                        dve.wait_ge(parts_written[t.parity(k - 1)], 16 * 2 * PARTS * (t.half(k - 1) + 1))
                    nc.vector.tensor_copy(part[0][:], qk[:]).then_inc(part1_made, 1)
                elif name == "v":
                    dve.wait_ge(m_ready, count)
                    if t.steady or t.c + k >= 2:
                        dve.wait_ge(c_ready, NG * (b - 1))
                    for n in range(NT):
                        add = nc.vector.tensor_tensor(
                            v_aug[t.parity(k)][:, n, :, 0:HD], m_bank[:, n * D:(n + 1) * D].rearrange("p (h d) -> p h d", d=HD),
                            v_bias[:].rearrange("p (h d) -> p h d", d=HD), ALU.add)
                    add.then_inc(m_taken, 1)
                elif name[:3] == "ctx":
                    n = int(name[-1])
                    dve.wait_ge(m_ready, count)
                    if n == 0 and t.has(-3):
                        dve.wait_ge(m_taken, t.before().misc_count("xturn"))
                        dve.wait_ge(x1_kept, 16 * b)
                    strips = m_bank[:].rearrange("p (h c) -> p h c", h=H)
                    nc.vector.reciprocal(inv_sum[:], strips[:, :, SUM_COL]).then_inc(sums_inverted, 1)
                    dve.wait_ge(sums_inverted, NT * b + n + 1)
                    nc.vector.tensor_tensor(ctx_n[:, n, :].rearrange("p (h d) -> p h d", h=H), strips[:, :, 0:HD],
                                            inv_sum[:].rearrange("p (h o) -> p h o", o=1).to_broadcast([P, H, HD]),
                                            ALU.mult).then_inc(m_taken, 1)
                elif name == "out":
                    dve.wait_ge(m_ready, count)
                    dve.wait_ge(x_plus_made, b + 1)
                    nc.vector.tensor_tensor(res[:].rearrange("p n d -> p (n d)"), m_bank[:],
                                            res[:].rearrange("p n d -> p (n d)"), ALU.add).then_inc(m_taken, 1)
                    dve.wait_ge(m_taken, count)
                    nc.vector.bn_stats(stats[:, 0, :], res[:, 0, :]).then_inc(stats_made, 1)
                    for n in range(1, NT):
                        nc.vector.bn_stats(stats[:, n, :], res[:, n, :]).then_inc(stats_made, 1)
                    if t.steady or t.c + k > 0:
                        dve.wait_ge(rstd_made, b)
                    for n in range(NT):
                        dve.wait_ge(stats_made, NT * b + n + 1)
                        dve.nop(nofuse=True)
                        nc.vector.bn_aggr(mean_var[:, n, :], stats[:, n, :]).then_inc(mean_made, 1)
                elif name == "gate":
                    dve.wait_ge(m_ready, count)
                    nc.vector.tensor_tensor(logits[:, bass.ds(b * NT, NT), :],
                                            m_bank[:, 0:NT * 8].rearrange("p (n e) -> p n e", n=NT), gate_bias[:],
                                            ALU.add).then_inc(m_taken, 1)

            def normalise(t):
                b = t.batch(-2)
                dve.wait_ge(rstd_made, b + 1)
                dve.wait_ge(m_taken, t.misc_count("turn"))
                for n in range(NT):
                    nc.vector.tensor_scalar(x1_now[:, n, :], res[:, n, :], mean_var[:, n, 0:1], rstd[:, n:n + 1],
                                            ALU.subtract, ALU.mult).then_inc(normed, 1)

            def body(t):
                for s in range(H):
                    if not t.steady and (t.c, s) == (-1, 6):
                        for p in range(2):
                            nc.vector.memset(v_aug[p][:], 1.0).then_inc(ones_made, 1)
                        nc.vector.memset(c_bank[:], 0.0).then_inc(ones_made, 1)
                    if not t.steady and (t.c, s) == (-1, 8):
                        nc.vector.memset(zeros, 0.0).then_inc(ones_made, 1)
                        ones_below(1)
                        dve.wait_ge(ones_made, ONES)
                    for slot, name, k in MISC:
                        if slot == s - 1 and t.has(k):
                            misc(t, name, k)
                    if s == 7 and t.has(1):
                        dve.wait_ge(rest_made, t.batch(1) + 1)
                        nc.vector.tensor_copy(part[1][:], rest[:]).then_inc(part2_made, 1)
                    if s == 10 and t.has(-2):
                        normalise(t)
                    if not t.steady and t.c == B + 1:
                        routing.lower(dve, arena, both_probs, s)
                    if t.has(0):
                        maxima(t, s)
                    if t.has(None) and s < 9:
                        routing.vector(dve, 0, s)
                    if t.has(None) and s == 12:
                        routing.vector(dve, 0, 10)
                    if not t.steady and t.c == B - 2 and s < 3:
                        routing.vector(dve, 0, 12 + s)

            turns(dve, B, body)



class Step:

    def __init__(self, j, c, first, count, period=2, steady=False):
        self.j, self.c, self.first, self.count, self.period, self.steady = j, c, first, count, period, steady

    def has(self, k):
        return self.steady or self.first <= self.c + k < self.first + self.count

    def block(self, k=0):
        return self.j * self.period + (self.c + k)

    def rows(self, k):
        return bass.ds((self.j * self.period + (self.c + k - self.first)) * P, P)

    def parity(self, k=0):
        return (self.c + k) % 2

    def half(self, k=0):
        return self.j * (self.period // 2) + (self.c + k) // 2

    def later(self, k, n):
        return self.steady or self.c + k >= n


def steps(eng, first, count, body, beside=None, turns=None):
    period = PERIOD if beside else 2
    start = first + (4 if first else FIRST_STEPS)
    for c in range(first - 1, start):
        body(Step(0, c, first, count))
    peeled = 2 if beside else 0
    for j in range(peeled):
        for n in range(period):
            body(Step(0, start + j * period + n, first, count))
            beside(j, n)
    if not beside:
        turns = (first + count - 2 - start) // period
    with eng.Fori(peeled, turns) as j:
        for n in range(period):
            body(Step(j, start + n, first, count, period, steady=True))
            if beside:
                beside(j, n)
    for c in range(start + turns * period, first + count + 3):
        body(Step(0, c, first, count))


def experts(nc, ctx, x1, arena, probs, routing, out):

    def sb(name, shape, dt=F32):
        return ctx.enter_context(nc.sbuf_tensor(name, shape, dt))

    def sem(name):
        return ctx.enter_context(nc.semaphore(name))

    tiles, chunks, blocks, first_block, n_blocks = (
        routing.tiles, routing.chunks, routing.blocks, routing.first_block, routing.n_blocks)
    x_slots, y_slots, slot, weight, w_offset = routing.x_slots, routing.y_slots, routing.slot, routing.weight, routing.w_offset
    w1 = [half[:, 0:E * FF].bitcast(F32R) for half in (probs, arena)]
    w3 = [half[:, E * FF:2 * E * FF].bitcast(F32R) for half in (probs, arena)]
    w2 = arena[:, 2 * E * FF:3 * E * FF]
    ident = sb("identity", [P, P])

    x_in = [sb(f"x_in{p}", [P, D]) for p in range(2)]
    x_t = [[sb(f"x_in_t{p}_{half}", [P, P], F32R) for half in ("upper", "lower")] for p in range(2)]
    silu = [sb(f"silu{p}", [P, FF]) for p in range(2)]
    gated = [sb(f"gated{p}", [P, FF]) for p in range(2)]
    h_t = [sb(f"h_t{p}", [P, FC, P]) for p in range(2)]
    y_out = [sb(f"y_out{p}", [P, D]) for p in range(2)]

    picks = [sb(f"picks{p}", [P, CG, TOP_K, D]) for p in range(2)]
    part_sum = sb("part_sum", [P, CG, D])
    total_sum = [sb(f"total_sum{p}", [P, CG, D]) for p in range(2)]
    stats = sb("stats2", [P, CG, 6])
    mean_var = [sb(f"mean_var2{p}", [P, CG, 2]) for p in range(2)]
    var_eps = sb("var_eps2", [P, CG])
    eps_col = sb("eps_col2", [P, CG])
    minus_half = sb("minus_half2", [P, CG])
    rstd = [sb(f"rstd2{p}", [P, CG]) for p in range(2)]
    final = [sb(f"final{p}", [P, CG, D]) for p in range(2)]

    def bank(name):
        return ctx.enter_context(nc.psum_tensor(name, [P, S], F32))
    h1_bank = [bank(f"h1_bank{p}") for p in range(2)]
    h3_bank = [bank(f"h3_bank{p}") for p in range(2)]
    ht_bank = [bank(f"ht_bank{p}") for p in range(2)]
    xt_bank = bank("xt_bank")
    y_bank = bank("y_bank")

    made = sem("made2")
    tiles_counted = sem("tiles_counted")
    tiles_read = sem("tiles_read")
    ranks_counted = sem("ranks_counted")
    ranks_read = sem("ranks_read")
    x_loaded = [sem(f"x_loaded{p}") for p in range(2)]
    x_turned = sem("x_turned")
    xt_upper_made = sem("xt_upper_made")
    xt_lower_made = sem("xt_lower_made")
    h1_ready = sem("h1_ready")
    h3_ready = sem("h3_ready")
    silu_made = sem("silu_made")
    h_gated = sem("h_gated")
    ht_ready = sem("ht_ready")
    ht_copied = sem("ht_copied")
    y_ready = sem("y_ready")
    y_copied = sem("y_copied")
    y_stored = [sem(f"y_stored{p}") for p in range(2)]
    gathered = [sem(f"gathered{p}") for p in range(2)]
    summed = sem("summed")
    sum_step = sem("sum_step")
    stats_made = sem("stats_made2")
    mean_made = sem("mean_made2")
    var_eps_made = sem("var_eps_made2")
    rstd_made = sem("rstd_made2")
    final_made = sem("final_made")
    stored = [sem(f"stored{p}") for p in range(2)]

    n_groups = tiles // CG
    beside_turns = min((blocks[1] - 6) // PERIOD, chunks[0][1] // CG // 2)
    assert beside_turns > 1

    def is_number(j, n):
        return isinstance(j, int) and j == n

    def y_all_stored(eng, block):
        for p in range(2):
            eng.wait_ge(y_stored[p], 16 * ((block - p + 1) // 2))

    with nc.Block() as block:

        @block.sync
        def _(sp):
            out_g = out.rearrange("(g n p) d -> g p n d", n=CG, p=P)

            def store(j, p):
                sp.wait_ge(final_made, (j * 2 + (p + 1)) * CG)
                sp.dma_start(out_g[j * 2 + p], final[p][:]).then_inc(stored[p], 16)

            def store_beside(j, n):
                if n == PERIOD // 2 - 1 and not is_number(j, 0):
                    store(j - 1, 1)
                elif n == PERIOD - 1:
                    store(j, 0)

            for c, (_, n_tiles) in enumerate(chunks):
                sp.wait_ge(routing.scattered[c], 16 * TOP_K * n_tiles)

                def load(t, k):
                    sp.dma_start(x_in[t.parity(k)][:], x_slots[c][t.rows(k), :]).then_inc(x_loaded[t.parity(k)], 16)

                def body(t):
                    if t.c == t.first - 1 and not t.steady:
                        load(t, 1)
                        load(t, 2)
                    elif t.has(0) and (t.steady or t.has(2)):
                        sp.wait_ge(x_turned, t.block() + 1)
                        load(t, 2)
                    if t.has(-3):
                        sp.wait_ge(y_copied, t.block(-2))
                        sp.dma_start(y_slots[c][t.rows(-3), :], y_out[t.parity(-3)][:]).then_inc(y_stored[t.parity(-3)], 16)

                steps(sp, first_block[c], blocks[c], body, *((store_beside, beside_turns) if c else ()))

            with sp.Fori(beside_turns, n_groups // 2) as j:
                store(j - 1, 1)
                store(j, 0)
            store(n_groups // 2 - 1, 1)
            y_all_stored(sp, n_blocks)
            for p in range(2):
                sp.wait_ge(stored[p], 16 * (n_groups // 2))

        @block.gpsimd
        def _(pool):
            pool.memset(ident[:], 0.0).then_inc(made, 1)
            pool.memset(eps_col[:], EPS).then_inc(made, 1)
            pool.memset(minus_half[:], -0.5).then_inc(made, 1)
            pool.wait_ge(made, 3)
            pool.affine_select(out=ident[:], in_=ident[:], compare_op=ALU.not_equal, fill=1.0, base=0,
                               pattern=[[-1, P]], channel_multiplier=1).then_inc(made, 1)
            routing.scatter(pool, 1)

            def scale(g):
                p = g % 2
                pool.wait_ge(mean_made, CG * (g + 1))
                if g >= 1:
                    pool.wait_ge(rstd_made, g)
                pool.tensor_tensor(var_eps[:], mean_var[p][:, :, 1], eps_col[:], ALU.add).then_inc(var_eps_made, 1)
                pool.wait_ge(var_eps_made, g + 1)
                if g >= 2:
                    pool.wait_ge(final_made, CG * (g - 1))
                pool.tensor_tensor(rstd[p][:], var_eps[:], minus_half[:], ALU.pow).then_inc(rstd_made, 1)

            for c, (t0, n_tiles) in enumerate(chunks):
                y_all_stored(pool, first_block[c] + blocks[c])
                for g in range(t0 // CG, (t0 + n_tiles) // CG):
                    if g >= 2:
                        pool.wait_ge(summed, CG * (g - 1))
                    for n in range(CG):
                        for k in range(TOP_K):
                            pool.indirect_dma_start(
                                out=picks[g % 2][:, n, k, :], out_offset=None, in_=y_slots[c],
                                in_offset=bass.IndirectOffsetOnAxis(ap=slot[k][:, g * CG + n:g * CG + n + 1], axis=0),
                            ).then_inc(gathered[g % 2], 16)
                    if g >= 1:
                        scale(g - 1)
            scale(n_groups - 1)

        @block.vector
        def _(dve):
            v = nc.vector
            def body(t):
                if not t.steady:
                    for stage in ROUTING_STEPS.get(t.c, ()):
                        if stage == 9:
                            dve.wait_ge(tiles_counted, 1)
                            routing.vector(dve, 1, stage, xt_bank, tiles_read, 1)
                        elif stage == 11:
                            dve.wait_ge(ranks_counted, 1)
                            routing.vector(dve, 1, stage, xt_bank, ranks_read, 1)
                        else:
                            routing.vector(dve, 1, stage)
                if t.has(1):
                    dve.wait_ge(xt_upper_made, t.block(2))
                    upper, lower = x_t[t.parity(1)]
                    v.tensor_tensor(lower[:], xt_bank[:, 0:P], upper[:].bitcast(F32), ALU.subtract).then_inc(xt_lower_made, 1)
                if t.has(0):
                    dve.wait_ge(silu_made, t.block(1))
                    dve.wait_ge(h3_ready, t.block(1))
                    if t.later(0, 2):
                        dve.wait_ge(ht_ready, t.block(-1))
                    v.tensor_tensor(gated[t.parity()][:], silu[t.parity()][:], h3_bank[t.parity()][:], ALU.mult).then_inc(h_gated, 1)

            def combine(j, p):
                g = j * 2 + p
                dve.wait_ge(gathered[p], 16 * CG * TOP_K * (j + 1))
                for n in range(CG):
                    tile = g * CG + n
                    v.scalar_tensor_tensor(out=part_sum[:, n, :], in0=picks[p][:, n, 0, :], scalar=weight[0][:, bass.ds(tile, 1)],
                                           in1=x1[:, tile, :], op0=ALU.mult, op1=ALU.add).then_inc(sum_step, 1)
                for n in range(CG):
                    tile = g * CG + n
                    dve.wait_ge(sum_step, tile + 1)
                    v.scalar_tensor_tensor(out=total_sum[p][:, n, :], in0=picks[p][:, n, 1, :], scalar=weight[1][:, bass.ds(tile, 1)],
                                           in1=part_sum[:, n, :], op0=ALU.mult, op1=ALU.add).then_inc(summed, 1)
                for n in range(CG):
                    dve.wait_ge(summed, g * CG + n + 1)
                    v.bn_stats(stats[:, n, :], total_sum[p][:, n, :]).then_inc(stats_made, 1)
                for n in range(CG):
                    dve.wait_ge(stats_made, g * CG + n + 1)
                    dve.nop(nofuse=True)
                    v.bn_aggr(mean_var[p][:, n, :], stats[:, n, :]).then_inc(mean_made, 1)

            def normalise(j, p, former):
                g = j * 2 + p
                dve.wait_ge(rstd_made, g + 1)
                if former:
                    dve.wait_ge(stored[p], 16 * j)
                for n in range(CG):
                    v.tensor_scalar(final[p][:, n, :], total_sum[p][:, n, :], mean_var[p][:, n, 0:1], rstd[p][:, n:n + 1],
                                    ALU.subtract, ALU.mult).then_inc(final_made, 1)

            def combine_beside(j, n):
                if n == 0:
                    combine(j, 0)
                elif n == PERIOD // 2 - 1 and not is_number(j, 0):
                    normalise(j - 1, 1, not is_number(j, 1))
                elif n == PERIOD // 2:
                    combine(j, 1)
                elif n == PERIOD - 1:
                    normalise(j, 0, not is_number(j, 0))

            for c in range(len(chunks)):
                steps(dve, first_block[c], blocks[c], body, *((combine_beside, beside_turns) if c else ()))
            with dve.Fori(beside_turns, n_groups // 2) as j:
                combine(j, 0)
                normalise(j - 1, 1, True)
                combine(j, 1)
                normalise(j, 0, True)
            normalise(n_groups // 2 - 1, 1, True)

        @block.scalar
        def _(act):
            def body(t):
                if t.has(-3):
                    act.wait_ge(y_ready, t.block(-2))
                    if t.later(-3, 2):
                        act.wait_ge(y_stored[t.parity(-3)], 16 * t.half(-3))
                    act.activation(y_out[t.parity(-3)][:], y_bank[:, 0:D], ACT.Copy).then_inc(y_copied, 1)
                if t.has(-2):
                    act.wait_ge(ht_ready, t.block(-1))
                    if t.later(-2, 2):
                        act.wait_ge(y_ready, t.block(-3))
                    act.activation(h_t[t.parity(-2)][:].rearrange("p c t -> p (c t)"), ht_bank[t.parity(-2)][:], ACT.Copy).then_inc(ht_copied, 1)
                if t.has(1):
                    act.wait_ge(x_turned, t.block(2))
                    if t.later(1, 2):
                        act.wait_ge(h3_ready, t.block())
                    act.activation(x_t[t.parity(1)][0][:], xt_bank[:, 0:P], ACT.Copy).then_inc(xt_upper_made, 1)
                if not t.steady and t.c == 0:
                    routing.exponentials(act, 1)
                if t.has(0):
                    act.wait_ge(h1_ready, t.block(1))
                    if t.later(0, 2):
                        act.wait_ge(h_gated, t.block(-1))
                    act.activation(silu[t.parity()][:], h1_bank[t.parity()][:], ACT.Silu).then_inc(silu_made, 1)

            for c in range(len(chunks)):
                steps(act, first_block[c], blocks[c], body)

        @block.tensor
        def _(pe):
            pe.wait_ge(made, 4)
            pe.wait_ge(routing.offsets_made, 1)
            pe.wait_ge(routing.lower_made, 2 * E)
            pe.wait_ge(routing.w2_loaded, 16 * E)

            def offset(t, k):
                return nc.s_assert_within(
                    pe.value_load(w_offset[0:1, bass.ds(t.block(k), 1)]), 0, (E - 1) * FF,
                    skip_runtime_bounds_check_because="VectorE makes it as FF times a count of at most E - 1 comparisons")

            def product(bank, x, w, e):
                pairs = ((0, 0), (0, 1), (1, 0))
                for n, (of_x, of_w) in enumerate(pairs):
                    mm = pe.matmul(bank[:], x[of_x][:], w[of_w][:, bass.ds(e, FF)], start=(n == 0), stop=(n == len(pairs) - 1))
                return mm

            def body(t):
                p = t.parity()
                before = offset(t, -3) if t.has(-3) else None
                e = offset(t, 0) if t.has(0) else None
                if t.has(-3):
                    pe.wait_ge(ht_copied, t.block(-2))
                    for f in range(FC):
                        mm = pe.matmul(y_bank[:, 0:D], h_t[t.parity(-3)][:, f, :], w2[:, bass.ds(before + f * D, D)],
                                       start=(f == 0), stop=(f == FC - 1))
                    mm.then_inc(y_ready, 1)
                if t.has(-2):
                    pe.wait_ge(h_gated, t.block(-1))
                    for f in range(FC):
                        mm = pe.transpose(ht_bank[t.parity(-2)][:, f * P:(f + 1) * P], gated[t.parity(-2)][:, f * P:(f + 1) * P], ident[:])
                    mm.then_inc(ht_ready, 1)
                if t.has(1):
                    if t.later(1, 1):
                        pe.wait_ge(xt_lower_made, t.block(1))
                    if not t.steady and t.c == TILES_STEP:
                        routing.count_tiles(pe, 1, xt_bank).then_inc(tiles_counted, 1)
                        pe.wait_ge(tiles_read, 1)
                    if not t.steady and t.c == RANKS_STEP:
                        routing.count_ranks(pe, 1, xt_bank).then_inc(ranks_counted, 1)
                        pe.wait_ge(ranks_read, 1)
                    pe.wait_ge(x_loaded[t.parity(1)], 16 * (t.half(1) + 1))
                    pe.transpose(xt_bank[:, 0:P], x_in[t.parity(1)][:], ident[:]).then_inc(x_turned, 1)
                if t.has(0):
                    if not t.has(1):
                        pe.wait_ge(xt_lower_made, t.block(1))
                    product(h1_bank[p], x_t[p], w1, e).then_inc(h1_ready, 1)
                    product(h3_bank[p], x_t[p], w3, e).then_inc(h3_ready, 1)

            for c in range(len(chunks)):
                if c:
                    pe.wait_ge(routing.offsets_made, c + 1)
                steps(pe, first_block[c], blocks[c], body)


def build(nc, a, out, B):
    with ExitStack() as ctx:
        x1 = ctx.enter_context(nc.sbuf_tensor("x1", [P, NT * B, D], F32))
        logits = ctx.enter_context(nc.sbuf_tensor("logits", [P, NT * B, E], F32))
        arena = ctx.enter_context(nc.sbuf_tensor("arena", [P, 2 * H * S], F32))
        probs = ctx.enter_context(nc.sbuf_tensor("probs", [P, 2 * GROUP * HEAD_P], F32))
        routing = Routing(nc, ctx, a, logits, x1, B)
        with ExitStack() as own:
            attention(nc, own, a, x1, logits, arena, probs, routing, B)
        with ExitStack() as own:
            experts(nc, own, x1, arena, probs, routing, out)


def kernel(**inputs):
    import concourse.bacc as bacc
    import numpy as np
    from concourse.bass_utils import run_bass_kernel_spmd

    w = {name.split("_", 2)[2]: np.asarray(value) for name, value in inputs.items()}
    B = w["x"].shape[0]
    across = lambda v, n: np.ascontiguousarray(np.broadcast_to(v, (P, n, v.shape[0])))
    layouts = {
        "x_t": w["x"].transpose(0, 2, 1),
        "x_rows": w["x"].reshape(B, NT, P, D).transpose(0, 2, 1, 3),
        "wq": w["Wq"], "wk": w["Wk"], "wv": w["Wv"], "wo": w["Wo"],
        "qk_bias": np.stack([w["bq"], w["bk"]], 1),
        "v_bias": across(w["bv"], 1)[:, 0], "o_bias": across(w["bo"], 1)[:, 0],
        "gate_w": w["gate_w"], "gate_bias": across(w["gate_b"], NT),
        "w1": w["w1"], "w3": w["w3"], "w2": w["w2"],
    }
    layouts = {f"in_{name}": np.ascontiguousarray(value) for name, value in layouts.items()}
    nc = bacc.Bacc("TRN2", target_bir_lowering=False, num_devices=1)
    a = {name[3:]: nc.dram_tensor(name, v.shape, mybir.dt.from_np(v.dtype), kind="ExternalInput").ap()
         for name, v in layouts.items()}
    out = nc.dram_tensor("out", [B * S, D], F32, kind="ExternalOutput").ap()
    build(nc, a, out, B)
    r = run_bass_kernel_spmd(nc, [layouts], core_ids=[0])
    return r.results[0]["out"].reshape(B, S, D)
```

```python
from contextlib import ExitStack

import concourse.bass as bass
from concourse import mybir

F32 = mybir.dt.float32
F32R = mybir.dt.float32r
BF16 = mybir.dt.bfloat16
I32 = mybir.dt.int32
ALU = mybir.AluOpType
ACT = mybir.ActivationFunctionType
AX = mybir.AxisListType

P = 128
D = 128
H = 16
HD = D // H
S = 512
NT = S // P
EPS = 1e-5
SCALE = float(HD) ** -0.5
MASKED = -1.0e30
ONES_16 = 1.0 + 0x3F80 / 2**23
PARTS = 3
SPLIT_ROWS = PARTS * PARTS * HD
STACK = SPLIT_ROWS + PARTS
PAIR = 2
LAG = 12
HALF = H // 2
GROUP = 4
NG = H // GROUP
DIAG, LONG, SHORT = S, S, S // 2
HEAD_P = DIAG + LONG + SHORT
E = 8
TOP_K = 2
FF = 512
FC = FF // P
PERIOD = 6
FIRST_STEPS = 8
ROUTING_STEPS = {-1: (0,), 0: (1, 2), 1: (3, 4), 2: (5, 6), 3: (7, 8), 4: (9,), 5: (10,), 6: (11, 12), 7: (13, 14)}
TILES_STEP, RANKS_STEP = 4, 6
CG = 4
ZERO_COLS = 8 * D
ROUTING_SLOTS = {0: (0,), 1: (1, 2), 2: (3, 4), 3: (5, 6), 4: (7, 8), 6: (10,), 8: (12,), 9: (13,), 10: (14,)}
SCATTER_SLOT = 10
SCATTERS = ((2, 1), (2, 1), (2, 1), (1, 1), (1, 1))
UPPER_STEPS = {(0, 12 + n): (2 * n, 2 * n + 1) for n in range(4)} | {(1, n): (8 + n,) for n in range(8)}
LOWER_STEPS = {(0, 14 + n): (2 * n, 2 * n + 1) for n in range(2)} | {(1, n): (4 + n,) for n in range(12)}
SUM_COL = HD

MISC = [
    (0, "q", 1), (1, "max1", -1), (2, "k", 1), (3, "ctx0", -2), (4, "ctx1", -2), (5, "ctx2", -2),
    (5, "tiles", None), (6, "ranks", None), (7, "ctx3", -2), (8, "turn", -2), (9, "out", -2),
    (10, "max0", 0), (12, "v", 0), (13, "xturn", -2), (14, "gate", -2),
]
LATE = 5


class Turn:

    def __init__(self, j, c, B, steady=False):
        self.j, self.c, self.B, self.steady = j, c, B, steady

    def has(self, k):
        return k is not None if self.steady else self.among(self.c, k)

    def among(self, c, k):
        return c == self.B - 3 if k is None else 0 <= c + k < self.B

    def batch(self, k):
        return self.j * 2 + (self.c + (k or 0))

    def parity(self, k):
        return (self.c + k) % 2

    def half(self, k):
        return self.j + (self.c + k) // 2

    def before(self):
        return Turn(self.j, self.c - 1, self.B, self.steady)

    def misc_count(self, name):
        n = 0
        for i in range(-1, self.c + 1):
            for _, other, k in MISC:
                if self.among(i, k):
                    n += 1
                if i == self.c and other == name:
                    return self.j * (2 * sum(k is not None for _, _, k in MISC)) + n


def turns(eng, B, body):
    first = 3
    pairs = (B - 3 - first) // 2
    for c in range(-1, first):
        body(Turn(0, c, B))
    with eng.Fori(0, pairs) as j:
        for c in (first, first + 1):
            body(Turn(j, c, B, steady=True))
    for c in range(first + 2 * pairs, B + 2):
        body(Turn(0, c, B))


def most_blocks(tiles):
    return (TOP_K * tiles * P + E * (P - 1)) // P


class Routing:

    def __init__(self, nc, ctx, a, logits, x1, B):
        self.nc, self.a, self.logits, self.x1 = nc, a, logits, x1
        self.chunks = [(0, NT * (B - LATE)), (NT * (B - LATE), NT * LATE)]
        self.tiles = NT * B
        self.blocks = [most_blocks(n) for _, n in self.chunks]
        self.first_block = [0, self.blocks[0]]
        self.n_blocks = sum(self.blocks)
        most, wide_b = max(n for _, n in self.chunks), max(self.blocks)

        def sb(name, shape, dt=F32):
            return ctx.enter_context(nc.sbuf_tensor(name, shape, dt))

        def sem(name):
            return ctx.enter_context(nc.semaphore(name))

        self.x_slots, self.y_slots = (
            [nc.dram_tensor(f"{name}{c}", [n * P, D], F32, kind="Internal").ap() for c, n in enumerate(self.blocks)]
            for name in ("x_slots", "y_slots"))
        self.iota_i = sb("iota_i", [P, E], I32)
        self.rank = sb("rank", [P, E])
        self.block_i = sb("block_i", [1, wide_b], I32)
        self.block_no = sb("block_no", [1, wide_b])
        self.earlier = sb("earlier", [P, P], BF16)
        self.ones16 = sb("ones16", [P, P], BF16)
        self.ones_row = sb("ones_row", [P, most])
        self.wide = {n: sb(n, [P, most, E], dt) for n, dt in (("prob", F32), ("match", F32), ("one_hot1", BF16), ("one_hot2", BF16))}
        self.chosen = sb("chosen", [P, most, E], BF16)
        self.tile_sum = sb("tile_sum", [P, E, most])
        self.tile_end = sb("tile_end", [P, E, most])
        self.thin = {n: sb(n, [P, most]) for n in ("top", "total", "inverse", "first_rank", "prob1", "prob2")}
        self.weight = [sb(f"weight{k}", [P, self.tiles]) for k in range(TOP_K)]
        self.slot = [sb(f"slot{k}", [P, self.tiles], I32) for k in range(TOP_K)]
        self.few = {n: sb(n, [P, E]) for n in ("filled", "ends", "starts")}
        self.few_i = sb("few_i", [P, E], I32)
        self.block_e = sb("block_e", [1, wide_b])
        self.w_offset = sb("w_offset", [1, self.n_blocks], I32)

        self.w13_loaded = sem("w13_loaded")
        self.w2_loaded = sem("w2_loaded")
        self.upper_made = sem("upper_made")
        self.lower_made = sem("lower_made")
        self.zeroed = sem("zeroed")
        self.made = sem("routing_made")
        self.iota_made = sem("iota_made")
        self.linked = sem("linked")
        self.logits_shifted = sem("logits_shifted")
        self.exp_done = sem("exp_done")
        self.chosen_made = sem("chosen_made")
        self.slots_made = sem("slots_made")
        self.offsets_made = sem("offsets_made")
        self.scattered = [sem(f"scattered{c}") for c in range(len(self.chunks))]
        self.links = 0
        self.sent = [0, 0]
        unit = ZERO_COLS // D
        self.zero_runs = [(c, at, min(unit, n - at)) for c, n in enumerate(self.blocks) for at in range(0, n, unit)]
        self.N_ZERO = len(self.zero_runs)

    def zero_slots(self, sp, zeros):
        for c, at, n in self.zero_runs:
            sp.dma_start(self.x_slots[c][at * P:(at + n) * P].rearrange("(p r) d -> p (r d)", p=P), zeros[:, 0:n * D]).then_inc(self.zeroed, 16)

    def load_weights(self, sp, arena, part):
        if part == 0:
            for n, name in enumerate(("w1", "w3")):
                sp.dma_start(arena[:, n * E * FF:(n + 1) * E * FF].rearrange("p (e f) -> p e f", e=E),
                             self.a[name].rearrange("e d f -> d e f")).then_inc(self.w13_loaded, 16)
        else:
            for e in range(E):
                sp.dma_start(arena[:, (2 * E + e) * FF:(2 * E + e + 1) * FF].rearrange("p (c d) -> p c d", c=FC),
                             self.a["w2"][e].rearrange("(c p) d -> p c d", p=P)).then_inc(self.w2_loaded, 16)

    def upper(self, act, arena, probs, n):
        if n == 0:
            act.wait_ge(self.w13_loaded, 16 * 2)
        at = slice(n * FF, (n + 1) * FF)
        act.activation(probs[:, at].bitcast(F32R), arena[:, at], ACT.Copy).then_inc(self.upper_made, 1)

    def lower(self, dve, arena, probs, n):
        dve.wait_ge(self.upper_made, n + 1)
        at = slice(n * FF, (n + 1) * FF)
        self.nc.vector.tensor_tensor(arena[:, at].bitcast(F32R), arena[:, at], probs[:, at], ALU.subtract).then_inc(self.lower_made, 1)

    def constants(self, pool):
        pool.iota(self.iota_i[:], [[-1, E]], base=E, channel_multiplier=0).then_inc(self.iota_made, 1)
        pool.iota(self.block_i[:], [[1, max(self.blocks)]], base=0, channel_multiplier=0).then_inc(self.iota_made, 1)
        pool.memset(self.earlier[:], 1.0).then_inc(self.made, 1)
        pool.memset(self.ones16[:], 1.0).then_inc(self.made, 1)
        pool.memset(self.ones_row[:], 1.0).then_inc(self.made, 1)
        pool.wait_ge(self.made, 3)
        pool.affine_select(out=self.earlier[:], in_=self.earlier[:], compare_op=ALU.is_ge, fill=0.0, base=-1,
                           pattern=[[1, P]], channel_multiplier=-1).then_inc(self.made, 1)

    def scatter(self, pool, c, count=None):
        t0, n = self.chunks[c]
        first = self.sent[c]
        self.sent[c] = TOP_K * n if count is None else min(first + count, TOP_K * n)
        if first == 0:
            pool.wait_ge(self.zeroed, 16 * self.N_ZERO)
            pool.wait_ge(self.slots_made, TOP_K * (c + 1))
        for at in range(first, self.sent[c]):
            tile, k = t0 + at // TOP_K, at % TOP_K
            pool.indirect_dma_start(
                out=self.x_slots[c], out_offset=bass.IndirectOffsetOnAxis(ap=self.slot[k][:, tile:tile + 1], axis=0),
                in_=self.x1[:, tile, :], in_offset=None).then_inc(self.scattered[c], 16)

    def exponentials(self, act, c):
        n = self.chunks[c][1]
        act.wait_ge(self.logits_shifted, c + 1)
        act.activation(self.wide["prob"][:, 0:n, :], self.wide["match"][:, 0:n, :], ACT.Exp).then_inc(self.exp_done, 1)

    def count_tiles(self, pe, c, bank):
        n = self.chunks[c][1]
        pe.wait_ge(self.made, 4)
        pe.wait_ge(self.chosen_made, c + 1)
        return pe.matmul(bank[:, 0:n * E], self.ones16[:], self.chosen[:, 0:n, :].rearrange("p n e -> p (n e)"), start=True, stop=True)

    def count_ranks(self, pe, c, bank):
        n = self.chunks[c][1]
        pe.wait_ge(self.chosen_made, c + 1)
        return pe.matmul(bank[:, 0:n * E], self.earlier[:], self.chosen[:, 0:n, :].rearrange("p n e -> p (n e)"), start=True, stop=True)

    def vector(self, dve, c, stage, bank=None, read=None, value=None):
        v = self.nc.vector

        def link(ins):
            self.links += 1
            ins.then_inc(self.linked, 1)
            dve.wait_ge(self.linked, self.links)

        t0, n = self.chunks[c]
        nb = self.blocks[c]
        prob, match, one_hot1, one_hot2 = (self.wide[x][:, 0:n, :] for x in ("prob", "match", "one_hot1", "one_hot2"))
        top, total, inverse, first_rank, prob1, prob2 = (self.thin[x][:, 0:n] for x in (
            "top", "total", "inverse", "first_rank", "prob1", "prob2"))
        filled, ends, starts = (self.few[x][:] for x in ("filled", "ends", "starts"))
        sums, ends_t = self.tile_sum[:, :, 0:n], self.tile_end[:, :, 0:n]
        per_tile = lambda x: x.rearrange("p (n o) -> p n o", o=1).to_broadcast([P, n, E])
        ranks = self.rank[:].rearrange("p (o e) -> p o e", o=1).to_broadcast([P, n, E])
        here = self.logits[:, t0:t0 + n, :]

        if stage == 0:
            if c == 0:
                dve.wait_ge(self.iota_made, 2)
                link(v.tensor_copy(self.rank[:], self.iota_i[:]))
                link(v.tensor_copy(self.block_no[:], self.block_i[:]))
            link(v.tensor_reduce(top, here, AX.X, ALU.max))
            v.tensor_tensor(match, here, per_tile(top), ALU.subtract).then_inc(self.logits_shifted, 1)
        elif stage == 1:
            dve.wait_ge(self.exp_done, c + 1)
            link(v.tensor_reduce(total, prob, AX.X, ALU.add))
            link(v.reciprocal(inverse, total))
            link(v.tensor_tensor(prob, prob, per_tile(inverse), ALU.mult))
        elif stage == 2:
            link(v.tensor_reduce(prob1, prob, AX.X, ALU.max))
            link(v.tensor_tensor(match, prob, per_tile(prob1), ALU.is_equal))
        elif stage == 3:
            link(v.tensor_tensor(match, match, ranks, ALU.mult))
            link(v.tensor_reduce(first_rank, match, AX.X, ALU.max))
        elif stage == 4:
            link(v.tensor_tensor(one_hot1, ranks, per_tile(first_rank), ALU.is_equal))
            link(v.scalar_tensor_tensor(out=prob, in0=one_hot1, scalar=-2.0, in1=prob, op0=ALU.mult, op1=ALU.add))
        elif stage == 5:
            link(v.tensor_reduce(prob2, prob, AX.X, ALU.max))
            link(v.tensor_tensor(match, prob, per_tile(prob2), ALU.is_equal))
        elif stage == 6:
            link(v.tensor_tensor(match, match, ranks, ALU.mult))
            link(v.tensor_reduce(first_rank, match, AX.X, ALU.max))
        elif stage == 7:
            link(v.tensor_tensor(one_hot2, ranks, per_tile(first_rank), ALU.is_equal))
            v.tensor_tensor(self.chosen[:, 0:n, :], one_hot1, one_hot2, ALU.add).then_inc(self.chosen_made, 1)
        elif stage == 8:
            link(v.tensor_tensor(total, prob1, prob2, ALU.add))
            link(v.reciprocal(inverse, total))
            link(v.tensor_tensor(self.weight[0][:, t0:t0 + n], prob1, inverse, ALU.mult))
            link(v.tensor_tensor(self.weight[1][:, t0:t0 + n], prob2, inverse, ALU.mult))
        elif stage == 9:
            v.tensor_copy(sums, bank[:, 0:n * E].rearrange("p (n e) -> p e n", e=E)).then_inc(read, 1)
            dve.wait_ge(read, value)
            for e in range(E):
                scan = v.tensor_tensor_scan(ends_t[:, e, :], self.ones_row[:, 0:n], sums[:, e, :], 0.0, ALU.mult, ALU.add)
                link(scan)
        elif stage == 10:
            link(v.tensor_scalar(self.few_i[:], ends_t[:, :, n - 1], float(P - 1), None, ALU.add))
            link(v.tensor_single_scalar(self.few_i[:], self.few_i[:], 7, ALU.logical_shift_right))
            link(v.tensor_copy(filled, self.few_i[:]))
            link(v.tensor_tensor_scan(ends, self.ones_row[:, 0:E], filled, 0.0, ALU.mult, ALU.add))
            link(v.tensor_tensor(starts, ends, filled, ALU.subtract))
            link(v.tensor_scalar(starts, starts, float(P), None, ALU.mult))
            link(v.tensor_tensor(ends_t, ends_t, sums, ALU.subtract))
            link(v.tensor_tensor(ends_t, ends_t, starts.rearrange("p (e o) -> p e o", o=1).to_broadcast([P, E, n]), ALU.add))
        elif stage == 11:
            v.tensor_tensor(match, bank[:, 0:n * E].rearrange("p (n e) -> p n e", e=E), ends_t.rearrange("p e n -> p n e"),
                            ALU.add).then_inc(read, 1)
            dve.wait_ge(read, value)
        elif stage in (12, 13):
            k = stage - 12
            link(v.tensor_tensor(prob, match, (one_hot1, one_hot2)[k], ALU.mult))
            link(v.tensor_reduce(first_rank, prob, AX.X, ALU.add))
            v.tensor_copy(self.slot[k][:, t0:t0 + n], first_rank).then_inc(self.slots_made, 1)
            dve.wait_ge(self.slots_made, TOP_K * c + k + 1)
        elif stage == 14:
            e_of, by = self.block_e[:, 0:nb], self.block_no[:, 0:nb]
            link(v.tensor_scalar(e_of, by, ends[0:1, 0:1], None, ALU.is_ge))
            for e in range(1, E - 1):
                link(v.scalar_tensor_tensor(out=e_of, in0=by, scalar=ends[0:1, e:e + 1], in1=e_of, op0=ALU.is_ge, op1=ALU.add))
            v.tensor_scalar(self.w_offset[:, self.first_block[c]:self.first_block[c] + nb], e_of, float(FF), None,
                            ALU.mult).then_inc(self.offsets_made, 1)


def attention(nc, ctx, a, x1, logits, arena, both_probs, routing, B):

    def sb(name, shape, dt=F32):
        return ctx.enter_context(nc.sbuf_tensor(name, shape, dt))

    def sem(name):
        return ctx.enter_context(nc.semaphore(name))

    stack_cols = H * S
    def stack(parity, which):
        n = stack_cols // 2
        at = (2 * parity + which) * n
        return arena[:, at:at + n].bitcast(BF16).rearrange("p (h t) -> p h t", h=H)
    q_stack = [stack(p, 0) for p in range(2)]
    k_stack = [stack(p, 1) for p in range(2)]

    wq, wk, wv, wo = (sb(n, [P, D]) for n in ("wq", "wk", "wv", "wo"))
    qk_bias = sb("qk_bias", [P, 2])
    v_bias = sb("v_bias", [P, D])
    o_bias = sb("o_bias", [P, D])
    gate_w = sb("gate_w", [P, 8])
    gate_bias = sb("gate_bias", [P, NT, 8])
    ident = sb("ident", [P, P])
    ident16 = sb("ident16", [P, P], BF16)
    above = sb("above", [P, NT, P], BF16)
    x_t = [sb(f"x_t{p}", [P, S]) for p in range(2)]
    qk = sb("qk", [P, 2, S])
    rest = sb("rest", [P, 2, S])
    part = [sb(f"part{n}", [P, 2, S], BF16) for n in range(PARTS)]
    v_aug = [sb(f"v_aug{p}", [P, NT, H, 16]) for p in range(2)]
    row_max = sb("row_max", [P, 2, NT, HALF])
    off_max = sb("off_max", [P, 2, NT - 1, HALF])
    max_rest = sb("max_rest", [P, NT, HALF])
    max_part = sb("max_part", [P, 2, NT, PARTS, HALF], BF16)
    max_rows = [sb(f"max_rows{h}", [PARTS * HALF, S], BF16) for h in range(2)]
    probs = [both_probs[:, p * GROUP * HEAD_P:(p + 1) * GROUP * HEAD_P] for p in range(2)]

    def probs_of(g, first, count):
        strip = lambda at, width: probs[g % 2][:, GROUP * at + first * width:GROUP * at + (first + count) * width]
        return strip(0, DIAG), strip(DIAG, LONG), strip(DIAG + LONG, SHORT)

    ctx_t = [sb(f"ctx_t{p}", [P, NG, S]) for p in range(2)]
    inv_sum = sb("inv_sum", [P, H])
    res = sb("res", [P, NT, D])
    stats = sb("stats", [P, NT, 6])
    mean_var = sb("mean_var", [P, NT, 2])
    var_eps = sb("var_eps", [P, NT])
    eps_col = sb("eps_col", [P, NT])
    minus_half = sb("minus_half", [P, NT])
    minus_one = sb("minus_one", [P, NT])
    rstd = sb("rstd", [P, NT])
    shift = sb("shift", [P, NT])
    ctx_n = sb("ctx_n", [P, NT, D])
    x1_now = ctx_n
    turned = sb("turned", [P, S])

    def bank(name):
        return ctx.enter_context(nc.psum_tensor(name, [P, S], F32))
    s_bank = [bank(f"s_bank{n}") for n in range(3)]
    t_bank = [bank(f"t_bank{n}") for n in range(3)]
    c_bank = bank("c_bank")
    m_bank = bank("m_bank")

    first_consts_loaded = sem("first_consts_loaded")
    consts_loaded = sem("consts_loaded")
    made = sem("made")
    ones_made = sem("ones_made")
    x_t_loaded = [sem(f"x_t_loaded{p}") for p in range(2)]
    x_rows_loaded = sem("x_rows_loaded")
    stacked = [[sem(f"stacked{p}{h}") for h in range(2)] for p in range(2)]
    max_stacked = [sem(f"max_stacked{h}") for h in range(2)]
    s_ready = [sem(f"s_ready{n}") for n in range(3)]
    s_taken = [sem(f"s_taken{n}") for n in range(3)]
    t_ready = [sem(f"t_ready{n}") for n in range(3)]
    t_taken = [sem(f"t_taken{n}") for n in range(3)]
    c_ready = sem("c_ready")
    c_taken = sem("c_taken")
    m_ready = sem("m_ready")
    m_taken = sem("m_taken")
    masked = sem("masked")
    parts_written = [sem(f"parts_written{p}") for p in range(2)]
    part1_made = sem("part1_made")
    rest_made = sem("rest_made")
    part2_made = sem("part2_made")
    part3_made = sem("part3_made")
    max_split = sem("max_split")
    max_step = sem("max_step")
    max_reduced = sem("max_reduced")
    max_copied = sem("max_copied")
    x_plus_made = sem("x_plus_made")
    sums_inverted = sem("sums_inverted")
    x1_kept = sem("x1_kept")
    stats_made = sem("stats_made")
    mean_made = sem("mean_made")
    rstd_made = sem("rstd_made")
    var_eps_made = sem("var_eps_made")
    mean_negated = sem("mean_negated")
    shift_made = sem("shift_made")
    normed = sem("normed")

    FIRST_CONSTS = ((wq, a["wq"]), (qk_bias, a["qk_bias"]), (wk, a["wk"]))
    CONSTS = ((wv, a["wv"]), (wo, a["wo"]), (v_bias, a["v_bias"]),
              (o_bias, a["o_bias"]), (gate_w, a["gate_w"]), (gate_bias, a["gate_bias"]))
    scratch = nc.dram_tensor("parts", [2, 2, PARTS, HD, H, S], BF16, kind="Internal").ap()
    STACK_COPIES = [(q_stack, 0, PARTS * c, 0, PARTS) for c in range(PARTS)]
    for c in range(PARTS):
        STACK_COPIES.append((k_stack, 1, PARTS * c, c, PARTS - c))
        if c:
            STACK_COPIES.append((k_stack, 1, PARTS * (c + 1) - c, 0, c))
    M16 = m_bank[:, 0:S // 2].bitcast(BF16)

    def wait_stacks(eng, t, k, half):
        eng.wait_ge(stacked[t.parity(k)][half], 16 * len(STACK_COPIES) * (t.half(k) + 1))

    def find_rest(eng, t):
        eng.wait_ge(part1_made, t.batch(1) + 1)
        eng.tensor_tensor(rest[:], qk[:], part[0][:], ALU.subtract).then_inc(rest_made, 1)

    def find_last_part(eng, t):
        eng.wait_ge(part2_made, t.batch(1) + 1)
        eng.tensor_tensor(part[2][:], rest[:], part[1][:], ALU.subtract).then_inc(part3_made, 1)

    zeros = probs[1][:, 0:ZERO_COLS]
    ONES_FIRST, ONES = 1, 6

    with nc.Block() as block:

        @block.sync
        def _(sp):
            def body(t):
                if t.c in (B, B + 1):
                    sp.wait_ge(t_ready[2], (H // PAIR) * (t.c - 1))
                    routing.load_weights(sp, arena, t.c - B)
                if t.has(1):
                    if t.has(-1):
                        sp.wait_ge(m_ready, t.before().misc_count("v"))
                    sp.dma_start(x_t[t.parity(1)][:], a["x_t"][t.batch(1)]).then_inc(x_t_loaded[t.parity(1)], 16)
                if not t.steady and t.c == -1:
                    for tile, src in FIRST_CONSTS:
                        sp.dma_start(tile[:], src).then_inc(first_consts_loaded, 16)
                    for tile, src in CONSTS:
                        sp.dma_start(tile[:], src).then_inc(consts_loaded, 16)
                if not t.steady and t.c in (-1, 0):
                    sp.wait_ge(ones_made, ONES_FIRST if t.c == -1 else ONES)
                if not t.steady and t.c == 0:
                    routing.zero_slots(sp, zeros)
                if t.has(1):
                    par = t.parity(1)
                    if t.has(-1):
                        for half in range(2):
                            wait_stacks(sp, t, -1, half)
                            sp.nop(nofuse=True)
                    for n, part_made in enumerate((part1_made, part2_made, part3_made)):
                        sp.wait_ge(part_made, t.batch(1) + 1)
                        for which in range(2):
                            sp.dma_start(scratch[par, which, n].rearrange("d h t -> h d t"),
                                         part[n][:, which, :]).then_inc(parts_written[par], 16)
                    sp.wait_ge(parts_written[par], 16 * 2 * PARTS * (t.half(1) + 1))
                    for half in range(2):
                        if t.has(-1):
                            sp.wait_ge(t_ready[2], (H // PAIR) * t.batch(-1) + (half + 1) * (HALF // PAIR))
                        for stacks, which, row, first, parts in STACK_COPIES:
                            heads = slice(half * HALF, (half + 1) * HALF)
                            sp.dma_start(
                                stacks[par][HD * row:HD * (row + parts), heads, :],
                                scratch[par, which, first:first + parts, :, heads, :].rearrange("n d h t -> (n d) h t"),
                            ).then_inc(stacked[par][half], 16)
                if t.has(-2):
                    sp.wait_ge(normed, NT * (t.batch(-2) + 1))
                    sp.dma_start(x1[:, bass.ds(NT * t.batch(-2), NT), :], x1_now[:]).then_inc(x1_kept, 16)
                if t.has(-1):
                    sp.dma_start(res[:], a["x_rows"][t.batch(-1)]).then_inc(x_rows_loaded, 16)


            turns(sp, B, body)
            sp.wait_ge(x1_kept, 16 * B)

        @block.gpsimd
        def _(pool):
            routing.constants(pool)
            pool.memset(ident[:], 0.0).then_inc(made, 1)
            pool.memset(ident16[:], 0.0).then_inc(made, 1)
            pool.memset(above[:], 0.0).then_inc(made, 1)
            pool.memset(eps_col[:], EPS).then_inc(made, 1)
            pool.memset(minus_half[:], -0.5).then_inc(made, 1)
            pool.memset(minus_one[:], -1.0).then_inc(made, 1)
            pool.wait_ge(made, 6)
            for tile in (ident, ident16):
                pool.affine_select(out=tile[:], in_=tile[:], compare_op=ALU.not_equal, fill=1.0, base=0,
                                   pattern=[[-1, P]], channel_multiplier=1).then_inc(made, 1)
            pool.affine_select(out=above[:], in_=above[:], compare_op=ALU.is_ge, fill=MASKED, base=0,
                               pattern=[[0, NT], [-1, P]], channel_multiplier=1).then_inc(made, 1)

            def mask(t, k, h):
                pool.wait_ge(t_taken[0], H * t.batch(k) + h + 1)
                diagonal, _, _ = probs_of(h // GROUP, h % GROUP - 1, PAIR)
                blocks = diagonal.rearrange("p (b c) -> p b c", c=P)
                pool.nop(nofuse=True)
                pool.affine_select(out=blocks, in_=blocks, compare_op=ALU.is_ge, fill=0.0, base=0,
                                   pattern=[[0, PAIR * NT], [1, P]], channel_multiplier=-1).then_inc(masked, 1)

            def body(t):
                for s in range(H):
                    h, k = ((s - LAG) % H, 0 if s >= LAG else -1)
                    if (t.c, s) == (B - 3, SCATTER_SLOT):
                        pool.wait_ge(x1_kept, 16 * (B - LATE))
                    if not t.steady and (t.c, s) >= (B - 3, SCATTER_SLOT):
                        routing.scatter(pool, 0, SCATTERS[t.c - (B - 3)][s % 2])
                    if s == 1 and t.has(-2):
                        pool.wait_ge(x_rows_loaded, 16 * (t.batch(-2) + 1))
                        pool.tensor_tensor(res[:], res[:], o_bias[:].rearrange("p (o d) -> p o d", o=1).to_broadcast([P, NT, D]),
                                           ALU.add).then_inc(x_plus_made, 1)
                    if s == 4 and t.has(1) and t.has(0):
                        find_rest(pool, t)
                    if s == 7 and t.has(1) and t.has(0):
                        find_last_part(pool, t)
                    if s == 11 and t.has(-2):
                        pool.wait_ge(mean_made, NT * (t.batch(-2) + 1))
                        if t.has(-3):
                            pool.wait_ge(normed, NT * (t.batch(-3) + 1))
                        pool.tensor_tensor(var_eps[:], mean_var[:, :, 1], eps_col[:], ALU.add).then_inc(var_eps_made, 1)
                        pool.wait_ge(var_eps_made, t.batch(-2) + 1)
                        pool.tensor_tensor(shift[:], mean_var[:, :, 0], minus_one[:], ALU.mult).then_inc(mean_negated, 1)
                        pool.tensor_tensor(rstd[:], var_eps[:], minus_half[:], ALU.pow).then_inc(rstd_made, 1)
                        pool.wait_ge(mean_negated, t.batch(-2) + 1)
                        pool.wait_ge(rstd_made, t.batch(-2) + 1)
                        pool.tensor_tensor(shift[:], shift[:], rstd[:], ALU.mult).then_inc(shift_made, 1)
                    if h % PAIR == 1 and t.has(k):
                        mask(t, k, h)

            pool.wait_ge(consts_loaded, 16 * len(CONSTS))
            pool.wait_ge(made, 9)
            turns(pool, B, body)
            routing.scatter(pool, 0)

        @block.tensor
        def _(pe):
            pe.wait_ge(first_consts_loaded, 16 * len(FIRST_CONSTS))

            def scores(t, h):
                par, b = t.parity(0), t.batch(0)
                first = not t.steady and t.c == 0 and h == 0
                if h % HALF == 0:
                    wait_stacks(pe, t, 0, h // HALF)
                q, k = q_stack[par][0:SPLIT_ROWS, h, :], k_stack[par][0:SPLIT_ROWS, h, :]

                def product(bank, at, n, first, blocks):
                    return pe.matmul(bank[:, at:at + blocks * P], q[:, n * P:(n + 1) * P], k[:, first * P:(first + blocks) * P],
                                     start=True, stop=True)

                if not first:
                    pe.wait_ge(s_taken[0], H * b + h)
                for n in range(NT):
                    pe.matmul(s_bank[0][:, n * P:(n + 1) * P], q[:, n * P:(n + 1) * P], k[:, n * P:(n + 1) * P],
                              start=(n == 0), stop=False, skip_group_check=True)
                pe.matmul(s_bank[0][:], ident16[:], above[:].rearrange("p n c -> p (n c)"), start=False, stop=True,
                          skip_group_check=True).then_inc(s_ready[0], 1)
                if not first:
                    pe.wait_ge(s_taken[1], H * b + h)
                product(s_bank[1], 0, 3, 0, 3)
                product(s_bank[1], 3 * P, 1, 0, 1).then_inc(s_ready[1], 1)
                if h % PAIR == 0:
                    if not first:
                        pe.wait_ge(s_taken[2], HALF * b + h // PAIR)
                    product(s_bank[2], 0, 2, 0, 2)
                else:
                    product(s_bank[2], SHORT, 2, 0, 2).then_inc(s_ready[2], 1)

            def scores_t(t, kk, h):
                par, b = t.parity(kk), t.batch(kk)
                first = not t.steady and t.c + kk == 0 and h == 0
                if h % HALF == 0:
                    pe.wait_ge(max_stacked[h // HALF], 16 * (b + 1))
                q, k = q_stack[par][0:STACK, h, :], k_stack[par][0:STACK, h, :]

                def product(bank, at, n, first, blocks):
                    return pe.matmul(bank[:, at:at + blocks * P], k[:, n * P:(n + 1) * P], q[:, first * P:(first + blocks) * P],
                                     start=True, stop=True)

                if not first:
                    pe.wait_ge(t_taken[0], H * b + h)
                for n in range(NT):
                    mm = product(t_bank[0], n * P, n, n, 1)
                mm.then_inc(t_ready[0], 1)
                if not first:
                    pe.wait_ge(t_taken[1], H * b + h)
                product(t_bank[1], 0, 0, 1, 3)
                product(t_bank[1], 3 * P, 2, 3, 1).then_inc(t_ready[1], 1)
                if h % PAIR == 0:
                    if not first:
                        pe.wait_ge(t_taken[2], HALF * b + h // PAIR)
                    product(t_bank[2], 0, 1, 2, 2)
                else:
                    product(t_bank[2], SHORT, 1, 2, 2).then_inc(t_ready[2], 1)

            def context(t, g, piece):
                b = t.batch(-1)
                if piece == 0:
                    pe.wait_ge(t_taken[1], H * b + GROUP * (g + 1))
                    pe.wait_ge(t_taken[2], (H // PAIR) * b + (GROUP // PAIR) * (g + 1))
                    if g > 0 or t.has(-2):
                        pe.wait_ge(c_taken, NG * b + g)
                    if g == 0:
                        pe.wait_ge(m_taken, t.before().misc_count("v"))
                if piece == 2:
                    pe.wait_ge(masked, (H // PAIR) * b + (GROUP // PAIR) * (g + 1))
                diagonal, long, short = probs_of(g, 0, GROUP)
                runs = [[(long, LONG, 0, 0, 1, 3)],
                        [(short, SHORT, 0, 1, 2, 2), (long, LONG, 3 * P, 2, 3, 1)],
                        [(diagonal, DIAG, n * P, n, n, 1) for n in range(NT)]][piece]
                for strip, width, at, n, first, count in runs:
                    for j in range(GROUP):
                        mm = pe.matmul(c_bank[32 * j:32 * j + 16, first * P:(first + count) * P],
                                       v_aug[t.parity(-1)][:, n, GROUP * g + j, :],
                                       strip[:, j * width + at:j * width + at + count * P],
                                       start=(piece == 0), stop=(n == NT - 1), skip_group_check=True)
                if piece == 2:
                    mm.then_inc(c_ready, 1)

            def misc(t, name, k):
                count = t.misc_count(name)
                b = t.batch(k)
                if t.steady or count > 1:
                    pe.wait_ge(m_taken, count - 1)
                if name == "tiles":
                    mm = routing.count_tiles(pe, 0, m_bank)
                elif name == "ranks":
                    mm = routing.count_ranks(pe, 0, m_bank)
                elif name in ("q", "k"):
                    if name == "q":
                        pe.wait_ge(x_t_loaded[t.parity(k)], 16 * (t.half(k) + 1))
                    mm = pe.matmul(m_bank[:], (wq if name == "q" else wk)[:], x_t[t.parity(k)][:], start=True, stop=True)
                elif name == "v":
                    for n in range(NT):
                        mm = pe.matmul(m_bank[:, n * D:(n + 1) * D], x_t[t.parity(k)][:, n * P:(n + 1) * P], wv[:],
                                       start=True, stop=True)
                elif name in ("max0", "max1"):
                    half = int(name[-1])
                    pe.wait_ge(max_split, 2 * b + half + 1)
                    for n in range(NT):
                        mm = pe.transpose(M16[0:PARTS * HALF, n * P:(n + 1) * P],
                                          max_part[:, half, n, :, :].rearrange("p a h -> p (a h)"), ident16[:])
                elif name[:3] == "ctx":
                    n = int(name[-1])
                    if n == 0:
                        pe.wait_ge(c_taken, NG * (b + 1))
                    for g in range(NG):
                        mm = pe.transpose(m_bank[:, g * P:(g + 1) * P], ctx_t[t.parity(k)][:, g, n * P:(n + 1) * P], ident[:])
                elif name == "turn":
                    for n in range(NT):
                        mm = pe.transpose(m_bank[:, n * P:(n + 1) * P], ctx_n[:, n, :], ident[:])
                elif name == "out":
                    for n in range(NT):
                        mm = pe.matmul(m_bank[:, n * D:(n + 1) * D], turned[:, n * P:(n + 1) * P], wo[:],
                                       start=True, stop=True)
                elif name == "xturn":
                    pe.wait_ge(normed, NT * (b + 1))
                    for n in range(NT):
                        mm = pe.transpose(m_bank[:, n * P:(n + 1) * P], x1_now[:, n, :], ident[:])
                elif name == "gate":
                    for n in range(NT):
                        mm = pe.matmul(m_bank[:, n * 8:(n + 1) * 8], turned[:, n * P:(n + 1) * P], gate_w[:],
                                       start=True, stop=True)
                mm.then_inc(m_ready, 1)

            def body(t):
                if not t.steady and t.c == 0:
                    pe.wait_ge(made, 9)
                    pe.wait_ge(consts_loaded, 16 * len(CONSTS))
                    pe.wait_ge(ones_made, ONES)
                for s in range(H):
                    if t.has(0):
                        scores(t, s)
                    kk = 0 if s >= LAG else -1
                    if t.has(kk):
                        scores_t(t, kk, (s - LAG) % H)
                    if s % GROUP > 0 and t.has(-1):
                        context(t, s // GROUP, s % GROUP - 1)
                    for slot, name, k in MISC:
                        if slot == s and t.has(k):
                            misc(t, name, k)

            turns(pe, B, body)

        @block.scalar
        def _(act):
            def exps(t, kk, h):
                b = t.batch(kk)
                diagonal, long, _ = probs_of(h // GROUP, h % GROUP, 1)
                if not t.steady and t.c + kk == 0 and h == GROUP:
                    act.wait_ge(routing.zeroed, 16 * routing.N_ZERO)
                if h % GROUP == 0 and (t.steady or NG * (t.c + kk) + h // GROUP >= 2):
                    act.wait_ge(c_ready, NG * b + h // GROUP - 1)
                act.wait_ge(t_ready[0], H * b + h + 1)
                act.activation(diagonal, t_bank[0][:], ACT.Exp, scale=SCALE).then_inc(t_taken[0], 1)

                act.wait_ge(t_ready[1], H * b + h + 1)
                act.activation(long, t_bank[1][:], ACT.Exp, scale=SCALE).then_inc(t_taken[1], 1)
                if h % PAIR == 1:
                    _, _, short = probs_of(h // GROUP, h % GROUP - 1, PAIR)
                    act.wait_ge(t_ready[2], HALF * b + h // PAIR + 1)
                    act.activation(short, t_bank[2][:], ACT.Exp, scale=SCALE).then_inc(t_taken[2], 1)

            def misc(t, name, k):
                count = t.misc_count(name)
                b = t.batch(k)
                if name in ("q", "k"):
                    which = int(name == "k")
                    act.wait_ge(m_ready, count)
                    if which == 0 and (t.steady or t.c + k > 0):
                        act.wait_ge(part3_made, b)
                    act.activation(qk[:, which, :], m_bank[:], ACT.Identity, bias=qk_bias[:, which:which + 1]).then_inc(m_taken, 1)
                    if name == "k":
                        act.wait_ge(m_taken, count)
                        if t.steady or t.c + k > 0:
                            act.wait_ge(parts_written[t.parity(k - 1)], 16 * 2 * PARTS * (t.half(k - 1) + 1))
                        act.activation(part[0][:], qk[:], ACT.Copy).then_inc(part1_made, 1)
                elif name in ("max0", "max1"):
                    half = int(name[-1])
                    act.wait_ge(m_ready, count)
                    if t.steady or t.c + k > 0:
                        act.wait_ge(max_stacked[half], 16 * b)
                    act.activation(max_rows[half][:], M16[0:PARTS * HALF, 0:S], ACT.Copy).then_inc(m_taken, 1)
                    act.wait_ge(m_taken, count)
                    act.dma_start(
                        q_stack[t.parity(k)][SPLIT_ROWS:STACK, half * HALF:(half + 1) * HALF, :],
                        max_rows[half][:],
                    ).then_inc(max_stacked[half], 16)
                elif name == "turn":
                    act.wait_ge(m_ready, count)
                    act.activation(turned[:], m_bank[:], ACT.Copy).then_inc(m_taken, 1)
                elif name == "xturn":
                    act.wait_ge(m_ready, count)
                    act.activation(turned[:], m_bank[:], ACT.Copy).then_inc(m_taken, 1)

            def normalise(t):
                b = t.batch(-2)
                act.wait_ge(shift_made, b + 1)
                for n in range(NT):
                    act.activation(x1_now[:, n, :], res[:, n, :], ACT.Identity, scale=rstd[:, n:n + 1],
                                   bias=shift[:, n:n + 1]).then_inc(normed, 1)

            def keep_context(t, k, g):
                act.wait_ge(c_ready, NG * t.batch(k) + g + 1)
                if g == 0 and t.has(-3):
                    act.wait_ge(m_taken, t.before().misc_count("ctx3"))
                act.activation(ctx_t[t.parity(k)][:, g, :], c_bank[:], ACT.Copy).then_inc(c_taken, 1)

            def body(t):
                for s in range(H):
                    if s == 1 and t.has(None):
                        routing.exponentials(act, 0)
                    if (t.c, s) == (B, 12):
                        act.wait_ge(c_ready, NG * B - 1)
                    if (t.c, s) == (B + 1, 0):
                        act.wait_ge(c_ready, NG * B)
                    for n in UPPER_STEPS.get((t.c - B, s), ()):
                        routing.upper(act, arena, both_probs, n)
                    if s == 0 and t.has(-2):
                        keep_context(t, -2, NG - 1)
                    if s % GROUP == 0 and s > 0 and t.has(-1):
                        keep_context(t, -1, s // GROUP - 1)
                    for slot, name, k in MISC:
                        if slot == s - 1 and t.has(k):
                            misc(t, name, k)
                    if s == 6 and t.has(1):
                        act.wait_ge(rest_made, t.batch(1) + 1)
                        act.activation(part[1][:], rest[:], ACT.Copy).then_inc(part2_made, 1)
                    if s == 13 and t.has(-2):
                        normalise(t)
                    kk = 0 if s >= LAG else -1
                    if t.has(kk):
                        exps(t, kk, (s - LAG) % H)

            act.wait_ge(first_consts_loaded, 16 * len(FIRST_CONSTS))
            turns(act, B, body)

        @block.vector
        def _(dve):
            def ones_below(parity):
                pairs = k_stack[parity][64:P, :, :].rearrange("p h t -> p (h t)").bitcast(F32)
                nc.vector.memset(pairs, ONES_16).then_inc(ones_made, 1)

            ones_below(0)

            def maxima(t, h):
                b = t.batch(0)
                half, hh = h // HALF, h % HALF
                if hh == 0 and (t.steady or t.c > 0):
                    dve.wait_ge(max_split, 2 * b + half - 1)
                off = lambda n: off_max[:, half, n - 1, hh:hh + 1]
                dve.wait_ge(s_ready[0], H * b + h + 1)
                nc.vector.tensor_reduce(row_max[:, half, :, hh], s_bank[0][:].rearrange("p (n c) -> p n c", n=NT), AX.X,
                                        ALU.max).then_inc(s_taken[0], 1)

                dve.wait_ge(s_ready[1], H * b + h + 1)
                nc.vector.tensor_reduce(off(3), s_bank[1][:, 0:3 * P], AX.X, ALU.max).then_inc(max_reduced, 1)
                nc.vector.tensor_reduce(off(1), s_bank[1][:, 3 * P:S], AX.X, ALU.max).then_inc(s_taken[1], 1)
                if h % PAIR == 1:
                    dve.wait_ge(s_ready[2], HALF * b + h // PAIR + 1)
                    nc.vector.tensor_reduce(off_max[:, half, 1, hh - 1:hh + 1],
                                            s_bank[2][:].rearrange("p (h c) -> p h c", h=PAIR), AX.X,
                                            ALU.max).then_inc(s_taken[2], 1)
                if hh == HALF - 1:
                    split_maxima(t, half)

            def split_maxima(t, half):
                b = t.batch(0)
                m = row_max[:, half, :, :]
                pieces = [max_part[:, half, :, n, :] for n in range(PARTS)]
                if t.steady or t.c > 0:
                    dve.wait_ge(m_ready, t.before().misc_count("max0") if half == 0 else t.misc_count("max1"))
                dve.wait_ge(s_taken[0], H * b + (half + 1) * HALF)
                dve.wait_ge(max_reduced, H * b + (half + 1) * HALF)
                dve.wait_ge(s_taken[1], H * b + (half + 1) * HALF)
                dve.wait_ge(s_taken[2], HALF * b + (half + 1) * (HALF // PAIR))
                step = 4 * (2 * b + half)
                nc.vector.tensor_tensor(m[:, 1:NT], m[:, 1:NT], off_max[:, half], ALU.max).then_inc(max_step, 1)
                dve.wait_ge(max_step, step + 1)
                nc.vector.tensor_scalar(pieces[0], m, -1.0, None, ALU.mult).then_inc(max_step, 1)
                dve.wait_ge(max_step, step + 2)
                nc.vector.scalar_tensor_tensor(out=max_rest[:], in0=m, scalar=-1.0, in1=pieces[0], op0=ALU.mult,
                                               op1=ALU.subtract).then_inc(max_step, 1)
                dve.wait_ge(max_step, step + 3)
                nc.vector.tensor_copy(pieces[1], max_rest[:]).then_inc(max_step, 1)
                dve.wait_ge(max_step, step + 4)
                nc.vector.tensor_tensor(pieces[2], max_rest[:], pieces[1], ALU.subtract).then_inc(max_split, 1)

            def misc(t, name, k):
                count = t.misc_count(name)
                b = t.batch(k)
                if name == "tiles":
                    dve.wait_ge(m_ready, count)
                    routing.vector(dve, 0, 9, m_bank, m_taken, count)
                elif name == "ranks":
                    dve.wait_ge(m_ready, count)
                    routing.vector(dve, 0, 11, m_bank, m_taken, count)
                elif name == "v":
                    dve.wait_ge(m_ready, count)
                    if t.steady or t.c + k >= 2:
                        dve.wait_ge(c_ready, NG * (b - 1))
                    for n in range(NT):
                        add = nc.vector.tensor_tensor(
                            v_aug[t.parity(k)][:, n, :, 0:HD], m_bank[:, n * D:(n + 1) * D].rearrange("p (h d) -> p h d", d=HD),
                            v_bias[:].rearrange("p (h d) -> p h d", d=HD), ALU.add)
                    add.then_inc(m_taken, 1)
                elif name[:3] == "ctx":
                    n = int(name[-1])
                    dve.wait_ge(m_ready, count)
                    if n == 0 and t.has(-3):
                        dve.wait_ge(m_taken, t.before().misc_count("xturn"))
                        dve.wait_ge(x1_kept, 16 * b)
                    strips = m_bank[:].rearrange("p (h c) -> p h c", h=H)
                    nc.vector.reciprocal(inv_sum[:], strips[:, :, SUM_COL]).then_inc(sums_inverted, 1)
                    dve.wait_ge(sums_inverted, NT * b + n + 1)
                    nc.vector.tensor_tensor(ctx_n[:, n, :].rearrange("p (h d) -> p h d", h=H), strips[:, :, 0:HD],
                                            inv_sum[:].rearrange("p (h o) -> p h o", o=1).to_broadcast([P, H, HD]),
                                            ALU.mult).then_inc(m_taken, 1)
                elif name == "out":
                    dve.wait_ge(m_ready, count)
                    dve.wait_ge(x_plus_made, b + 1)
                    nc.vector.tensor_tensor(res[:].rearrange("p n d -> p (n d)"), m_bank[:],
                                            res[:].rearrange("p n d -> p (n d)"), ALU.add).then_inc(m_taken, 1)
                    dve.wait_ge(m_taken, count)
                    nc.vector.bn_stats(stats[:, 0, :], res[:, 0, :]).then_inc(stats_made, 1)
                    for n in range(1, NT):
                        nc.vector.bn_stats(stats[:, n, :], res[:, n, :]).then_inc(stats_made, 1)
                elif name == "gate":
                    dve.wait_ge(m_ready, count)
                    nc.vector.tensor_tensor(logits[:, bass.ds(b * NT, NT), :],
                                            m_bank[:, 0:NT * 8].rearrange("p (n e) -> p n e", n=NT), gate_bias[:],
                                            ALU.add).then_inc(m_taken, 1)

            def moments(t):
                b = t.batch(-2)
                if t.has(-3):
                    dve.wait_ge(shift_made, b)
                for n in range(NT):
                    dve.wait_ge(stats_made, NT * b + n + 1)
                    dve.nop(nofuse=True)
                    nc.vector.bn_aggr(mean_var[:, n, :], stats[:, n, :]).then_inc(mean_made, 1)

            def body(t):
                for s in range(H):
                    if (t.c, s) == (-1, 2):
                        for p in range(2):
                            nc.vector.memset(v_aug[p][:], 1.0).then_inc(ones_made, 1)
                        nc.vector.memset(c_bank[:], 0.0).then_inc(ones_made, 1)
                        nc.vector.memset(zeros, 0.0).then_inc(ones_made, 1)
                    if (t.c, s) == (-1, 4):
                        find_rest(nc.vector, t)
                    if (t.c, s) == (-1, 7):
                        find_last_part(nc.vector, t)
                        ones_below(1)
                        dve.wait_ge(ones_made, ONES)
                        dve.wait_ge(consts_loaded, 16 * len(CONSTS))
                    for slot, name, k in MISC:
                        if slot == s - 1 and t.has(k):
                            misc(t, name, k)
                    if s == 11 and t.has(-2):
                        moments(t)
                    for n in LOWER_STEPS.get((t.c - B, s), ()):
                        routing.lower(dve, arena, both_probs, n)
                    if t.has(0):
                        maxima(t, s)
                    if t.has(None):
                        for stage in ROUTING_SLOTS.get(s, ()):
                            routing.vector(dve, 0, stage)

            turns(dve, B, body)



class Step:

    def __init__(self, j, c, n, late, period=2, chunk=None):
        self.j, self.c, self.n, self.late, self.period, self.of = j, c, n, late, period, chunk
        self.steady = chunk is not None

    def has(self, k):
        return self.steady or 0 <= self.c + k < self.n

    def block(self, k=0):
        return self.j * self.period + (self.c + k)

    def chunk(self, k):
        return self.of if self.steady else int(self.c + k >= self.late)

    def rows(self, k):
        return bass.ds((self.j * self.period + (self.c + k - self.chunk(k) * self.late)) * P, P)

    def parity(self, k=0):
        return (self.c + k) % 2

    def half(self, k=0):
        return self.j * (self.period // 2) + (self.c + k) // 2

    def later(self, k, n):
        return self.steady or self.c + k >= n


def steps(eng, n, late, body, beside=None, turns=None):
    for c in range(-1, FIRST_STEPS):
        body(Step(0, c, n, late))
    pairs = (late - 2 - FIRST_STEPS) // 2
    with eng.Fori(0, pairs) as j:
        for c in (FIRST_STEPS, FIRST_STEPS + 1):
            body(Step(j, c, n, late, chunk=0))
    start = late + 4
    for c in range(FIRST_STEPS + 2 * pairs, start):
        body(Step(0, c, n, late))
    period = PERIOD if beside else 2
    peeled = 2 if beside else 0
    for j in range(peeled):
        for i in range(period):
            body(Step(0, start + j * period + i, n, late))
            beside(j, i)
    if not beside:
        turns = (n - 2 - start) // period
    with eng.Fori(peeled, turns) as j:
        for i in range(period):
            body(Step(j, start + i, n, late, period, chunk=1))
            if beside:
                beside(j, i)
    for c in range(start + turns * period, n + 3):
        body(Step(0, c, n, late))


def experts(nc, ctx, x1, arena, probs, routing, out):

    def sb(name, shape, dt=F32):
        return ctx.enter_context(nc.sbuf_tensor(name, shape, dt))

    def sem(name):
        return ctx.enter_context(nc.semaphore(name))

    tiles, chunks, blocks, first_block, n_blocks = (
        routing.tiles, routing.chunks, routing.blocks, routing.first_block, routing.n_blocks)
    x_slots, y_slots, slot, weight, w_offset = routing.x_slots, routing.y_slots, routing.slot, routing.weight, routing.w_offset
    w1 = [half[:, 0:E * FF].bitcast(F32R) for half in (probs, arena)]
    w3 = [half[:, E * FF:2 * E * FF].bitcast(F32R) for half in (probs, arena)]
    w2 = arena[:, 2 * E * FF:3 * E * FF]
    ident = sb("identity", [P, P])

    x_in = [sb(f"x_in{p}", [P, D]) for p in range(2)]
    x_t = [[sb(f"x_in_t{p}_{half}", [P, P], F32R) for half in ("upper", "lower")] for p in range(2)]
    silu = [sb(f"silu{p}", [P, FF]) for p in range(2)]
    gated = [sb(f"gated{p}", [P, FF]) for p in range(2)]
    h_t = [sb(f"h_t{p}", [P, FC, P]) for p in range(2)]
    y_out = [sb(f"y_out{p}", [P, D]) for p in range(2)]

    picks = [sb(f"picks{p}", [P, CG, TOP_K, D]) for p in range(2)]
    part_sum = sb("part_sum", [P, CG, D])
    total_sum = [sb(f"total_sum{p}", [P, CG, D]) for p in range(2)]
    stats = sb("stats2", [P, CG, 6])
    mean_var = [sb(f"mean_var2{p}", [P, CG, 2]) for p in range(2)]
    var_eps = [sb(f"var_eps2{p}", [P, CG]) for p in range(2)]
    minus_half = sb("minus_half2", [P, CG])
    rstd = [sb(f"rstd2{p}", [P, CG]) for p in range(2)]
    final = [sb(f"final{p}", [P, CG, D]) for p in range(2)]

    def bank(name):
        return ctx.enter_context(nc.psum_tensor(name, [P, S], F32))
    h1_bank = [bank(f"h1_bank{p}") for p in range(2)]
    h3_bank = [bank(f"h3_bank{p}") for p in range(2)]
    ht_bank = [bank(f"ht_bank{p}") for p in range(2)]
    xt_bank = bank("xt_bank")
    y_bank = bank("y_bank")

    made = sem("made2")
    tiles_counted = sem("tiles_counted")
    tiles_read = sem("tiles_read")
    ranks_counted = sem("ranks_counted")
    ranks_read = sem("ranks_read")
    x_loaded = [sem(f"x_loaded{p}") for p in range(2)]
    x_turned = sem("x_turned")
    xt_upper_made = sem("xt_upper_made")
    xt_lower_made = sem("xt_lower_made")
    h1_ready = sem("h1_ready")
    h3_ready = sem("h3_ready")
    silu_made = sem("silu_made")
    h_gated = sem("h_gated")
    ht_ready = sem("ht_ready")
    ht_copied = sem("ht_copied")
    y_ready = sem("y_ready")
    y_copied = sem("y_copied")
    y_stored = [sem(f"y_stored{p}") for p in range(2)]
    gathered = [sem(f"gathered{p}") for p in range(2)]
    summed = sem("summed")
    sum_step = sem("sum_step")
    stats_made = sem("stats_made2")
    mean_made = sem("mean_made2")
    var_eps_made = sem("var_eps_made2")
    rstd_made = sem("rstd_made2")
    final_made = sem("final_made")
    stored = [sem(f"stored{p}") for p in range(2)]

    n_groups = tiles // CG
    beside_turns = min((blocks[1] - 6) // PERIOD, chunks[0][1] // CG // 2)
    assert beside_turns > 1

    def is_number(j, n):
        return isinstance(j, int) and j == n

    def y_all_stored(eng, block):
        for p in range(2):
            eng.wait_ge(y_stored[p], 16 * ((block - p + 1) // 2))

    with nc.Block() as block:

        @block.sync
        def _(sp):
            out_g = out.rearrange("(g n p) d -> g p n d", n=CG, p=P)

            def store(j, p):
                sp.wait_ge(final_made, (j * 2 + (p + 1)) * CG)
                sp.dma_start(out_g[j * 2 + p], final[p][:]).then_inc(stored[p], 16)

            def store_beside(j, n):
                if n in (1, PERIOD // 2 + 1) and not is_number(j, 0):
                    store(j - 1, int(n > 1))

            def load(t, k):
                c = t.chunk(k)
                if not t.steady and t.c + k in first_block:
                    sp.wait_ge(routing.scattered[c], 16 * TOP_K * chunks[c][1])
                sp.dma_start(x_in[t.parity(k)][:], x_slots[c][t.rows(k), :]).then_inc(x_loaded[t.parity(k)], 16)

            def body(t):
                if t.c == -1:
                    load(t, 1)
                    load(t, 2)
                elif t.has(0) and t.has(2):
                    sp.wait_ge(x_turned, t.block() + 1)
                    load(t, 2)
                if t.has(-3):
                    sp.wait_ge(y_copied, t.block(-2))
                    sp.dma_start(y_slots[t.chunk(-3)][t.rows(-3), :], y_out[t.parity(-3)][:]).then_inc(y_stored[t.parity(-3)], 16)

            steps(sp, n_blocks, first_block[1], body, store_beside, beside_turns)
            store(beside_turns - 1, 0)
            with sp.Fori(beside_turns, n_groups // 2) as j:
                store(j - 1, 1)
                store(j, 0)
            store(n_groups // 2 - 1, 1)
            y_all_stored(sp, n_blocks)
            for p in range(2):
                sp.wait_ge(stored[p], 16 * (n_groups // 2))

        @block.gpsimd
        def _(pool):
            pool.memset(ident[:], 0.0).then_inc(made, 1)
            pool.memset(minus_half[:], -0.5).then_inc(made, 1)
            pool.wait_ge(made, 2)
            pool.affine_select(out=ident[:], in_=ident[:], compare_op=ALU.not_equal, fill=1.0, base=0,
                               pattern=[[-1, P]], channel_multiplier=1).then_inc(made, 1)
            routing.scatter(pool, 1)

            def scale(g):
                p = g % 2
                pool.wait_ge(var_eps_made, g + 1)
                if g >= 2:
                    pool.wait_ge(final_made, CG * (g - 1))
                pool.tensor_tensor(rstd[p][:], var_eps[p][:], minus_half[:], ALU.pow).then_inc(rstd_made, 1)

            for c, (t0, n_tiles) in enumerate(chunks):
                y_all_stored(pool, first_block[c] + blocks[c])
                for g in range(t0 // CG, (t0 + n_tiles) // CG):
                    if g >= 2:
                        pool.wait_ge(summed, CG * (g - 1))
                    for n in range(CG):
                        for k in range(TOP_K):
                            pool.indirect_dma_start(
                                out=picks[g % 2][:, n, k, :], out_offset=None, in_=y_slots[c],
                                in_offset=bass.IndirectOffsetOnAxis(ap=slot[k][:, g * CG + n:g * CG + n + 1], axis=0),
                            ).then_inc(gathered[g % 2], 16)
                    if g >= 1:
                        scale(g - 1)
            scale(n_groups - 1)

        @block.vector
        def _(dve):
            v = nc.vector
            def body(t):
                if not t.steady:
                    for stage in ROUTING_STEPS.get(t.c, ()):
                        if stage == 9:
                            dve.wait_ge(tiles_counted, 1)
                            routing.vector(dve, 1, stage, xt_bank, tiles_read, 1)
                        elif stage == 11:
                            dve.wait_ge(ranks_counted, 1)
                            routing.vector(dve, 1, stage, xt_bank, ranks_read, 1)
                        else:
                            routing.vector(dve, 1, stage)
                if t.has(1):
                    dve.wait_ge(xt_upper_made, t.block(2))
                    upper, lower = x_t[t.parity(1)]
                    v.tensor_tensor(lower[:], xt_bank[:, 0:P], upper[:].bitcast(F32), ALU.subtract).then_inc(xt_lower_made, 1)
                if t.has(0):
                    dve.wait_ge(silu_made, t.block(1))
                    dve.wait_ge(h3_ready, t.block(1))
                    if t.later(0, 2):
                        dve.wait_ge(ht_ready, t.block(-1))
                    v.tensor_tensor(gated[t.parity()][:], silu[t.parity()][:], h3_bank[t.parity()][:], ALU.mult).then_inc(h_gated, 1)

            def combine(j, p, half):
                g = j * 2 + p
                if half == 0:
                    dve.wait_ge(gathered[p], 16 * CG * TOP_K * (j + 1))
                members = range(half * (CG // 2), (half + 1) * (CG // 2))
                for n in members:
                    tile = g * CG + n
                    v.scalar_tensor_tensor(out=part_sum[:, n, :], in0=picks[p][:, n, 0, :], scalar=weight[0][:, bass.ds(tile, 1)],
                                           in1=x1[:, tile, :], op0=ALU.mult, op1=ALU.add).then_inc(sum_step, 1)
                for n in members:
                    tile = g * CG + n
                    dve.wait_ge(sum_step, tile + 1)
                    v.scalar_tensor_tensor(out=total_sum[p][:, n, :], in0=picks[p][:, n, 1, :], scalar=weight[1][:, bass.ds(tile, 1)],
                                           in1=part_sum[:, n, :], op0=ALU.mult, op1=ALU.add).then_inc(summed, 1)
                for n in members:
                    dve.wait_ge(summed, g * CG + n + 1)
                    v.bn_stats(stats[:, n, :], total_sum[p][:, n, :]).then_inc(stats_made, 1)
                for n in members:
                    dve.wait_ge(stats_made, g * CG + n + 1)
                    dve.nop(nofuse=True)
                    v.bn_aggr(mean_var[p][:, n, :], stats[:, n, :]).then_inc(mean_made, 1)
                if half == 1:
                    dve.wait_ge(mean_made, CG * (g + 1))
                    v.tensor_scalar(var_eps[p][:], mean_var[p][:, :, 1], EPS, None, ALU.add).then_inc(var_eps_made, 1)

            def normalise(j, p, former):
                g = j * 2 + p
                dve.wait_ge(rstd_made, g + 1)
                if former:
                    dve.wait_ge(stored[p], 16 * j)
                for n in range(CG):
                    v.tensor_scalar(final[p][:, n, :], total_sum[p][:, n, :], mean_var[p][:, n, 0:1], rstd[p][:, n:n + 1],
                                    ALU.subtract, ALU.mult).then_inc(final_made, 1)

            def combine_beside(j, n):
                p, part = n // (PERIOD // 2), n % (PERIOD // 2)
                if part < 2:
                    combine(j, p, part)
                elif p == 1:
                    normalise(j, 0, not is_number(j, 0))
                elif not is_number(j, 0):
                    normalise(j - 1, 1, not is_number(j, 1))

            steps(dve, n_blocks, first_block[1], body, combine_beside, beside_turns)
            with dve.Fori(beside_turns, n_groups // 2) as j:
                for p in range(2):
                    for half in range(2):
                        combine(j, p, half)
                    normalise(j - 1 + p, 1 - p, True)
            normalise(n_groups // 2 - 1, 1, True)

        @block.scalar
        def _(act):
            def body(t):
                if t.has(-3):
                    act.wait_ge(y_ready, t.block(-2))
                    if t.later(-3, 2):
                        act.wait_ge(y_stored[t.parity(-3)], 16 * t.half(-3))
                    act.activation(y_out[t.parity(-3)][:], y_bank[:, 0:D], ACT.Copy).then_inc(y_copied, 1)
                if t.has(-2):
                    act.wait_ge(ht_ready, t.block(-1))
                    if t.later(-2, 2):
                        act.wait_ge(y_ready, t.block(-3))
                    act.activation(h_t[t.parity(-2)][:].rearrange("p c t -> p (c t)"), ht_bank[t.parity(-2)][:], ACT.Copy).then_inc(ht_copied, 1)
                if t.has(1):
                    act.wait_ge(x_turned, t.block(2))
                    if t.later(1, 2):
                        act.wait_ge(h3_ready, t.block())
                    act.activation(x_t[t.parity(1)][0][:], xt_bank[:, 0:P], ACT.Copy).then_inc(xt_upper_made, 1)
                if not t.steady and t.c == 0:
                    routing.exponentials(act, 1)
                if t.has(0):
                    act.wait_ge(h1_ready, t.block(1))
                    if t.later(0, 2):
                        act.wait_ge(h_gated, t.block(-1))
                    act.activation(silu[t.parity()][:], h1_bank[t.parity()][:], ACT.Silu).then_inc(silu_made, 1)

            steps(act, n_blocks, first_block[1], body)

        @block.tensor
        def _(pe):
            pe.wait_ge(made, 3)
            pe.wait_ge(routing.offsets_made, 1)
            pe.wait_ge(routing.lower_made, 2 * E)
            pe.wait_ge(routing.w2_loaded, 16 * E)

            def offset(t, k):
                return nc.s_assert_within(
                    pe.value_load(w_offset[0:1, bass.ds(t.block(k), 1)]), 0, (E - 1) * FF,
                    skip_runtime_bounds_check_because="VectorE makes it as FF times a count of at most E - 1 comparisons")

            def product(bank, x, w, e):
                pairs = ((0, 0), (0, 1), (1, 0))
                for n, (of_x, of_w) in enumerate(pairs):
                    mm = pe.matmul(bank[:], x[of_x][:], w[of_w][:, bass.ds(e, FF)], start=(n == 0), stop=(n == len(pairs) - 1))
                return mm

            def body(t):
                p = t.parity()
                if t.c == first_block[1] and not t.steady:
                    pe.wait_ge(routing.offsets_made, 2)
                before = offset(t, -3) if t.has(-3) else None
                e = offset(t, 0) if t.has(0) else None
                if t.has(-3):
                    pe.wait_ge(ht_copied, t.block(-2))
                    for f in range(FC):
                        mm = pe.matmul(y_bank[:, 0:D], h_t[t.parity(-3)][:, f, :], w2[:, bass.ds(before + f * D, D)],
                                       start=(f == 0), stop=(f == FC - 1))
                    mm.then_inc(y_ready, 1)
                if t.has(-2):
                    pe.wait_ge(h_gated, t.block(-1))
                    for f in range(FC):
                        mm = pe.transpose(ht_bank[t.parity(-2)][:, f * P:(f + 1) * P], gated[t.parity(-2)][:, f * P:(f + 1) * P], ident[:])
                    mm.then_inc(ht_ready, 1)
                if t.has(1):
                    if t.later(1, 1):
                        pe.wait_ge(xt_lower_made, t.block(1))
                    if not t.steady and t.c == TILES_STEP:
                        routing.count_tiles(pe, 1, xt_bank).then_inc(tiles_counted, 1)
                        pe.wait_ge(tiles_read, 1)
                    if not t.steady and t.c == RANKS_STEP:
                        routing.count_ranks(pe, 1, xt_bank).then_inc(ranks_counted, 1)
                        pe.wait_ge(ranks_read, 1)
                    pe.wait_ge(x_loaded[t.parity(1)], 16 * (t.half(1) + 1))
                    pe.transpose(xt_bank[:, 0:P], x_in[t.parity(1)][:], ident[:]).then_inc(x_turned, 1)
                if t.has(0):
                    if not t.has(1):
                        pe.wait_ge(xt_lower_made, t.block(1))
                    product(h1_bank[p], x_t[p], w1, e).then_inc(h1_ready, 1)
                    product(h3_bank[p], x_t[p], w3, e).then_inc(h3_ready, 1)

            steps(pe, n_blocks, first_block[1], body)


def build(nc, a, out, B):
    with ExitStack() as ctx:
        x1 = ctx.enter_context(nc.sbuf_tensor("x1", [P, NT * B, D], F32))
        logits = ctx.enter_context(nc.sbuf_tensor("logits", [P, NT * B, E], F32))
        arena = ctx.enter_context(nc.sbuf_tensor("arena", [P, 2 * H * S], F32))
        probs = ctx.enter_context(nc.sbuf_tensor("probs", [P, 2 * GROUP * HEAD_P], F32))
        routing = Routing(nc, ctx, a, logits, x1, B)
        with ExitStack() as own:
            attention(nc, own, a, x1, logits, arena, probs, routing, B)
        with ExitStack() as own:
            experts(nc, own, x1, arena, probs, routing, out)


def kernel(**inputs):
    import concourse.bacc as bacc
    import numpy as np
    from concourse.bass_utils import run_bass_kernel_spmd

    w = {name.split("_", 2)[2]: np.asarray(value) for name, value in inputs.items()}
    B = w["x"].shape[0]
    across = lambda v, n: np.ascontiguousarray(np.broadcast_to(v, (P, n, v.shape[0])))
    layouts = {
        "x_t": w["x"].transpose(0, 2, 1),
        "x_rows": w["x"].reshape(B, NT, P, D).transpose(0, 2, 1, 3),
        "wq": w["Wq"], "wk": w["Wk"], "wv": w["Wv"], "wo": w["Wo"],
        "qk_bias": np.stack([w["bq"], w["bk"]], 1),
        "v_bias": across(w["bv"], 1)[:, 0], "o_bias": across(w["bo"], 1)[:, 0],
        "gate_w": w["gate_w"], "gate_bias": across(w["gate_b"], NT),
        "w1": w["w1"], "w3": w["w3"], "w2": w["w2"],
    }
    layouts = {f"in_{name}": np.ascontiguousarray(value) for name, value in layouts.items()}
    nc = bacc.Bacc("TRN2", target_bir_lowering=False, num_devices=1)
    a = {name[3:]: nc.dram_tensor(name, v.shape, mybir.dt.from_np(v.dtype), kind="ExternalInput").ap()
         for name, v in layouts.items()}
    out = nc.dram_tensor("out", [B * S, D], F32, kind="ExternalOutput").ap()
    build(nc, a, out, B)
    r = run_bass_kernel_spmd(nc, [layouts], core_ids=[0])
    return r.results[0]["out"].reshape(B, S, D)
```
